# Optimizing a Trainium2 kernel written in Bass

```python
import numpy as np
import jax
import jax.numpy as jnp

def _softmax(x, axis=-1):
    return jax.nn.softmax(x, axis=axis)

def _gelu(x):
    return jax.nn.gelu(x, approximate=True)

def _silu(x):
    return jax.nn.silu(x)

def _sigmoid(x):
    return jax.nn.sigmoid(x)

def _layernorm(x, axis=-1, eps=1e-05):
    m = jnp.mean(x, axis=axis, keepdims=True)
    v = jnp.var(x, axis=axis, keepdims=True)
    return (x - m) / jnp.sqrt(v + eps)

def _scatter_add(tgt, idx, src, axis=0):
    return tgt.at[idx].add(src)

def _segment_sum(src, seg, n):
    return jax.ops.segment_sum(src, seg, n)
kernel_name = 'mk_xattn_ffn_d2_seqx_r8_6c1c96'

def setup_inputs(seed: int=0):
    np.random.seed(seed)
    _w = jnp.asarray

    def _rec_inputs():
        import jax
        import jax.numpy as jnp
        _rk = jax.random.key(seed)
        x = 7.22e-05 + 1 * jax.random.normal(jax.random.fold_in(_rk, 1), (4, 256, 512), jnp.float32)
        _lenS = 256 - jax.random.randint(jax.random.fold_in(_rk, 7), (4,), 0, max(1, 256 // 4) + 1, jnp.int32)
        _lenS2 = 1601 - jax.random.randint(jax.random.fold_in(_rk, 8), (4,), 0, max(1, 1601 // 4) + 1, jnp.int32)
        _ctx_4096P = jax.random.normal(jax.random.fold_in(_rk, 11), (4, 16, 512), jnp.float32)
        _ctx_4096c = jax.random.dirichlet(jax.random.fold_in(_rk, 511), 0.3 * jnp.ones((16,), jnp.float32), (4, 1601))
        _ctx_4096t = jnp.einsum('bsk,bkd->bsd', _ctx_4096c, _ctx_4096P)
        _ctx_4096t = _ctx_4096t * jax.lax.rsqrt(jnp.mean(jnp.square(_ctx_4096t)) + 1e-12) * 0.953939
        ctx_4096 = 2.81802e-05 + 1.00001 * (_ctx_4096t + 0.3 * jax.random.normal(jax.random.fold_in(_rk, 611), (4, 1601, 512), jnp.float32))
        return (x, ctx_4096)
    x, ctx_4096 = _rec_inputs()

    def _L0_xattn_setup():
        import jax, jax.numpy as jnp
        import numpy as np
        HIDDEN = 512
        N_HEADS = 32
        N_KV_HEADS = 8
        HEAD_DIM = HIDDEN // N_HEADS
        N_REP = N_HEADS // N_KV_HEADS
        EPS = 1e-05

        def _rmsnorm(x, w):
            xf = x.astype(jnp.float32)
            var = jnp.mean(xf * xf, axis=-1, keepdims=True)
            return (xf * jax.lax.rsqrt(var + EPS)).astype(x.dtype) * w
        key = jax.random.key(seed)
        ks = jax.random.split(key, 7)
        B, Q, K = (2, 128, 256)
        scale = 0.02
        return {'hidden_states': jax.random.normal(ks[0], (B, Q, HIDDEN), jnp.float32), 'encoder_hidden_states': jax.random.normal(ks[1], (B, K, HIDDEN), jnp.float32), 'wq': jax.random.normal(ks[2], (N_HEADS * HEAD_DIM, HIDDEN), jnp.float32) * scale, 'wk': jax.random.normal(ks[3], (N_KV_HEADS * HEAD_DIM, HIDDEN), jnp.float32) * scale, 'wv': jax.random.normal(ks[4], (N_KV_HEADS * HEAD_DIM, HIDDEN), jnp.float32) * scale, 'wo': jax.random.normal(ks[5], (HIDDEN, N_HEADS * HEAD_DIM), jnp.float32) * scale, 'ln_w': jnp.ones((HIDDEN,), jnp.float32)}
    _L0_xattn_all = _L0_xattn_setup()
    _L0_xattn_in = {k: v for k, v in _L0_xattn_all.items() if k in ('wq', 'wk', 'wv', 'wo', 'ln_w')}
    del _L0_xattn_all

    def _L0_ffn_setup():
        import jax, jax.numpy as jnp
        import numpy as np
        IN_F = 512
        OUT_F = 512
        RANK = 8
        NUM_EXPERTS = 64
        TOP_K = 16
        ROUTER_DIM = 16
        ALPHA = 32
        SCALING = ALPHA / TOP_K
        BOTTLENECK = NUM_EXPERTS * RANK
        key = jax.random.key(seed)
        ks = jax.random.split(key, 5)
        x = jax.random.normal(ks[0], (4, 512, IN_F), dtype=jnp.float32)
        bound_a = float(np.sqrt(6.0 / IN_F))
        A_w = jax.random.uniform(ks[1], (BOTTLENECK, IN_F), jnp.float32, -bound_a, bound_a)
        B_w = jax.random.normal(ks[2], (OUT_F, BOTTLENECK), dtype=jnp.float32) * 0.02
        Wq_w = jax.random.normal(ks[3], (ROUTER_DIM, IN_F), dtype=jnp.float32) * 0.02
        keys = jax.random.normal(ks[4], (NUM_EXPERTS, ROUTER_DIM), dtype=jnp.float32) * 0.01
        return {'x': x, 'A_w': A_w, 'B_w': B_w, 'Wq_w': Wq_w, 'keys': keys}
    _L0_ffn_all = _L0_ffn_setup()
    _L0_ffn_in = {k: v for k, v in _L0_ffn_all.items() if k in ('A_w', 'B_w', 'Wq_w', 'keys')}
    del _L0_ffn_all

    def _L1_xattn_setup():
        import jax, jax.numpy as jnp
        import numpy as np
        B, Q, D = (8, 64, 512)
        CTX = 512
        H, KV, HD = (16, 4, 96)
        G = H // KV
        key = jax.random.key(seed)
        ks = jax.random.split(key, 6)
        s = 0.02
        return {'latents': jax.random.normal(ks[0], (B, Q, D), jnp.float32), 'context': jax.random.normal(ks[1], (B, CTX, D), jnp.float32), 'Wq': jax.random.normal(ks[2], (H * HD, D), jnp.float32) * s, 'Wk': jax.random.normal(ks[3], (KV * HD, D), jnp.float32) * s, 'Wv': jax.random.normal(ks[4], (KV * HD, D), jnp.float32) * s, 'Wo': jax.random.normal(ks[5], (D, H * HD), jnp.float32) * s}
    _L1_xattn_all = _L1_xattn_setup()
    _L1_xattn_in = {k: v for k, v in _L1_xattn_all.items() if k in ('Wq', 'Wk', 'Wv', 'Wo')}
    del _L1_xattn_all

    def _L1_ffn_setup():
        import jax, jax.numpy as jnp
        import numpy as np
        EPS = 1e-06
        QMAX = 127.0

        def _quant_act(x):
            s = jnp.max(jnp.abs(x), axis=-1, keepdims=True) / QMAX
            s = jnp.maximum(s, 1e-08)
            q = jnp.clip(jnp.round(x / s), -QMAX, QMAX)
            return (q, s)

        def _quant_w(W):
            ws = jnp.max(jnp.abs(W), axis=1, keepdims=True) / QMAX
            ws = jnp.maximum(ws, 1e-08)
            Wq = jnp.clip(jnp.round(W / ws), -QMAX, QMAX)
            return (Wq, ws)
        key = jax.random.key(seed)
        k1, k2, k3, k4, k5 = jax.random.split(key, 5)
        B, S, D, I = (4, 256, 512, 1376)
        return {'hidden_states': jax.random.normal(k1, (B, S, D), dtype=jnp.float32), 'rmsnorm_weight': jax.random.uniform(k2, (D,), dtype=jnp.float32), 'Wg': jax.random.normal(k3, (I, D), dtype=jnp.float32) * 0.02, 'Wu': jax.random.normal(k4, (I, D), dtype=jnp.float32) * 0.02, 'Wd': jax.random.normal(k5, (D, I), dtype=jnp.float32) * 0.02}
    _L1_ffn_all = _L1_ffn_setup()
    _L1_ffn_in = {k: v for k, v in _L1_ffn_all.items() if k in ('rmsnorm_weight', 'Wg', 'Wu', 'Wd')}
    del _L1_ffn_all
    return {'x': x, 'ctx_4096': ctx_4096, 'L0_xattn_wq': _L0_xattn_in['wq'], 'L0_xattn_wk': _L0_xattn_in['wk'], 'L0_xattn_wv': _L0_xattn_in['wv'], 'L0_xattn_wo': _L0_xattn_in['wo'], 'L0_xattn_ln_w': _L0_xattn_in['ln_w'], 'L0_ffn_A_w': _L0_ffn_in['A_w'], 'L0_ffn_B_w': _L0_ffn_in['B_w'], 'L0_ffn_Wq_w': _L0_ffn_in['Wq_w'], 'L0_ffn_keys': _L0_ffn_in['keys'], 'L1_xattn_Wq': _L1_xattn_in['Wq'], 'L1_xattn_Wk': _L1_xattn_in['Wk'], 'L1_xattn_Wv': _L1_xattn_in['Wv'], 'L1_xattn_Wo': _L1_xattn_in['Wo'], 'L1_ffn_rmsnorm_weight': _L1_ffn_in['rmsnorm_weight'], 'L1_ffn_Wg': _L1_ffn_in['Wg'], 'L1_ffn_Wu': _L1_ffn_in['Wu'], 'L1_ffn_Wd': _L1_ffn_in['Wd']}

def reference(x, ctx_4096, L0_xattn_wq, L0_xattn_wk, L0_xattn_wv, L0_xattn_wo, L0_xattn_ln_w, L0_ffn_A_w, L0_ffn_B_w, L0_ffn_Wq_w, L0_ffn_keys, L1_xattn_Wq, L1_xattn_Wk, L1_xattn_Wv, L1_xattn_Wo, L1_ffn_rmsnorm_weight, L1_ffn_Wg, L1_ffn_Wu, L1_ffn_Wd):
    import jax
    import jax.numpy as jnp

    def _L0_xattn_ref(hidden_states, encoder_hidden_states, wq, wk, wv, wo, ln_w):
        import jax, jax.numpy as jnp
        import numpy as np
        HIDDEN = 512
        N_HEADS = 32
        N_KV_HEADS = 8
        HEAD_DIM = HIDDEN // N_HEADS
        N_REP = N_HEADS // N_KV_HEADS
        EPS = 1e-05

        def _rmsnorm(x, w):
            xf = x.astype(jnp.float32)
            var = jnp.mean(xf * xf, axis=-1, keepdims=True)
            return (xf * jax.lax.rsqrt(var + EPS)).astype(x.dtype) * w
        B, Qlen, _ = hidden_states.shape
        _, Klen, _ = encoder_hidden_states.shape
        x = _rmsnorm(hidden_states, ln_w)
        q = jnp.einsum('bqd,hd->bqh', x, wq).reshape(B, Qlen, N_HEADS, HEAD_DIM)
        k = jnp.einsum('bkd,hd->bkh', encoder_hidden_states, wk).reshape(B, Klen, N_KV_HEADS, HEAD_DIM)
        v = jnp.einsum('bkd,hd->bkh', encoder_hidden_states, wv).reshape(B, Klen, N_KV_HEADS, HEAD_DIM)
        q = q.transpose(0, 2, 1, 3)
        k = k.transpose(0, 2, 1, 3)
        v = v.transpose(0, 2, 1, 3)
        k = jnp.repeat(k, N_REP, axis=1)
        v = jnp.repeat(v, N_REP, axis=1)
        scores = jnp.einsum('bhqd,bhkd->bhqk', q, k) / np.sqrt(HEAD_DIM).astype(np.float32)
        attn = jax.nn.softmax(scores.astype(jnp.float32), axis=-1).astype(q.dtype)
        out = jnp.einsum('bhqk,bhkd->bhqd', attn, v)
        out = out.transpose(0, 2, 1, 3).reshape(B, Qlen, HIDDEN)
        return jnp.einsum('bqh,dh->bqd', out, wo)

    def _L0_ffn_ref(x, A_w, B_w, Wq_w, keys):
        import jax, jax.numpy as jnp
        import numpy as np
        IN_F = 512
        OUT_F = 512
        RANK = 8
        NUM_EXPERTS = 64
        TOP_K = 16
        ROUTER_DIM = 16
        ALPHA = 32
        SCALING = ALPHA / TOP_K
        BOTTLENECK = NUM_EXPERTS * RANK
        q = jnp.einsum('bsd,rd->bsr', x, Wq_w)
        scores = jnp.einsum('bsr,er->bse', q, keys)
        top_vals, top_idx = jax.lax.top_k(scores, TOP_K)
        top_w = jax.nn.softmax(top_vals, axis=-1)
        gate = jnp.sum(jax.nn.one_hot(top_idx, NUM_EXPERTS, dtype=top_w.dtype) * top_w[..., None], axis=-2)
        z = jnp.einsum('bsd,nd->bsn', x, A_w)
        z = z.reshape(*z.shape[:-1], NUM_EXPERTS, RANK)
        z_gated = (z * gate[..., None]).reshape(*z.shape[:-2], BOTTLENECK)
        out = jnp.einsum('bsn,on->bso', z_gated, B_w) * SCALING
        return out

    def _L1_xattn_ref(latents, context, Wq, Wk, Wv, Wo):
        import jax, jax.numpy as jnp
        import numpy as np
        B, Q, D = (8, 64, 512)
        CTX = 512
        H, KV, HD = (16, 4, 96)
        G = H // KV
        b, q_len, _ = latents.shape
        hidden = jnp.concatenate([context, latents], axis=1)
        s_len = hidden.shape[1]
        q = (latents @ Wq.T).reshape(b, q_len, H, HD)
        k = (hidden @ Wk.T).reshape(b, s_len, KV, HD)
        v = (hidden @ Wv.T).reshape(b, s_len, KV, HD)
        q = q.transpose(0, 2, 1, 3).reshape(b, KV, G, q_len, HD)
        k = k.transpose(0, 2, 1, 3)
        v = v.transpose(0, 2, 1, 3)
        scale = 1.0 / jnp.sqrt(jnp.asarray(HD, q.dtype))
        scores = jnp.einsum('bkgqd,bksd->bkgqs', q, k) * scale
        attn = jax.nn.softmax(scores.astype(jnp.float32), axis=-1).astype(q.dtype)
        out = jnp.einsum('bkgqs,bksd->bkgqd', attn, v)
        out = out.reshape(b, H, q_len, HD).transpose(0, 2, 1, 3).reshape(b, q_len, H * HD)
        return out @ Wo.T

    def _L1_ffn_ref(hidden_states, rmsnorm_weight, Wg, Wu, Wd):
        import jax, jax.numpy as jnp
        import numpy as np
        EPS = 1e-06
        QMAX = 127.0

        def _quant_act(x):
            s = jnp.max(jnp.abs(x), axis=-1, keepdims=True) / QMAX
            s = jnp.maximum(s, 1e-08)
            q = jnp.clip(jnp.round(x / s), -QMAX, QMAX)
            return (q, s)

        def _quant_w(W):
            ws = jnp.max(jnp.abs(W), axis=1, keepdims=True) / QMAX
            ws = jnp.maximum(ws, 1e-08)
            Wq = jnp.clip(jnp.round(W / ws), -QMAX, QMAX)
            return (Wq, ws)
        B, S, D = hidden_states.shape
        x = hidden_states.reshape(B * S, D)
        x = x * jax.lax.rsqrt(jnp.mean(x * x, axis=-1, keepdims=True) + EPS)
        x = x * rmsnorm_weight
        q, s = _quant_act(x)
        Wgq, wsg = _quant_w(Wg)
        Wuq, wsu = _quant_w(Wu)
        gate = jnp.einsum('td,id->ti', q, Wgq) * s * wsg.T
        up = jnp.einsum('td,id->ti', q, Wuq) * s * wsu.T
        h = jax.nn.silu(gate) * up
        q2, s2 = _quant_act(h)
        Wdq, wsd = _quant_w(Wd)
        out = jnp.einsum('ti,di->td', q2, Wdq) * s2 * wsd.T
        return out.reshape(B, S, D)
    x = x + _L0_xattn_ref(_layernorm(x, axis=-1), ctx_4096, L0_xattn_wq, L0_xattn_wk, L0_xattn_wv, L0_xattn_wo, L0_xattn_ln_w)
    x = x + _L0_ffn_ref(_layernorm(x, axis=-1), L0_ffn_A_w, L0_ffn_B_w, L0_ffn_Wq_w, L0_ffn_keys)
    x = x + _L1_xattn_ref(_layernorm(x, axis=-1), ctx_4096, L1_xattn_Wq, L1_xattn_Wk, L1_xattn_Wv, L1_xattn_Wo)
    x = x + _L1_ffn_ref(_layernorm(x, axis=-1), L1_ffn_rmsnorm_weight, L1_ffn_Wg, L1_ffn_Wu, L1_ffn_Wd)
    return x

_drawn_inputs = setup_inputs


def setup_inputs(seed=0):
    import zlib

    import numpy as np

    out = dict(_drawn_inputs(seed))
    spreads = {'L0_xattn_ln_w': (1.0, 0.6)}
    factors = {'L0_xattn_wq': 6.52,
     'L0_xattn_wk': 6.523,
     'L1_xattn_Wq': 5.128,
     'L1_xattn_Wk': 5.109,
     'L1_ffn_rmsnorm_weight': 3.417}
    for name, (base, spread) in spreads.items():
        noise = np.random.default_rng([zlib.crc32(name.encode()), seed]).standard_normal(out[name].shape)
        drawn = base * np.exp(spread * noise) if base else spread * noise
        out[name] = jnp.asarray(drawn.astype(out[name].dtype))
    for name, factor in factors.items():
        out[name] = (out[name] * factor).astype(out[name].dtype)
    return out
```

```python
from contextlib import ExitStack

import numpy as np

import concourse.bass as bass
from concourse import mybir

F32 = mybir.dt.float32
F16 = mybir.dt.float16
ACT = mybir.ActivationFunctionType
ALU = mybir.AluOpType
AX = mybir.AxisListType.X

P = 128
B, QL, D = 4, 256, 512
CTX = 1601
DC = D // P
TOK = B * QL
TT = TOK // P
QT = QL // P
BANK = 512
S_KEY = QL + CTX
LN_EPS = 1e-5


def cdiv(a, b):
    return -(-a // b)


class Layer:

    def __init__(self, heads, kv, hd, latents_are_keys, parts, scales):
        self.H, self.G, self.HD = heads, kv, hd
        self.R = heads // kv
        self.K0 = 0 if latents_are_keys else QL
        self.NK = S_KEY - self.K0
        self.T = cdiv(self.NK, P)
        self.DO = heads * hd
        self.CO = self.DO // P
        self.KV = kv * hd
        self.parts = parts
        self.sq, self.sk, self.sv, self.so = scales
        self.stacked = parts == 1
        self.VW = 32 if self.stacked else hd + 1
        self.heads_per_tile = P // hd if self.stacked else 1
        self.MQ = P if self.stacked else hd
        self.NQ = self.DO // self.MQ
        self.NKT = self.KV // self.MQ

    def rows(self, t):
        return min(P, self.NK - t * P)


def wait(eng, sem, value):
    if not (isinstance(value, int) and value <= 0):
        eng.wait_ge(sem, value)


def chunks(n, step):
    return [(a, min(step, n - a)) for a in range(0, n, step)]


def attention(nc, L, x_sb, ident32, ident16, ctxT, w, ln_w, tag):
    wq, wk, wv, wo = w
    G, R, T, CO, VW, HD = L.G, L.R, L.T, L.CO, L.VW, L.HD
    KCH = chunks(L.NK, BANK)
    NC = len(KCH)
    JOBS = R * QT * NC
    SHIFT = 96
    KR = SHIFT + 2

    qper = BANK // QL
    first = [("T", j) for j in range(QT)]
    first += [("K", (m, n)) for m in range(L.NKT) for n in range(NC)]
    first += [("Q", n) for n in range(L.NQ // qper)]
    first += [("V", t) for t in range(T)]
    second = [("A", (j, n)) for j in range(QT) for n in range(CO // 4)] + [("O", j) for j in range(QT)]
    groups = first + second
    by_act = [k in "TKQVA" for k, _ in groups]
    by_dve = [k in "TKQAO" for k, _ in groups]
    NA, ND, NG = sum(by_act), sum(by_dve), len(groups)

    ctx = ExitStack()
    sb = lambda name, shape, dt: ctx.enter_context(nc.sbuf_tensor(f"{tag}_{name}", shape, dt))
    sem = lambda name: ctx.enter_context(nc.semaphore(f"{tag}_{name}"))
    with ctx:
        stage = sb("stage", [P, 2, CTX], F32)
        hT_flat = sb("hT", [P, 2, DC * S_KEY], F16)
        hT = hT_flat[:, :, :].rearrange("p s (c n) -> p s c n", c=DC)
        if L.stacked:
            k_tile = sb("k", [P, 1, G, L.NK], F16)
            q_tile = sb("q", [P, 1, G, R * QL], F16)
            k_flat = sb("k_flat", [P, 2, L.NK], F16)
            q_flat = sb("q_flat", [P, 2, L.NQ, QL], F16)
        else:
            k_tile = sb("k", [KR, 2, G, L.NK], F16)
            q_tile = sb("q", [KR, 2, G, R * QL], F16)
        v_all = sb("v", [P, T, G, VW], F32)
        v_g = sb("v_g", [P, 2, T, VW], F32) if L.stacked else None
        p_buf = sb("p", [P, 2, R * QL], F32)
        wqT = sb("wqT", [P, 2, DC, L.DO], F16)
        wkT = sb("wkT", [P, 2, DC, L.KV], F16)
        wvT = sb("wvT", [P, 2, DC, L.KV], F16)
        woT = sb("woT", [P, 2, CO, D], F16)
        scratch = sb("scratch", [P, 1024], F32)
        xn = scratch[:, :].rearrange("p (j n) -> p j n", j=QT)
        attn_flat = hT_flat[:, 1, :].bitcast(F32)
        attn = attn_flat[:, 0:QT * L.DO].rearrange("p (j n) -> p j n", j=QT)
        aT_flat = hT_flat[:, 0, :]
        aT = [aT_flat[:, i * CO * QL:(i + 1) * CO * QL].rearrange("p (c n) -> p c n", c=CO) for i in range(2)]
        lnw = sb("lnw", [P, D], F32) if ln_w is not None else None
        stats = sb("stats", [P, QT, 6], F32)
        mv = sb("mv", [P, QT, 2], F32)
        var = sb("var", [P, QT], F32)
        std = sb("std", [P, QT], F32)
        rstd = sb("rstd", [P, QT], F32)
        mpart = sb("mpart", [P, R * QT, NC], F32)
        negm = sb("negm", [P, R * QT], F32)
        mm = sb("mm", [P, R * QT, 2], F16)
        rec = sb("rec", [P, R * QT], F32)

        psum = ctx.enter_context(nc.psum_tensor(f"{tag}_ps", [P, 8, BANK], F32))
        st = [psum[:, 2 * i:2 * i + 2, :] for i in range(2)]
        oT = psum[:, 4:6, :]
        mx = psum[:, 6:8, :]

        s_w = [sem(f"loaded{i}") for i in range(2)]
        s_lnw = sem("lnw_in")
        s_const = sem("const")
        s_hi = sem("hi")
        s_lo = sem("lo")
        s_var = sem("var_ready")
        s_std = sem("std_ready")
        s_xn = sem("xn_ready")
        s_pg = sem("product")
        s_ga = sem("act_took")
        s_gd = sem("dve_took")
        s_kq = sem("kq_placed")
        s_vg = sem("v_placed")
        s_mx = sem("mx")
        s_red = sem("red")
        s_m = sem("m_ready")
        s_sh = sem("shift_turned")
        s_shc = sem("shift_placed")
        s_st = sem("st")
        s_exp = sem("exp")
        s_pv = sem("pv")
        s_otc = sem("oT_taken")
        s_tr = sem("o_turned")
        s_norm = sem("o_normed")
        s_step = sem("dve_step")

        witems = []
        for src, dst, scale, nchunk, width in ((wq, wqT, L.sq, DC, L.DO), (wk, wkT, L.sk, DC, L.KV),
                                               (wv, wvT, L.sv, DC, L.KV), (wo, woT, L.so, CO, D)):
            per = CTX // width
            for c in range(0, nchunk, per):
                m = min(per, nchunk - c)
                witems.append((src.rearrange("(c p) n -> p c n", p=P)[:, c:c + m, :],
                               dst[:, 0, c:c + m, :], dst[:, 1, c:c + m, :], scale, m, width))
        NW = len(witems)
        assert NW % 2 == 0

        def stage_of(i, m, width):
            return stage[:, i % 2, 0:m * width].rearrange("p (c n) -> p c n", c=m)

        def run_phases(eng, phase):
            if L.stacked:
                phase(0, 0, True, True)
                with eng.Fori(0, G // 2 - 1) as i:
                    phase(2 * i + 1, 1, True, False)
                    phase(2 * i + 2, 0, True, False)
                phase(G - 1, 1, False, False)
            else:
                for g in range(G):
                    phase(g, g % 2, g < G - 1, g == 0)

        block = ctx.enter_context(nc.Block())

        @block.sync
        def _(sp):
            if lnw is not None:
                sp.dma_start(lnw[:, :], ln_w.partition_broadcast(P)).then_inc(s_lnw, 16)
            for i, (src, _, _, _, m, width) in enumerate(witems):
                wait(sp, s_lo, i - 1)
                sp.dma_start(stage_of(i, m, width), src).then_inc(s_w[i % 2], 16)
            with sp.Fori(0, B) as b:
                for c in range(DC):
                    sp.wait_ge(s_lo, NW + b * DC + c - 1)
                    sp.dma_start(stage[:, c % 2, :], ctxT[b, c * P:(c + 1) * P, :]).then_inc(s_w[c % 2], 16)
                if L.stacked:
                    last_k = max(i for i, (k, _) in enumerate(groups) if k in "KQ")
                    sp.wait_ge(s_gd, b * ND + sum(by_dve[:last_k + 1]))
                    sp.wait_ge(s_ga, b * NA + sum(by_act[:last_k + 1]))
                    for s, (kp, qp) in enumerate(((0, 0), (0, 1), (1, 0))):
                        for g in range(G):
                            sp.dma_start(k_tile[s * HD:(s + 1) * HD, 0, g, :],
                                         k_flat[g * HD:(g + 1) * HD, kp, :]).then_inc(s_kq, 16)
                        for h in range(L.heads_per_tile):
                            dst = q_tile[s * HD:(s + 1) * HD, 0, :, :].rearrange(
                                "p (m a) (r q) -> p m a r q", m=L.NQ, r=R)[:, :, h // R, h % R, :]
                            sp.dma_start(dst, q_flat[h * HD:(h + 1) * HD, qp, :, :]).then_inc(s_kq, 16)

        NKQ = 16 * 3 * (G + L.heads_per_tile) if L.stacked else 0

        NCONST = 5 if L.stacked else 2

        @block.gpsimd
        def _(pool):
            n = 0
            if L.stacked:
                for tile in (k_tile[:, 0, :, :], q_tile[:, 0, :, :], v_all[:, :, :, :]):
                    pool.memset(tile, 0.0).then_inc(s_const, 1)
                    n += 1
                    pool.wait_ge(s_const, n)
            pool.memset(k_tile[SHIFT:KR, 0, :, :], 1.0).then_inc(s_const, 1)
            pool.wait_ge(s_const, n + 1)
            pool.memset(v_all[:, :, :, HD:HD + 1], 1.0).then_inc(s_const, 1)
            if L.stacked:
                last_v = NG - len(second)

                def copy(b, g, par, used):
                    pool.wait_ge(s_ga, b * NA + sum(by_act[:last_v]))
                    if used:
                        pool.wait_ge(s_pv, b * (G * T) + (g - 1) * T)
                    pool.tensor_copy(v_g[:, par, :, :], v_all[:, :, g, :]).then_inc(s_vg, 1)

                copy(0, 0, 0, False)
                copy(0, 1, 1, False)
                with pool.Fori(1, G // 2) as i:
                    copy(0, 2 * i, 0, True)
                    copy(0, 2 * i + 1, 1, True)
                with pool.Fori(1, B) as b:
                    with pool.Fori(0, G // 2) as i:
                        copy(b, 2 * i, 0, True)
                        copy(b, 2 * i + 1, 1, True)

        @block.scalar
        def _(act):
            for i, (_, hi, _, scale, m, width) in enumerate(witems):
                act.wait_ge(s_w[i % 2], 16 * (i // 2 + 1))
                act.activation(hi, stage_of(i, m, width), ACT.Copy, scale=scale).then_inc(s_hi, 1)
            act.wait_ge(s_const, NCONST)
            with act.Fori(0, B) as b:
                nroot = 2 if lnw is not None else 1
                act.wait_ge(s_var, b * nroot + 1)
                act.activation(std[:, :], var[:, :], ACT.Sqrt).then_inc(s_std, 1)
                for c in range(DC):
                    act.wait_ge(s_w[c % 2], 16 * (NW // 2 + c // 2 + 1) + b * (16 * (DC // 2)))
                    act.activation(hT[:, 0, c, QL:S_KEY], stage[:, c % 2, :], ACT.Copy).then_inc(s_hi, 1)
                if nroot == 2:
                    act.wait_ge(s_var, b * nroot + 2)
                    act.activation(std[:, :], var[:, :], ACT.Sqrt).then_inc(s_std, 1)

                def take(i):
                    kind, at = groups[i]
                    bank = psum[:, i % 8, :]
                    act.wait_ge(s_pg, b * NG + i + 1)
                    if kind == "T":
                        act.activation(hT[:, 0, :, at * P:(at + 1) * P],
                                       bank.rearrange("p (c n) -> p c n", c=DC), ACT.Copy).then_inc(s_ga, 1)
                    elif kind == "K":
                        m, n = at
                        a, ln = KCH[n]
                        dst = k_flat[:, 0, a:a + ln] if L.stacked else k_tile[0:HD, 0, m, a:a + ln]
                        act.activation(dst, bank[0:L.MQ, 0:ln], ACT.Copy, scale=1.0 / L.sk).then_inc(s_ga, 1)
                    elif kind == "Q":
                        if L.stacked:
                            dst = q_flat[:, 0, qper * at:qper * at + qper, :]
                        else:
                            dst = q_tile[0:HD, 0, :, :].rearrange("p g (r q) -> p (g r) q", q=QL)[
                                :, qper * at:qper * at + qper, :]
                        act.activation(dst, bank[0:L.MQ, :].rearrange("p (h q) -> p h q", q=QL),
                                       ACT.Copy, scale=1.0 / L.sq).then_inc(s_ga, 1)
                    elif kind == "V":
                        n = L.rows(at)
                        act.activation(v_all[0:n, at, :, 0:HD],
                                       bank[0:n, 0:L.KV].rearrange("p (g d) -> p g d", g=G),
                                       ACT.Copy, scale=1.0 / L.sv).then_inc(s_ga, 1)
                    elif kind == "A":
                        j, n = at
                        act.activation(aT[0][:, 4 * n:4 * n + 4, j * P:(j + 1) * P],
                                       bank.rearrange("p (c n) -> p c n", c=4), ACT.Copy).then_inc(s_ga, 1)

                for i in range(len(first)):
                    if by_act[i]:
                        take(i)

                def place_shift(g):
                    act.wait_ge(s_sh, b * G + g + 1)
                    act.activation(q_tile[SHIFT:KR, 0, g, :], mx[SHIFT:KR, :, :].rearrange("p a n -> p (a n)"),
                                   ACT.Copy).then_inc(s_shc, 1)

                def phase(g, par, more, start):
                    for t in range(T):
                        e = b * (G * T) + g * T + t
                        n = L.rows(t)
                        buf = (par + t) % 2
                        act.wait_ge(s_st, e + 1)
                        if not (start and t < 2):
                            act.wait_ge(s_pv, e - 1)
                        act.activation(p_buf[0:n, buf, :], st[buf][0:n, :, :].rearrange("p a n -> p (a n)"),
                                       ACT.Exp, scale=float(HD) ** -0.5).then_inc(s_exp, 1)
                        if more and t == T - 2:
                            place_shift(g + 1)

                place_shift(0)
                run_phases(act, phase)
                for i in range(len(first), NG):
                    if by_act[i]:
                        take(i)

        rms = lnw is not None
        STEPS = 2 * QT + 1 + (2 * QT + 1 if rms else 0) + G * 3

        @block.vector
        def _(dve):
            for i, (_, hi, lo, scale, m, width) in enumerate(witems):
                dve.wait_ge(s_hi, i + 1)
                dve.scalar_tensor_tensor(lo, stage_of(i, m, width), scale, hi, ALU.mult,
                                         ALU.subtract).then_inc(s_lo, 1)
            if rms:
                dve.wait_ge(s_lnw, 16)
            with dve.Fori(0, B) as b:
                step = [0]

                def after(ins):
                    step[0] += 1
                    ins.then_inc(s_step, 1)

                def settle():
                    dve.wait_ge(s_step, b * STEPS + step[0])

                for j in range(QT):
                    after(dve.bn_stats(stats[:, j, :], x_sb[:, b * QT + j, :]))
                dve.drain()
                for j in range(QT):
                    after(dve.bn_aggr(mv[:, j, :], stats[:, j, :]))
                settle()
                dve.tensor_scalar(var[:, :], mv[:, :, 1], LN_EPS, None, ALU.add).then_inc(s_var, 1)
                nroot = 2 if rms else 1
                for c in range(DC):
                    dve.wait_ge(s_hi, NW + b * DC + c + 1)
                    dve.tensor_tensor(hT[:, 1, c, QL:S_KEY], stage[:, c % 2, :], hT[:, 0, c, QL:S_KEY],
                                      ALU.subtract).then_inc(s_lo, 1)
                dve.wait_ge(s_std, b * nroot + 1)
                after(dve.reciprocal(rstd[:, :], std[:, :]))
                settle()
                for j in range(QT):
                    ins = dve.tensor_scalar(xn[:, j, :], x_sb[:, b * QT + j, :], mv[:, j, 0:1], rstd[:, j:j + 1],
                                            ALU.subtract, ALU.mult)
                    if rms:
                        after(ins)
                    else:
                        ins.then_inc(s_xn, 1)
                if rms:
                    settle()
                    for j in range(QT):
                        after(dve.tensor_tensor_reduce(p_buf[:, j, 0:D], xn[:, j, :], xn[:, j, :], 1.0, 0.0,
                                                       ALU.mult, ALU.add, std[:, j:j + 1]))
                    settle()
                    dve.tensor_scalar(var[:, :], std[:, :], 1.0 / D, 1e-5, ALU.mult, ALU.add).then_inc(s_var, 1)
                    dve.wait_ge(s_std, b * nroot + 2)
                    after(dve.reciprocal(rstd[:, :], std[:, :]))
                    settle()
                    for j in range(QT):
                        dve.scalar_tensor_tensor(xn[:, j, :], xn[:, j, :], rstd[:, j:j + 1], lnw[:, :],
                                                 ALU.mult, ALU.mult).then_inc(s_xn, 1)

                def take(i):
                    kind, at = groups[i]
                    bank = psum[:, i % 8, :]
                    if kind == "O":
                        dve.wait_ge(s_pg, b * NG + i + 1)
                        dve.scalar_tensor_tensor(x_sb[:, b * QT + at, :], bank, 1.0 / L.so,
                                                 x_sb[:, b * QT + at, :], ALU.mult, ALU.add).then_inc(s_gd, 1)
                        return
                    dve.wait_ge(s_ga, b * NA + sum(by_act[:i + 1]))
                    if kind == "T":
                        src, scale = bank.rearrange("p (c n) -> p c n", c=DC), 1.0
                        hi, lo = (hT[:, s, :, at * P:(at + 1) * P] for s in range(2))
                    elif kind == "K":
                        m, n = at
                        a, ln = KCH[n]
                        src, scale = bank[0:L.MQ, 0:ln], 1.0 / L.sk
                        if L.stacked:
                            hi, lo = (k_flat[:, s, a:a + ln] for s in range(2))
                        else:
                            hi, lo = (k_tile[0:HD, s, m, a:a + ln] for s in range(2))
                    elif kind == "Q":
                        src, scale = bank[0:L.MQ, :].rearrange("p (h q) -> p h q", q=QL), 1.0 / L.sq
                        if L.stacked:
                            hi, lo = (q_flat[:, s, qper * at:qper * at + qper, :] for s in range(2))
                        else:
                            hi, lo = (q_tile[0:HD, s, :, :].rearrange("p g (r q) -> p (g r) q", q=QL)[
                                :, qper * at:qper * at + qper, :] for s in range(2))
                    else:
                        j, n = at
                        src, scale = bank.rearrange("p (c n) -> p c n", c=4), 1.0
                        hi, lo = (aT[s][:, 4 * n:4 * n + 4, j * P:(j + 1) * P] for s in range(2))
                    dve.scalar_tensor_tensor(lo, src, scale, hi, ALU.mult, ALU.subtract).then_inc(s_gd, 1)

                for i in range(len(first)):
                    if by_dve[i]:
                        take(i)

                def maxima(g):
                    for k in range(JOBS):
                        m, n = divmod(k, NC)
                        n_red = b * (G * JOBS) + g * JOBS + k
                        dve.wait_ge(s_mx, n_red + 1)
                        dve.tensor_reduce(mpart[:, m, n:n + 1], mx[:, k % 2, 0:KCH[n][1]], AX,
                                          ALU.max).then_inc(s_red, 1)
                    dve.wait_ge(s_red, b * (G * JOBS) + g * JOBS + JOBS)
                    base = b * STEPS + step[0]
                    return base

                def shift(g, base, k):
                    dve.tensor_reduce(negm[:, :], mpart[:, :, :], AX, ALU.max, negate=True).then_inc(s_step, 1)
                    dve.wait_ge(s_step, base + k + 1)
                    dve.tensor_copy(mm[:, :, 0], negm[:, :]).then_inc(s_step, 1)
                    dve.wait_ge(s_step, base + k + 2)
                    dve.tensor_tensor(mm[:, :, 1], negm[:, :], mm[:, :, 0], ALU.subtract).then_inc(s_m, 1)

                def norm(g, base, k):
                    dve.wait_ge(s_tr, b * G + g + 1)
                    if L.stacked:
                        o = mx[:, 0, 0:QT * P].rearrange("p (j r n) -> p j r n", j=QT, r=R)
                        r4 = rec[:, :].rearrange("p (j r o) -> p j r o", j=QT, o=1)
                        dve.reciprocal(r4, o[:, :, :, HD:HD + 1]).then_inc(s_step, 1)
                        dve.wait_ge(s_step, base + k + 1)
                        dst = attn[:, :, bass.ds(g * (R * HD), R * HD)].rearrange("p j (r d) -> p j r d", r=R)
                        dve.tensor_tensor(dst, o[:, :, :, 0:HD], r4.to_broadcast([P, QT, R, HD]),
                                          ALU.mult).then_inc(s_norm, 1)
                    else:
                        o = mx[:, :, 0:4 * VW].rearrange("p a (m n) -> p a m n", m=4)
                        r4 = rec[:, :].rearrange("p (a m o) -> p a m o", a=2, o=1)
                        dve.reciprocal(r4, o[:, :, :, HD:HD + 1]).then_inc(s_step, 1)
                        dve.wait_ge(s_step, base + k + 1)
                        for a in range(2):
                            dst = attn[:, :, (g * R + 2 * a) * HD:(g * R + 2 * a + 2) * HD].rearrange(
                                "p j (r d) -> p r j d", r=2)
                            src = o[:, a, :, 0:HD].rearrange("p (r j) d -> p r j d", r=2)
                            rb = rec[:, 4 * a:4 * a + 4].rearrange("p (r j o) -> p r j o", r=2, o=1)
                            dve.tensor_tensor(dst, src, rb.to_broadcast([P, 2, QT, HD]),
                                              ALU.mult).then_inc(s_norm, 1)

                def take_oT(g):
                    dve.wait_ge(s_pv, b * (G * T) + g * T + T)
                    if L.stacked:
                        dst, src = scratch[:, 0:QL], oT[:, 0, 0:QL]
                    else:
                        dst, src = scratch[0:VW, :], oT[0:VW, :, :].rearrange("p a n -> p (a n)")
                    if not (isinstance(g, int) and g == 0):
                        dve.wait_ge(s_tr, b * G + g)
                    dve.tensor_copy(dst, src).then_inc(s_otc, 1)

                own = b * STEPS + step[0]
                base = maxima(0)
                shift(0, own, 0)

                def phase(g, par, more, start):
                    here = own + 2 + g * 3 - (0 if start else 1)
                    k = 0
                    if not start:
                        norm(g - 1, here, 0)
                        k = 1
                    if more:
                        maxima(g + 1)
                        shift(g + 1, here, k)
                    take_oT(g)

                run_phases(dve, phase)
                norm(G - 1, own + 2 + (G - 1) * 3, 0)
                for i in range(len(first), NG):
                    if by_dve[i]:
                        take(i)

        NORMS = 1 if L.stacked else 2

        @block.tensor
        def _(pe):
            pe.wait_ge(s_const, NCONST)
            with pe.Fori(0, B) as b:
                def product(i):
                    kind, at = groups[i]
                    bank = psum[:, i % 8, :]
                    if i >= 8:
                        if by_dve[i - 8]:
                            pe.wait_ge(s_gd, b * ND + sum(by_dve[:i - 7]))
                        else:
                            pe.wait_ge(s_ga, b * NA + sum(by_act[:i - 7]))
                    if kind == "T":
                        pe.wait_ge(s_xn, b * QT + at + 1)
                        for c in range(DC):
                            ins = pe.transpose(bank[:, c * P:(c + 1) * P], xn[:, at, c * P:(c + 1) * P], ident32)
                    elif kind in "KQV":
                        if groups[i - 1][0] == "T":
                            pe.wait_ge(s_lo, NW + b * DC + DC)
                            pe.wait_ge(s_gd, b * ND + QT)
                        ops = []
                        for c in range(DC):
                            for wp, xp in ((0, 0), (0, 1), (1, 0)):
                                ops.append((c, wp, xp))
                        if kind == "K":
                            m, n = at
                            a, ln = KCH[n]
                            for o, (c, wp, xp) in enumerate(ops):
                                ins = pe.matmul(bank[0:L.MQ, 0:ln], wkT[:, wp, c, m * L.MQ:(m + 1) * L.MQ],
                                                hT[:, xp, c, L.K0 + a:L.K0 + a + ln],
                                                start=o == 0, stop=o == len(ops) - 1)
                        elif kind == "Q":
                            for u in range(qper):
                                m = at * qper + u
                                for o, (c, wp, xp) in enumerate(ops):
                                    ins = pe.matmul(bank[0:L.MQ, u * QL:(u + 1) * QL],
                                                    wqT[:, wp, c, m * L.MQ:(m + 1) * L.MQ],
                                                    hT[:, xp, c, 0:QL], start=o == 0, stop=o == len(ops) - 1)
                        else:
                            n = L.rows(at)
                            for o, (c, wp, xp) in enumerate(ops):
                                ins = pe.matmul(bank[0:n, 0:L.KV], hT[:, xp, c, L.K0 + at * P:L.K0 + at * P + n],
                                                wvT[:, wp, c, :], start=o == 0, stop=o == len(ops) - 1)
                    elif kind == "A":
                        j, n = at
                        for c in range(4):
                            s = (4 * n + c) * P
                            ins = pe.transpose(bank[:, c * P:(c + 1) * P], attn[:, j, s:s + P], ident32)
                    else:
                        if at == 0:
                            pe.wait_ge(s_gd, b * ND + sum(by_dve[:NG - QT]))
                        o = 0
                        for c in range(CO):
                            for wp, xp in ((0, 0), (0, 1), (1, 0)):
                                ins = pe.matmul(bank, aT[xp][:, c, at * P:(at + 1) * P], woT[:, wp, c, :],
                                                start=o == 0, stop=o == 3 * CO - 1)
                                o += 1
                    ins.then_inc(s_pg, 1)

                for i in range(len(first)):
                    product(i)
                pe.wait_ge(s_ga, b * NA + sum(by_act[:len(first)]))
                pe.wait_ge(s_gd, b * ND + sum(by_dve[:len(first)]))
                if L.stacked:
                    pe.wait_ge(s_kq, (b + 1) * NKQ)

                def max_job(g, k, head):
                    m, n = divmod(k, NC)
                    a, ln = KCH[n]
                    done = b * (G * JOBS) + g * JOBS + k
                    if k >= 2:
                        pe.wait_ge(s_red, done - 1)
                    elif head == 1:
                        pe.wait_ge(s_shc, b * G + g)
                    elif head >= 2:
                        pe.wait_ge(s_norm, (b * G + g - 1) * NORMS)
                    pe.matmul(mx[:, k % 2, 0:ln], q_tile[0:SHIFT, 0, g, m * P:(m + 1) * P],
                              k_tile[0:SHIFT, 0, g, a:a + ln], start=True, stop=True).then_inc(s_mx, 1)

                def turn_shift(g):
                    pe.wait_ge(s_m, b * G + g + 1)
                    for m in range(R * QT):
                        ins = pe.matmul(mx[SHIFT:KR, m // 4, (m % 4) * P:(m % 4 + 1) * P], mm[:, m, :], ident16,
                                        start=True, stop=True, tile_position=(0, SHIFT))
                    ins.then_inc(s_sh, 1)

                def score_T(g, t, par, start):
                    e = b * (G * T) + g * T + t
                    n = L.rows(t)
                    if not (start and t < 2):
                        pe.wait_ge(s_exp, e - 1)
                    if t == 0:
                        pe.wait_ge(s_shc, b * G + g + 1)
                    buf = (par + t) % 2
                    passes = ((0, 0),) if L.stacked else ((0, 0), (0, 1), (1, 0))
                    for h in range(2):
                        for o, (kp, qp) in enumerate(passes):
                            kr = KR if o == 0 else HD
                            ins = pe.matmul(st[buf][0:n, h, :], k_tile[0:kr, kp, g, t * P:t * P + n],
                                            q_tile[0:kr, qp, g, h * BANK:(h + 1) * BANK],
                                            start=o == 0, stop=o == len(passes) - 1)
                    ins.then_inc(s_st, 1)

                def p_v(g, t, par):
                    e = b * (G * T) + g * T + t
                    n = L.rows(t)
                    pe.wait_ge(s_exp, e + 1)
                    buf = (par + t) % 2
                    if L.stacked:
                        if t == 0:
                            pe.wait_ge(s_vg, b * G + g + 1)
                        for r in range(R):
                            ins = pe.matmul(oT[32 * r:32 * r + VW, 0, 0:QL], v_g[0:n, par, t, :],
                                            p_buf[0:n, buf, r * QL:(r + 1) * QL], start=t == 0, stop=t == T - 1,
                                            tile_position=(0, 32 * r))
                    else:
                        for h in range(2):
                            ins = pe.matmul(oT[0:VW, h, :], v_all[0:n, t, g, :],
                                            p_buf[0:n, buf, h * BANK:(h + 1) * BANK],
                                            start=t == 0, stop=t == T - 1)
                    ins.then_inc(s_pv, 1)

                def turn_o(g):
                    pe.wait_ge(s_otc, b * G + g + 1)
                    if L.stacked:
                        for j in range(QT):
                            ins = pe.transpose(mx[:, 0, j * P:(j + 1) * P], scratch[:, j * P:(j + 1) * P], ident32)
                    else:
                        for m in range(R * QT):
                            ins = pe.transpose(mx[:, m // 4, (m % 4) * VW:(m % 4 + 1) * VW],
                                               scratch[0:VW, m * P:(m + 1) * P], ident32[0:VW, 0:VW])
                    ins.then_inc(s_tr, 1)

                for k in range(JOBS):
                    max_job(0, k, 0)
                turn_shift(0)
                slots = T - 3

                def phase(g, par, more, start):
                    score_T(g, 0, par, start)
                    done = 0
                    for t in range(T):
                        if t + 1 < T:
                            score_T(g, t + 1, par, start)
                        if t == 0 and not start:
                            turn_o(g - 1)
                        if more:
                            upto = min(JOBS, cdiv(JOBS * (t + 1), slots))
                            for k in range(done, upto):
                                max_job(g + 1, k, 1 if start else 2)
                            done = upto
                            if t == T - 2:
                                turn_shift(g + 1)
                        p_v(g, t, par)

                run_phases(pe, phase)
                turn_o(G - 1)
                pe.wait_ge(s_norm, (b + 1) * G * NORMS)
                for i in range(len(first), NG):
                    product(i)


def routed_ffn(nc, x_sb, ident32, wA, wB, wR, keysT, tag):
    E, RANK, RD, SCALING = 64, 8, 16, 2.0
    NB = E * RANK
    SW = 64.0
    NEG = -3.0e38
    ctx = ExitStack()
    sb = lambda name, shape, dt: ctx.enter_context(nc.sbuf_tensor(f"{tag}_{name}", shape, dt))
    sem = lambda name: ctx.enter_context(nc.semaphore(f"{tag}_{name}"))
    with ctx:
        wa32 = sb("wa32", [P, DC, NB], F32)
        wb32 = sb("wb32", [P, NB // P, D], F32)
        wr32 = sb("wr32", [P, DC, RD], F32)
        keys = sb("keys", [RD, E], F32)
        wa = sb("wa", [P, 2, DC, NB], F16)
        wb = sb("wb", [P, 2, NB // P, D], F16)
        wr = sb("wr", [P, 2, DC, RD], F16)
        xn = sb("xn", [P, D], F32)
        xT = sb("xT", [P, 2, DC, P], F16)
        zT = sb("zT", [P, 2, NB // P, P], F16)
        zg = sb("zg", [P, E, RANK], F32)
        qT = sb("qT", [RD, P], F32)
        sc = sb("sc", [P, E], F32)
        w1 = sb("w1", [P, E], F32)
        w2 = sb("w2", [P, E], F32)
        mask = sb("mask", [P, E], F32)
        ex = sb("ex", [P, E], F32)
        gm = sb("gm", [P, E], F32)
        gate = sb("gate", [P, E], F32)
        top = sb("top", [P, 2, 8], F32)
        stats = sb("stats", [P, 6], F32)
        mv = sb("mv", [P, 2], F32)
        small = sb("small", [P, 8], F32)
        psum = ctx.enter_context(nc.psum_tensor(f"{tag}_ps", [P, 6, BANK], F32))
        p_xT, p_q, p_s, p_z, p_zT, p_y = (psum[:, i, :] for i in range(6))

        s_in, s_hi, s_lo = sem("in"), sem("hi"), sem("lo")
        s_var, s_std, s_xn = sem("var"), sem("std"), sem("xn")
        s_xT, s_xhi, s_xlo = sem("xT"), sem("xhi"), sem("xlo")
        s_q, s_qc, s_s, s_z = sem("q"), sem("qc"), sem("s"), sem("z")
        s_nmax, s_ex, s_zg = sem("nmax"), sem("ex"), sem("zg")
        s_zT, s_zhi, s_zlo, s_y, s_x = sem("zT"), sem("zhi"), sem("zlo"), sem("y"), sem("x")
        s_step = sem("dve_step")
        block = ctx.enter_context(nc.Block())
        pairs = ((wa32, wa), (wb32, wb), (wr32, wr))

        @block.sync
        def _(sp):
            for dst, src in ((wa32, wA), (wb32, wB), (wr32, wR)):
                sp.dma_start(dst[:, :, :], src.rearrange("(c p) n -> p c n", p=P)).then_inc(s_in, 16)
            sp.dma_start(keys[:, :], keysT).then_inc(s_in, 16)

        @block.scalar
        def _(act):
            act.wait_ge(s_in, 64)
            for src, dst in pairs:
                act.activation(dst[:, 0, :, :], src[:, :, :], ACT.Copy, scale=SW).then_inc(s_hi, 1)
            with act.Fori(0, TT) as i:
                act.wait_ge(s_var, i + 1)
                act.activation(small[:, 1:2], small[:, 0:1], ACT.Sqrt).then_inc(s_std, 1)
                act.wait_ge(s_xT, i + 1)
                act.activation(xT[:, 0, :, :], p_xT.rearrange("p (c n) -> p c n", c=DC), ACT.Copy).then_inc(s_xhi, 1)
                act.wait_ge(s_q, i + 1)
                act.activation(qT[:, :], p_q[0:RD, 0:P], ACT.Copy, scale=1.0 / SW).then_inc(s_qc, 1)
                act.wait_ge(s_nmax, i + 1)
                act.activation(ex[:, :], sc[:, :], ACT.Exp, bias=small[:, 3:4]).then_inc(s_ex, 1)
                act.wait_ge(s_zT, i + 1)
                act.activation(zT[:, 0, :, :], p_zT.rearrange("p (c n) -> p c n", c=NB // P),
                               ACT.Copy).then_inc(s_zhi, 1)

        STEPS = 7

        @block.vector
        def _(dve):
            for n, (src, dst) in enumerate(pairs):
                dve.wait_ge(s_hi, n + 1)
                dve.scalar_tensor_tensor(dst[:, 1, :, :], src[:, :, :], SW, dst[:, 0, :, :], ALU.mult,
                                         ALU.subtract).then_inc(s_lo, 1)
            with dve.Fori(0, TT) as i:
                count = [0]

                def step(ins):
                    count[0] += 1
                    ins.then_inc(s_step, 1)
                    dve.wait_ge(s_step, i * STEPS + count[0])

                dve.bn_stats(stats[:, :], x_sb[:, i, :])
                dve.drain()
                step(dve.bn_aggr(mv[:, :], stats[:, :]))
                dve.tensor_scalar(small[:, 0:1], mv[:, 1:2], LN_EPS, None, ALU.add).then_inc(s_var, 1)
                dve.wait_ge(s_std, i + 1)
                step(dve.reciprocal(small[:, 2:3], small[:, 1:2]))
                dve.tensor_scalar(xn[:, :], x_sb[:, i, :], mv[:, 0:1], small[:, 2:3], ALU.subtract,
                                  ALU.mult).then_inc(s_xn, 1)
                dve.wait_ge(s_xhi, i + 1)
                dve.tensor_tensor(xT[:, 1, :, :], p_xT.rearrange("p (c n) -> p c n", c=DC), xT[:, 0, :, :],
                                  ALU.subtract).then_inc(s_xlo, 1)
                dve.wait_ge(s_s, i + 1)
                dve.tensor_copy(sc[:, :], p_s[:, 0:E])
                dve.drain()
                step(dve.max(top[:, 0, :], sc[:, :]))
                dve.tensor_scalar(small[:, 3:4], top[:, 0, 0:1], -1.0, None, ALU.mult).then_inc(s_nmax, 1)
                dve.match_replace(w1[:, :], top[:, 0, :], sc[:, :], NEG)
                dve.drain()
                dve.max(top[:, 1, :], w1[:, :])
                dve.drain()
                step(dve.match_replace(w2[:, :], top[:, 1, :], w1[:, :], NEG))
                step(dve.tensor_scalar(mask[:, :], w2[:, :], NEG, None, ALU.is_equal))
                dve.wait_ge(s_ex, i + 1)
                step(dve.tensor_tensor_reduce(gm[:, :], ex[:, :], mask[:, :], 1.0, 0.0, ALU.mult, ALU.add,
                                              small[:, 4:5]))
                step(dve.reciprocal(small[:, 5:6], small[:, 4:5]))
                dve.tensor_scalar(gate[:, :], gm[:, :], small[:, 5:6], SCALING / SW, ALU.mult,
                                  ALU.mult).then_inc(s_zg, 1)
                dve.wait_ge(s_zg, 2 * i + 1)
                dve.wait_ge(s_z, i + 1)
                dve.tensor_tensor(zg[:, :, :], p_z.rearrange("p (e r) -> p e r", r=RANK),
                                  gate[:, :].rearrange("p (e o) -> p e o", o=1).to_broadcast([P, E, RANK]),
                                  ALU.mult).then_inc(s_zg, 1)
                dve.wait_ge(s_zhi, i + 1)
                dve.tensor_tensor(zT[:, 1, :, :], p_zT.rearrange("p (c n) -> p c n", c=NB // P), zT[:, 0, :, :],
                                  ALU.subtract).then_inc(s_zlo, 1)
                dve.wait_ge(s_y, i + 1)
                dve.scalar_tensor_tensor(x_sb[:, i, :], p_y, 1.0 / SW, x_sb[:, i, :], ALU.mult,
                                         ALU.add).then_inc(s_x, 1)
                assert count[0] == STEPS

        @block.tensor
        def _(pe):
            pe.wait_ge(s_lo, len(pairs))
            with pe.Fori(0, TT) as i:
                ops = [(c, wp, xp) for c in range(DC) for wp, xp in ((0, 0), (0, 1), (1, 0))]
                pe.wait_ge(s_xn, i + 1)
                for c in range(DC):
                    ins = pe.transpose(p_xT[:, c * P:(c + 1) * P], xn[:, c * P:(c + 1) * P], ident32)
                ins.then_inc(s_xT, 1)
                pe.wait_ge(s_xlo, i + 1)
                for o, (c, wp, xp) in enumerate(ops):
                    ins = pe.matmul(p_q[0:RD, 0:P], wr[:, wp, c, :], xT[:, xp, c, :], start=o == 0,
                                    stop=o == len(ops) - 1)
                ins.then_inc(s_q, 1)
                for o, (c, wp, xp) in enumerate(ops):
                    ins = pe.matmul(p_z, xT[:, xp, c, :], wa[:, wp, c, :], start=o == 0, stop=o == len(ops) - 1)
                ins.then_inc(s_z, 1)
                pe.wait_ge(s_qc, i + 1)
                pe.matmul(p_s[:, 0:E], qT[:, :], keys[:, :], start=True, stop=True).then_inc(s_s, 1)
                pe.wait_ge(s_zg, 2 * i + 2)
                zf = zg[:, :, :].rearrange("p e r -> p (e r)")
                for c in range(NB // P):
                    ins = pe.transpose(p_zT[:, c * P:(c + 1) * P], zf[:, c * P:(c + 1) * P], ident32)
                ins.then_inc(s_zT, 1)
                pe.wait_ge(s_zlo, i + 1)
                for o, (c, wp, xp) in enumerate(ops):
                    ins = pe.matmul(p_y, zT[:, xp, c, :], wb[:, wp, c, :], start=o == 0, stop=o == len(ops) - 1)
                ins.then_inc(s_y, 1)


def int8_ffn(nc, x_sb, ident32, ident16, norm_w, Wg, Wu, Wd, out, tag):
    I = Wg.shape[0]
    IT = cdiv(I, P)
    ICH = chunks(I, BANK)
    QMAX, FLOOR, EPS = 127.0, 1e-8, 1e-6
    ROUND = 1.5 * 2.0 ** 23
    ctx = ExitStack()
    sb = lambda name, shape, dt: ctx.enter_context(nc.sbuf_tensor(f"{tag}_{name}", shape, dt))
    sem = lambda name: ctx.enter_context(nc.semaphore(f"{tag}_{name}"))
    with ctx:
        wgT = sb("wgT", [P, DC, I], F16)
        wuT = sb("wuT", [P, DC, I], F16)
        wdT = sb("wdT", [P, IT, D], F16)
        wsg = sb("wsg", [P, I], F32)
        wsu = sb("wsu", [P, I], F32)
        wsd = sb("wsd", [P, D], F32)
        items = []
        for W, dst, row, width in ((Wg, wgT, wsg, D), (Wu, wuT, wsu, D), (Wd, wdT, wsd, I)):
            for a, n in chunks(W.shape[0], P):
                items.append((W[a:a + n, :], dst, row, a, n, width))
        NI = len(items)
        raw = sb("raw", [P, 2, I], F32)
        work = sb("work", [P, I], F32)
        quant = sb("quant", [P, 2, I], F16)
        wsc = sb("wsc", [P, 4], F32)
        wcol = sb("wcol", [P, P], F32)
        ones = sb("ones", [P, P], F32)
        nw = sb("nw", [P, D], F32)
        xn = sb("xn", [P, D], F32)
        xr = sb("xr", [P, D], F32)
        xq = sb("xq", [P, D], F16)
        xqT = sb("xqT", [P, DC, P], F16)
        gl = sb("gl", [P, I], F32)
        ul = sb("ul", [P, I], F32)
        hq = sb("hq", [P, I], F16)
        hqT = sb("hqT", [P, IT, P], F16)
        res = sb("res", [P, D], F32)
        stats = sb("stats", [P, 6], F32)
        mv = sb("mv", [P, 2], F32)
        sm = sb("sm", [P, 12], F32)
        pbig = ctx.enter_context(nc.psum_tensor(f"{tag}_pb", [P, 6, BANK], F32))
        ptr = ctx.enter_context(nc.psum_tensor(f"{tag}_pt", [P, 1024], F16))
        py = ctx.enter_context(nc.psum_tensor(f"{tag}_py", [P, BANK], F32))

        s_raw = [sem("raw0"), sem("raw1")]
        s_nw, s_out = sem("nw"), sem("out")
        s_wq, s_wt, s_wc, s_wr, s_wb, s_step = sem("wq"), sem("wt"), sem("wc"), sem("wr"), sem("wb"), sem("step")
        s_ones = sem("ones")
        s_var, s_std, s_xq, s_xT, s_xTc = sem("var"), sem("std"), sem("xq"), sem("xT"), sem("xTc")
        s_gu, s_gl, s_sl, s_hq, s_hT, s_hTc, s_y, s_x = (sem(n) for n in ("gu", "gl", "sl", "hq", "hT", "hTc", "y", "x"))
        batches = []
        for n, it in enumerate(items):
            for a, m in chunks(cdiv(it[5], P), 8):
                batches.append((n, a, m))
        block = ctx.enter_context(nc.Block())

        @block.sync
        def _(sp):
            sp.dma_start(nw[:, :], norm_w.partition_broadcast(P)).then_inc(s_nw, 16)
            for n, (src, _, _, a, m, width) in enumerate(items):
                wait(sp, s_wq, n - 1)
                sp.dma_start(raw[0:m, n % 2, 0:width], src).then_inc(s_raw[n % 2], 16)
            with sp.Fori(0, TT) as i:
                sp.wait_ge(s_x, i + 1)
                sp.dma_start(out[bass.ds(i * P, P), :], x_sb[:, i, :]).then_inc(s_out, 16)
            sp.wait_ge(s_out, 16 * TT)

        @block.gpsimd
        def _(pool):
            pool.memset(ones[:, :], 1.0).then_inc(s_ones, 1)

        @block.scalar
        def _(act):
            for k, (n, a, m) in enumerate(batches):
                _, dst, _, col, rows, width = items[n]
                act.wait_ge(s_wt, k + 1)
                full = m if (a + m) * P <= width else m - 1
                src = ptr[:, 0:m * P].rearrange("p (c n) -> p c n", c=m)
                last = None
                if full:
                    last = act.activation(dst[:, a:a + full, col:col + rows], src[:, 0:full, 0:rows], ACT.Copy)
                if full < m:
                    if last is not None:
                        last.then_inc(s_wc, 1)
                    part = width - (a + full) * P
                    last = act.activation(dst[0:part, a + full, col:col + rows], src[0:part, full, 0:rows], ACT.Copy)
                last.then_inc(s_wc, 1)
            with act.Fori(0, TT) as i:
                for k in range(2):
                    act.wait_ge(s_var, 2 * i + k + 1)
                    act.activation(sm[:, 1:2], sm[:, 0:1], ACT.Sqrt).then_inc(s_std, 1)
                act.wait_ge(s_xT, i + 1)
                act.activation(xqT[:, :, :], ptr[:, 0:DC * P].rearrange("p (c n) -> p c n", c=DC),
                               ACT.Copy).then_inc(s_xTc, 1)
                act.wait_ge(s_gl, i + 1)
                act.activation(gl[:, :], gl[:, :], ACT.Silu, scale=sm[:, 4:5]).then_inc(s_sl, 1)
                for k, (a, m) in enumerate(chunks(IT, 8)):
                    act.wait_ge(s_hT, 2 * i + k + 1)
                    src = ptr[:, 0:m * P].rearrange("p (c n) -> p c n", c=m)
                    full = m if (a + m) * P <= I else m - 1
                    act.activation(hqT[:, a:a + full, :], src[:, 0:full, :], ACT.Copy).then_inc(s_hTc, 1)
                    if full < m:
                        part = I - (a + full) * P
                        act.activation(hqT[0:part, a + full, :], src[0:part, full, :], ACT.Copy).then_inc(s_hTc, 1)

        WSTEPS = 5
        XSTEPS = 19

        @block.vector
        def _(dve):
            def quantise(step, rows, width, src, scale, inverse, tmp, dst):
                step(dve.tensor_reduce(scale, src, AX, ALU.max, apply_absolute_value=True))
                step(dve.tensor_scalar(scale, scale, 1.0 / QMAX, FLOOR, ALU.mult, ALU.max))
                step(dve.reciprocal(inverse, scale))
                step(dve.tensor_scalar(tmp, src, inverse, QMAX, ALU.mult, ALU.min))
                step(dve.tensor_scalar(tmp, tmp, -QMAX, ROUND, ALU.max, ALU.add))
                return dve.tensor_scalar(dst, tmp, ROUND, None, ALU.subtract)

            dve.wait_ge(s_ones, 1)
            for n, (_, _, row, a, m, width) in enumerate(items):
                count = [0]

                def wstep(ins):
                    count[0] += 1
                    ins.then_inc(s_step, 1)
                    dve.wait_ge(s_step, n * WSTEPS + count[0])

                dve.wait_ge(s_raw[n % 2], 16 * (n // 2 + 1))
                if n >= 2:
                    dve.wait_ge(s_wt, sum(1 for t in batches if t[0] <= n - 2))
                quantise(wstep, m, width, raw[0:m, n % 2, 0:width], wsc[0:m, 0:1], wsc[0:m, 1:2],
                         work[0:m, 0:width], quant[0:m, n % 2, 0:width]).then_inc(s_wq, 1)
                wait(dve, s_wr, n)
                dve.tensor_scalar(wcol[0:m, :], ones[0:m, :], wsc[0:m, 0:1], None, ALU.mult).then_inc(s_wb, 1)
                dve.wait_ge(s_wr, n + 1)
                dve.tensor_copy(row[:, a:a + m], py[:, 0:m]).then_inc(s_wb, 1)
                assert count[0] == WSTEPS
            dve.wait_ge(s_wq, NI)
            dve.wait_ge(s_wb, 2 * NI)
            dve.wait_ge(s_nw, 16)
            with dve.Fori(0, TT) as i:
                count = [0]

                def step(ins):
                    count[0] += 1
                    ins.then_inc(s_step, 1)
                    dve.wait_ge(s_step, NI * WSTEPS + i * XSTEPS + count[0])

                dve.bn_stats(stats[:, :], x_sb[:, i, :])
                dve.drain()
                step(dve.bn_aggr(mv[:, :], stats[:, :]))
                dve.tensor_scalar(sm[:, 0:1], mv[:, 1:2], LN_EPS, None, ALU.add).then_inc(s_var, 1)
                dve.wait_ge(s_std, 2 * i + 1)
                step(dve.reciprocal(sm[:, 2:3], sm[:, 1:2]))
                step(dve.tensor_scalar(xn[:, :], x_sb[:, i, :], mv[:, 0:1], sm[:, 2:3], ALU.subtract, ALU.mult))
                step(dve.tensor_tensor_reduce(xr[:, :], xn[:, :], xn[:, :], 1.0, 0.0, ALU.mult, ALU.add, sm[:, 3:4]))
                dve.tensor_scalar(sm[:, 0:1], sm[:, 3:4], 1.0 / D, EPS, ALU.mult, ALU.add).then_inc(s_var, 1)
                dve.wait_ge(s_std, 2 * i + 2)
                step(dve.reciprocal(sm[:, 2:3], sm[:, 1:2]))
                step(dve.scalar_tensor_tensor(xr[:, :], xn[:, :], sm[:, 2:3], nw[:, :], ALU.mult, ALU.mult))
                quantise(step, P, D, xr[:, :], sm[:, 4:5], sm[:, 5:6], xn[:, :], xq[:, :]).then_inc(s_xq, 1)
                dve.wait_ge(s_gu, 2 * i + 1)
                dve.tensor_tensor(gl[:, :], pbig[:, 0:3, :].rearrange("p a n -> p (a n)")[:, 0:I], wsg[:, :],
                                  ALU.mult).then_inc(s_gl, 1)
                dve.wait_ge(s_gu, 2 * i + 2)
                step(dve.tensor_tensor(ul[:, :], pbig[:, 3:6, :].rearrange("p a n -> p (a n)")[:, 0:I], wsu[:, :],
                                       ALU.mult))
                dve.wait_ge(s_sl, i + 1)
                step(dve.scalar_tensor_tensor(ul[:, :], ul[:, :], sm[:, 4:5], gl[:, :], ALU.mult, ALU.mult))
                quantise(step, P, I, ul[:, :], sm[:, 6:7], sm[:, 7:8], work[:, :], hq[:, :]).then_inc(s_hq, 1)
                dve.wait_ge(s_y, i + 1)
                step(dve.scalar_tensor_tensor(res[:, :], py[:, :], sm[:, 6:7], wsd[:, :], ALU.mult, ALU.mult))
                dve.tensor_tensor(x_sb[:, i, :], res[:, :], x_sb[:, i, :], ALU.add).then_inc(s_x, 1)
                assert count[0] == XSTEPS, count[0]

        @block.tensor
        def _(pe):
            taken = 0
            k = 0
            for n, (_, dst, row, col, rows, width) in enumerate(items):
                pe.wait_ge(s_wq, n + 1)
                for a, m in chunks(cdiv(width, P), 8):
                    wait(pe, s_wc, taken)
                    for c in range(m):
                        w = min(P, width - (a + c) * P)
                        ins = pe.transpose(ptr[0:w, c * P:c * P + rows],
                                           quant[0:rows, n % 2, (a + c) * P:(a + c) * P + w], ident16[0:rows, 0:rows])
                    ins.then_inc(s_wt, 1)
                    full = m if (a + m) * P <= width else m - 1
                    taken += (1 if full else 0) + (1 if full < m else 0)
                    k += 1
                pe.wait_ge(s_wb, 2 * n + 1)
                pe.matmul(py[:, 0:rows], wcol[0:rows, :], ident32[0:rows, 0:rows], start=True,
                          stop=True).then_inc(s_wr, 1)
            pe.wait_ge(s_wc, taken)
            pe.wait_ge(s_wb, 2 * NI)
            with pe.Fori(0, TT) as i:
                pe.wait_ge(s_xq, i + 1)
                for c in range(DC):
                    ins = pe.transpose(ptr[:, c * P:(c + 1) * P], xq[:, c * P:(c + 1) * P], ident16)
                ins.then_inc(s_xT, 1)
                pe.wait_ge(s_xTc, i + 1)
                for half, w in enumerate((wgT, wuT)):
                    for n, (a, m) in enumerate(ICH):
                        for c in range(DC):
                            ins = pe.matmul(pbig[:, 3 * half + n, 0:m], xqT[:, c, :], w[:, c, a:a + m],
                                            start=c == 0, stop=c == DC - 1)
                    ins.then_inc(s_gu, 1)
                pe.wait_ge(s_hq, i + 1)
                for k, (a, m) in enumerate(chunks(IT, 8)):
                    if k == 1:
                        pe.wait_ge(s_hTc, 3 * i + 1)
                    for c in range(m):
                        w = min(P, I - (a + c) * P)
                        ins = pe.transpose(ptr[0:w, c * P:(c + 1) * P], hq[:, (a + c) * P:(a + c) * P + w], ident16)
                    ins.then_inc(s_hT, 1)
                pe.wait_ge(s_hTc, 3 * i + 3)
                for c in range(IT):
                    w = min(P, I - c * P)
                    ins = pe.matmul(py[:, :], hqT[0:w, c, :], wdT[0:w, c, :], start=c == 0, stop=c == IT - 1)
                ins.then_inc(s_y, 1)


def build(nc, a, out, upto=4, start=0):
    with ExitStack() as ctx:
        sb = lambda name, shape, dt: ctx.enter_context(nc.sbuf_tensor(name, shape, dt))
        x_sb = sb("x_sb", [P, TT, D], F32)
        id32 = sb("id32", [P, P], F32)
        id16 = sb("id16", [P, P], F16)
        s_x = ctx.enter_context(nc.semaphore("x_in"))
        s_id = ctx.enter_context(nc.semaphore("ident"))
        with nc.Block() as block:
            @block.sync
            def _(sp):
                sp.dma_start(x_sb[:, :, :], a["x"].rearrange("(t p) n -> p t n", p=P)).then_inc(s_x, 16)
                sp.wait_ge(s_x, 16)

            @block.gpsimd
            def _(pool):
                pool.memset(id32[:, :], 0.0).then_inc(s_id, 1)
                pool.memset(id16[:, :], 0.0).then_inc(s_id, 1)
                pool.wait_ge(s_id, 2)
                for m in (id32, id16):
                    pool.affine_select(out=m[:, :], in_=m[:, :], compare_op=ALU.not_equal, fill=1.0, base=0,
                                       pattern=[[-1, P]], channel_multiplier=1).then_inc(s_id, 1)
        ident32, ident16 = id32[:, :], id16[:, :]
        L0 = Layer(32, 8, 16, False, 1, (16.0, 16.0, 64.0, 64.0))
        L1 = Layer(16, 4, 96, True, 3, (16.0, 16.0, 64.0, 64.0))
        if upto >= 1 > start:
            attention(nc, L0, x_sb, ident32, ident16, a["ctxT"], (a["wq0"], a["wk0"], a["wv0"], a["wo0"]),
                      a["ln_w"], "a0")
        if upto >= 2 > start:
            routed_ffn(nc, x_sb, ident32, a["wA"], a["wB"], a["wR"], a["keysT"], "f0")
        if upto >= 3 > start:
            attention(nc, L1, x_sb, ident32, ident16, a["ctxT"], (a["wq1"], a["wk1"], a["wv1"], a["wo1"]), None, "a1")
        if upto >= 4 > start:
            int8_ffn(nc, x_sb, ident32, ident16, a["norm_w"], a["Wg"], a["Wu"], a["Wd"], out, "f1")
        else:
            s_dbg = ctx.enter_context(nc.semaphore("dbg"))
            with nc.Block() as block:
                @block.sync
                def _(sp):
                    sp.dma_start(out.rearrange("(t p) n -> p t n", p=P), x_sb[:, :, :]).then_inc(s_dbg, 16)
                    sp.wait_ge(s_dbg, 16)


def lay_out(x, ctx_4096, L0_xattn_wq, L0_xattn_wk, L0_xattn_wv, L0_xattn_wo, L0_xattn_ln_w, L0_ffn_A_w, L0_ffn_B_w,
            L0_ffn_Wq_w, L0_ffn_keys, L1_xattn_Wq, L1_xattn_Wk, L1_xattn_Wv, L1_xattn_Wo, L1_ffn_rmsnorm_weight,
            L1_ffn_Wg, L1_ffn_Wu, L1_ffn_Wd):
    n = np.asarray
    t = lambda w: np.ascontiguousarray(n(w).T)
    return {
        "x": n(x).reshape(TOK, D), "ctxT": np.ascontiguousarray(n(ctx_4096).transpose(0, 2, 1)),
        "wq0": t(L0_xattn_wq), "wk0": t(L0_xattn_wk), "wv0": t(L0_xattn_wv), "wo0": t(L0_xattn_wo),
        "ln_w": n(L0_xattn_ln_w), "wA": t(L0_ffn_A_w), "wB": t(L0_ffn_B_w), "wR": t(L0_ffn_Wq_w),
        "keysT": t(L0_ffn_keys), "wq1": t(L1_xattn_Wq), "wk1": t(L1_xattn_Wk), "wv1": t(L1_xattn_Wv),
        "wo1": t(L1_xattn_Wo), "norm_w": n(L1_ffn_rmsnorm_weight), "Wg": n(L1_ffn_Wg), "Wu": n(L1_ffn_Wu),
        "Wd": n(L1_ffn_Wd),
    }


def kernel(**inputs):
    import concourse.bacc as bacc
    from concourse.bass_utils import run_bass_kernel_spmd

    nc = bacc.Bacc("TRN2", target_bir_lowering=False, num_devices=1)
    arrays = lay_out(**inputs)
    aps = {k: nc.dram_tensor(f"in_{k}", v.shape, mybir.dt.from_np(v.dtype), kind="ExternalInput").ap()
           for k, v in arrays.items()}
    out = nc.dram_tensor("out", (TOK, D), F32, kind="ExternalOutput").ap()
    build(nc, aps, out)
    r = run_bass_kernel_spmd(nc, [{f"in_{k}": v for k, v in arrays.items()}], core_ids=[0])
    return r.results[0]["out"].reshape(B, QL, D)
```

```python
from contextlib import ExitStack

import numpy as np

import concourse.bass as bass
from concourse import mybir

F32 = mybir.dt.float32
F16 = mybir.dt.float16
ACT = mybir.ActivationFunctionType
ALU = mybir.AluOpType
AX = mybir.AxisListType.X

P = 128
B, QL, D = 4, 256, 512
CTX = 1601
DC = D // P
TOK = B * QL
TT = TOK // P
QT = QL // P
BANK = 512
S_KEY = QL + CTX
LN_EPS = 1e-5


def cdiv(a, b):
    return -(-a // b)


class Layer:

    def __init__(self, heads, kv, hd, latents_are_keys, parts, scales):
        self.H, self.G, self.HD = heads, kv, hd
        self.R = heads // kv
        self.K0 = 0 if latents_are_keys else QL
        self.NK = S_KEY - self.K0
        self.T = cdiv(self.NK, P)
        self.DO = heads * hd
        self.CO = self.DO // P
        self.KV = kv * hd
        self.parts = parts
        self.sq, self.sk, self.sv, self.so = scales
        self.stacked = parts == 1
        self.VW = 32 if self.stacked else hd + 1
        self.heads_per_tile = P // hd if self.stacked else 1
        self.MQ = P if self.stacked else hd
        self.NQ = self.DO // self.MQ
        self.NKT = self.KV // self.MQ

    def rows(self, t):
        return min(P, self.NK - t * P)


def wait(eng, sem, value):
    if not (isinstance(value, int) and value <= 0):
        eng.wait_ge(sem, value)


def chunks(n, step):
    return [(a, min(step, n - a)) for a in range(0, n, step)]


def split_items(src, dst, scale):
    _, _, nchunk, width = dst.shape
    per = max(m for m in range(1, nchunk + 1) if nchunk % m == 0 and m * width <= CTX)
    return [(src.rearrange("(c p) n -> p c n", p=P)[:, c:c + per, :], dst[:, 0, c:c + per, :],
             dst[:, 1, c:c + per, :], scale, per, width) for c in range(0, nchunk, per)]


def attention(nc, L, x_sb, id32, id16, ctxT, wqkv, wo, ln_w, tag, x_in=None, own=(), later=()):
    G, R, T, CO, VW, HD = L.G, L.R, L.T, L.CO, L.VW, L.HD
    KCH = chunks(L.NK, BANK)
    NC = len(KCH)
    JOBS = R * QT * NC
    SHIFT = 96
    KR = SHIFT + 2
    RQ = R * QL
    NP, NMX = 5, 3
    NST = 4 if L.stacked else 3
    BOOST = 0.0 if L.stacked else 1024.0
    lift = float(np.log(BOOST) * HD ** 0.5) if BOOST else 0.0

    qper = BANK // QL
    fresh = [n for n in range(NC) if L.K0 > 0 or n > 0]
    first = [("K", (m, n)) for n in fresh for m in range(L.NKT)]
    first += [("T", j) for j in range(QT)]
    first += [("K", (m, n)) for n in range(NC) if n not in fresh for m in range(L.NKT)]
    first += [("Q", n) for n in range(L.NQ // qper)]
    NKQP = len(first)
    first += [("V", t) for t in range(T)]
    second = [("A", (j, n)) for j in range(QT) for n in range(CO // 4)] + [("O", j) for j in range(QT)]
    groups = first + second
    by_act = [k in "TKQVA" for k, _ in groups]
    by_dve = [k in "TKQAO" or (k == "V" and not L.stacked) for k, _ in groups]
    NA, ND, NG = sum(by_act), sum(by_dve), len(groups)
    opening, done = [("P", i) for i in range(NKQP)], 0
    for t in range(T):
        opening.append(("P", NKQP + t))
        upto = cdiv(JOBS * max(0, t - 1), T - 2)
        opening += [("M", k) for k in range(done, upto)]
        done = upto
    SLOTS = T - 3

    def jobs_beside(t):
        return range(min(JOBS, cdiv(JOBS * t, SLOTS)), min(JOBS, cdiv(JOBS * (t + 1), SLOTS)))

    def score_bank(par, t, h):
        return (2 * ((par + t) % 2) + h) if L.stacked else (2 * t + h) % 3

    ctx = ExitStack()
    sb = lambda name, shape, dt: ctx.enter_context(nc.sbuf_tensor(f"{tag}_{name}", shape, dt))
    sem = lambda name: ctx.enter_context(nc.semaphore(f"{tag}_{name}"))
    with ctx:
        wqT, wkT, wvT = wqkv
        woT = sb("woT", [P, 2, CO, D], F16)
        stage = sb("stage", [P, 2, CTX], F32)
        hT = sb("hT", [P, 2, DC, S_KEY], F16)
        q_raw = sb("q", [P, G, (1 if L.stacked else 2) * RQ], F16)
        q_tile = q_raw[:, :, :].rearrange("p g (s n) -> p s g n", n=RQ)
        if L.stacked:
            k_tile = sb("k", [P, 1, G, L.NK], F16)
            k_flat = sb("k_flat", [P, 2, L.NK], F16)
            q_flat = sb("q_flat", [P, 2, L.NQ, QL], F16)
            v_all = sb("v", [P, T, G, VW], F32)
            v_g = sb("v_g", [P, 2, T, VW], F32)
            p_buf = sb("p", [P, 2, RQ], F32)
            attn = sb("attn", [P, QT, L.DO], F32)
            aT_raw = sb("aT", [P, 2 * CO * QL], F16)[:, :]
            attn_block = lambda j, c: attn[:, j, c * P:(c + 1) * P]
        else:
            k_raw = sb("k", [P, 2, G * L.NK], F16)
            k_tile = k_raw[:, :, :].rearrange("p s (g n) -> p s g n", g=G)
            v_all = sb("v", [P, 2, T, G, VW], F16)
            p32 = sb("p32", [P, 2, BANK], F32)
            p_buf = sb("p", [P, 2, 2, RQ], F16)
            attn_g = q_raw[:, :, :].bitcast(F32)[:, :, 0:QT * R * HD].rearrange("p g (j n) -> p g j n", j=QT)
            aT_raw = k_raw[:, 1, 0:2 * CO * QL]
            per_g = R * HD // P
            attn_block = lambda j, c: attn_g[:, c // per_g, j, (c % per_g) * P:(c % per_g + 1) * P]
        aT = aT_raw.rearrange("p (s c n) -> p s c n", s=2, c=CO)
        scratch = sb("scratch", [P, RQ], F32)
        xn = scratch[:, :].rearrange("p (j n) -> p j n", j=QT)
        lnw = sb("lnw", [P, D], F32) if ln_w is not None else None
        one = sb("one", [P, 1], F32)
        stats = sb("stats", [P, QT, 6], F32)
        mv = sb("mv", [P, QT, 2], F32)
        var = sb("var", [P, QT], F32)
        std = sb("std", [P, QT], F32)
        rstd = sb("rstd", [P, QT], F32)
        mpart = sb("mpart", [P, R * QT, NC], F32)
        negm = sb("negm", [P, R * QT], F32)
        mm = sb("mm", [P, R * QT, 2], F16)
        rec = sb("rec", [P, R * QT], F32)

        psum = ctx.enter_context(nc.psum_tensor(f"{tag}_ps", [P, 8, BANK], F32))
        oT = psum[:, 4:5, :] if L.stacked else psum[:, 3:5, :]
        mx = psum[:, NP:8, :]

        s_w = [sem(f"loaded{i}") for i in range(2)]
        s_x = sem("x_in")
        s_lnw = sem("lnw_in")
        s_const = sem("const")
        s_hi = sem("hi")
        s_lo = sem("lo")
        s_ctx = sem("context")
        s_pool = sem("pool_step")
        s_var = sem("var_ready")
        s_std = sem("std_ready")
        s_xn = sem("xn_ready")
        s_pg = sem("product")
        s_ga = sem("act_took")
        s_gd = sem("dve_took")
        s_kq = sem("kq_placed")
        s_kd, s_qd = sem("k_in_dram"), sem("q_in_dram")
        s_vg = sem("v_placed")
        s_mx = sem("mx")
        s_red = sem("red")
        s_m = sem("m_ready")
        s_sh = sem("shift_turned")
        s_shc = sem("shift_placed")
        s_st = sem("st")
        s_exp = sem("exp")
        s_plo = sem("p_lo")
        s_pv = sem("pv")
        s_otc = sem("oT_taken")
        s_tr = sem("o_turned")
        s_norm = sem("o_normed")
        s_step = sem("dve_step")

        items = [it for w in own[1:] for it in w]
        items += [(ctxT[0, c * P:(c + 1) * P, :], hT[:, 0, c, QL:S_KEY], hT[:, 1, c, QL:S_KEY], 1.0, 1, CTX)
                  for c in range(DC)]
        is_ctx = [False] * (len(items) - DC) + [True] * DC
        rest = [it for w in own[:1] for it in w] + split_items(wo, woT, L.so)
        items += rest
        is_ctx += [False] * len(rest)
        NI, NW = len(items), len(items) - DC
        assert NI % 2 == 0 and len(later) % 2 == 0

        def stage_of(i, m, width):
            return stage[:, i % 2, 0:m * width].rearrange("p (c n) -> p c n", c=m)

        def shaped(ap, m):
            return ap.rearrange("p (c n) -> p c n", c=1) if len(ap.shape) == 2 else ap

        NKQ = 16 * 3 * (1 + L.NQ) if L.stacked else 0
        NKD = max(i for i, (k, _) in enumerate(groups) if k == "K") + 1
        if L.stacked:
            k_dram = nc.dram_tensor(f"{tag}_k_parts", (2, P, L.NK), F16, kind="Internal").ap()
            q_dram = nc.dram_tensor(f"{tag}_q_parts", (2, P, L.NQ * QL), F16, kind="Internal").ap()

        def q_dst(part, at):
            if L.stacked:
                return q_flat[:, part, qper * at:qper * at + qper, :]
            g, r = divmod(qper * at, R)
            return q_tile[0:HD, part, g, r * QL:(r + qper) * QL].rearrange("p (h q) -> p h q", q=QL)

        def run_phases(eng, phase):
            if L.stacked:
                phase(0, 0, True, True)
                with eng.Fori(0, G // 2 - 1) as i:
                    phase(2 * i + 1, 1, True, False)
                    phase(2 * i + 2, 0, True, False)
                phase(G - 1, 1, False, False)
            else:
                for g in range(G):
                    phase(g, g % 2, g < G - 1, g == 0)

        block = ctx.enter_context(nc.Block())

        @block.sync
        def _(sp):
            for i, (src, _, _, _, m, width) in enumerate(items):
                if i >= 2:
                    sp.wait_ge(s_ctx if is_ctx[i - 2] else s_lo,
                               sum(1 for c in is_ctx[:i - 1] if c == is_ctx[i - 2]))
                sp.dma_start(stage_of(i, m, width), shaped(src, m)).then_inc(s_w[i % 2], 16)
                if i == 1 and x_in is not None:
                    sp.dma_start(x_sb[:, :, :], x_in.rearrange("(t p) n -> p t n", p=P)).then_inc(s_x, 16)
                if i == 1 and lnw is not None:
                    sp.dma_start(lnw[:, :], ln_w.partition_broadcast(P)).then_inc(s_lnw, 16)
            sp.wait_ge(s_lo, NW)

            def place_kq(b, again):
                if again:
                    sp.wait_ge(s_kq, b * NKQ)
                sp.wait_ge(s_gd, b * ND + sum(by_dve[:NKD]))
                for part in range(2):
                    sp.dma_start(k_dram[part], k_flat[:, part, :]).then_inc(s_kd, 16)
                sp.wait_ge(s_gd, b * ND + sum(by_dve[:NKQP]))
                for part in range(2):
                    sp.dma_start(q_dram[part], q_flat[:, part, :, :].rearrange("p m q -> p (m q)")).then_inc(s_qd, 16)
                sp.wait_ge(s_kd, (b + 1) * 32)
                for s, part in enumerate((0, 0, 1)):
                    sp.dma_start(k_tile[s * HD:(s + 1) * HD, 0, :, :],
                                 k_dram[part].rearrange("(g d) n -> d g n", d=HD)).then_inc(s_kq, 16)
                sp.wait_ge(s_qd, (b + 1) * 32)
                for s, part in enumerate((0, 1, 0)):
                    for m in range(L.NQ):
                        dst = q_tile[s * HD:(s + 1) * HD, 0, :, :].rearrange("p g n -> p (g n)")[
                            :, m * L.heads_per_tile * QL:(m + 1) * L.heads_per_tile * QL]
                        src = q_dram[part][:, m * QL:(m + 1) * QL].rearrange("(h d) q -> d h q", d=HD)
                        sp.dma_start(dst.rearrange("p (h q) -> p h q", q=QL), src).then_inc(s_kq, 16)

            if L.stacked:
                place_kq(0, False)
            with sp.Fori(1, B) as b:
                for c in range(DC):
                    sp.wait_ge(s_ctx, b * DC + c - 1)
                    sp.dma_start(stage[:, c % 2, :], ctxT[b, c * P:(c + 1) * P, :]).then_inc(s_w[c % 2], 16)
                if L.stacked:
                    place_kq(b, True)
            for i, (src, _, _, _, m, width) in enumerate(later):
                sp.wait_ge(s_ctx, B * DC + i - 1)
                sp.dma_start(stage_of(i, m, width), src).then_inc(s_w[i % 2], 16)

        NCONST = (4 if x_in is not None else 0) + (6 if L.stacked else 4)

        @block.gpsimd
        def _(pool):
            sets = [(one[:, :], 1.0)]
            if x_in is not None:
                sets += [(id32[:, :], 0.0), (id16[:, :], 0.0)]
            if L.stacked:
                sets += [(k_tile[:, 0, :, :], 0.0), (q_tile[:, 0, :, :], 0.0), (v_all[:, :, :, :], 0.0)]
            sets.append((k_tile[SHIFT:KR, 0, :, :], 1.0))
            if L.stacked:
                sets.append((v_all[:, :, :, HD:HD + 1], 1.0))
            else:
                sets += [(v_all[:, 0, :, :, HD:HD + 1], 1.0), (v_all[:, 1, :, :, HD:HD + 1], 0.0)]
            for n, (ap, value) in enumerate(sets):
                wait(pool, s_const, n)
                pool.memset(ap, value).then_inc(s_const, 1)
            if x_in is not None:
                for n, m in enumerate((id32, id16)):
                    pool.wait_ge(s_const, len(sets) + n)
                    pool.affine_select(out=m[:, :], in_=m[:, :], compare_op=ALU.not_equal, fill=1.0, base=0,
                                       pattern=[[-1, P]], channel_multiplier=1).then_inc(s_const, 1)
            pool.wait_ge(s_const, NCONST)
            with pool.Fori(1, B) as b:
                for c in range(DC):
                    pool.wait_ge(s_w[c % 2], 16 * (NI // 2 + c // 2 + 1) + (b - 1) * (16 * (DC // 2)))
                    pool.wait_ge(s_pg, (b - 1) * NG + len(first))
                    pool.tensor_tensor(hT[:, 0, c, QL:S_KEY], stage[:, c % 2, :],
                                       one[:, :].to_broadcast([P, CTX]), ALU.mult).then_inc(s_pool, 1)
                    pool.wait_ge(s_pool, (b - 1) * DC + c + 1)
                    pool.tensor_tensor(hT[:, 1, c, QL:S_KEY], stage[:, c % 2, :], hT[:, 0, c, QL:S_KEY],
                                       ALU.subtract).then_inc(s_ctx, 1)
            for i, (_, hi, lo, scale, m, width) in enumerate(later):
                pool.wait_ge(s_w[i % 2], 16 * (NI // 2 + (B - 1) * DC // 2 + i // 2 + 1))
                pool.tensor_scalar(hi, stage_of(i, m, width), scale, 0.0, ALU.mult, ALU.add).then_inc(s_pool, 1)
                pool.wait_ge(s_pool, (B - 1) * DC + 2 * i + 1)
                pool.tensor_scalar(stage_of(i, m, width), stage_of(i, m, width), scale, 0.0, ALU.mult,
                                   ALU.add).then_inc(s_pool, 1)
                pool.wait_ge(s_pool, (B - 1) * DC + 2 * i + 2)
                pool.tensor_tensor(lo, stage_of(i, m, width), hi, ALU.subtract).then_inc(s_ctx, 1)

        @block.scalar
        def _(act):
            for i, (_, hi, _, scale, m, width) in enumerate(items):
                act.wait_ge(s_w[i % 2], 16 * (i // 2 + 1))
                act.activation(shaped(hi, m), stage_of(i, m, width), ACT.Copy, scale=scale).then_inc(s_hi, 1)
            act.wait_ge(s_const, NCONST)
            with act.Fori(0, B) as b:
                nroot = 2 if lnw is not None else 1
                for k in range(nroot):
                    act.wait_ge(s_var, b * nroot + k + 1)
                    act.activation(std[:, :], var[:, :], ACT.Sqrt).then_inc(s_std, 1)

                def take(i):
                    kind, at = groups[i]
                    bank = psum[:, i % NP, :]
                    act.wait_ge(s_pg, b * NG + i + 1)
                    if kind == "T":
                        act.activation(hT[:, 0, :, at * P:(at + 1) * P],
                                       bank.rearrange("p (c n) -> p c n", c=DC), ACT.Copy).then_inc(s_ga, 1)
                    elif kind == "K":
                        m, n = at
                        a, ln = KCH[n]
                        dst = k_flat[:, 0, a:a + ln] if L.stacked else k_tile[0:HD, 0, m, a:a + ln]
                        act.activation(dst, bank[0:L.MQ, 0:ln], ACT.Copy, scale=1.0 / L.sk).then_inc(s_ga, 1)
                    elif kind == "Q":
                        act.activation(q_dst(0, at), bank[0:L.MQ, :].rearrange("p (h q) -> p h q", q=QL),
                                       ACT.Copy, scale=1.0 / L.sq).then_inc(s_ga, 1)
                    elif kind == "V":
                        n = L.rows(at)
                        dst = v_all[0:n, at, :, 0:HD] if L.stacked else v_all[0:n, 0, at, :, 0:HD]
                        act.activation(dst, bank[0:n, 0:L.KV].rearrange("p (g d) -> p g d", g=G),
                                       ACT.Copy, scale=1.0 / L.sv).then_inc(s_ga, 1)
                    elif kind == "A":
                        j, n = at
                        act.activation(aT[:, 0, 4 * n:4 * n + 4, j * P:(j + 1) * P],
                                       bank.rearrange("p (c n) -> p c n", c=4), ACT.Copy).then_inc(s_ga, 1)

                for i in range(len(first)):
                    if by_act[i]:
                        take(i)

                def place_shift(g):
                    act.wait_ge(s_sh, b * G + g + 1)
                    act.activation(q_tile[SHIFT:KR, 0, g, :], mx[SHIFT:KR, 0:2, :].rearrange("p a n -> p (a n)"),
                                   ACT.Copy).then_inc(s_shc, 1)

                def place_v(g, par):
                    act.activation(v_g[:, par, :, :], v_all[:, :, g, :], ACT.Copy).then_inc(s_vg, 1)

                def phase(g, par, more, start):
                    for t in range(T):
                        e = b * (G * T) + g * T + t
                        n = L.rows(t)
                        buf = (par + t) % 2
                        if not (start and t < 2):
                            act.wait_ge(s_pv, e - 1)
                        for h in range(2):
                            act.wait_ge(s_st, 2 * e + h + 1)
                            src = psum[0:n, score_bank(par, t, h), :]
                            cols = slice(h * BANK, (h + 1) * BANK)
                            if L.stacked:
                                act.activation(p_buf[0:n, buf, cols], src, ACT.Exp,
                                               scale=float(HD) ** -0.5).then_inc(s_exp, 1)
                            else:
                                if not (start and t == 0):
                                    act.wait_ge(s_plo, 2 * e + h - 1)
                                act.activation(p32[0:n, h, :], src, ACT.Exp, scale=float(HD) ** -0.5)
                                act.activation(p_buf[0:n, buf, 0, cols], src, ACT.Exp,
                                               scale=float(HD) ** -0.5).then_inc(s_exp, 1)
                        if more and t == 4 and L.stacked:
                            place_v(g + 1, 1 - par)
                        if more and t == T - 2:
                            place_shift(g + 1)

                place_shift(0)
                if L.stacked:
                    act.wait_ge(s_ga, b * NA + sum(by_act[:len(first)]))
                    place_v(0, 0)
                run_phases(act, phase)
                for i in range(len(first), NG):
                    if by_act[i]:
                        take(i)

        rms = lnw is not None
        STEPS = QT + 1 + (2 * QT + 1 if rms else 0) + G * 3

        @block.vector
        def _(dve):
            for i, (_, hi, lo, scale, m, width) in enumerate(items):
                dve.wait_ge(s_hi, i + 1)
                dve.scalar_tensor_tensor(shaped(lo, m), stage_of(i, m, width), scale, shaped(hi, m), ALU.mult,
                                         ALU.subtract).then_inc(s_ctx if is_ctx[i] else s_lo, 1)
            if rms:
                dve.wait_ge(s_lnw, 16)
            if x_in is not None:
                dve.wait_ge(s_x, 16)
            with dve.Fori(0, B) as b:
                step = [0]

                def after(ins):
                    step[0] += 1
                    ins.then_inc(s_step, 1)

                def settle():
                    dve.wait_ge(s_step, b * STEPS + step[0])

                for j in range(QT):
                    dve.bn_stats(stats[:, j, :], x_sb[:, b * QT + j, :])
                dve.drain()
                for j in range(QT):
                    after(dve.bn_aggr(mv[:, j, :], stats[:, j, :]))
                settle()
                dve.tensor_scalar(var[:, :], mv[:, :, 1], LN_EPS, None, ALU.add).then_inc(s_var, 1)
                nroot = 2 if rms else 1
                dve.wait_ge(s_std, b * nroot + 1)
                after(dve.reciprocal(rstd[:, :], std[:, :]))
                settle()
                for j in range(QT):
                    ins = dve.tensor_scalar(xn[:, j, :], x_sb[:, b * QT + j, :], mv[:, j, 0:1], rstd[:, j:j + 1],
                                            ALU.subtract, ALU.mult)
                    if rms:
                        after(ins)
                    else:
                        ins.then_inc(s_xn, 1)
                if rms:
                    settle()
                    for j in range(QT):
                        after(dve.tensor_tensor_reduce(p_buf[:, j, 0:D], xn[:, j, :], xn[:, j, :], 1.0, 0.0,
                                                       ALU.mult, ALU.add, std[:, j:j + 1]))
                    settle()
                    dve.tensor_scalar(var[:, :], std[:, :], 1.0 / D, 1e-5, ALU.mult, ALU.add).then_inc(s_var, 1)
                    dve.wait_ge(s_std, b * nroot + 2)
                    after(dve.reciprocal(rstd[:, :], std[:, :]))
                    settle()
                    for j in range(QT):
                        dve.scalar_tensor_tensor(xn[:, j, :], xn[:, j, :], rstd[:, j:j + 1], lnw[:, :],
                                                 ALU.mult, ALU.mult).then_inc(s_xn, 1)

                def take(i):
                    kind, at = groups[i]
                    bank = psum[:, i % NP, :]
                    if kind == "O":
                        dve.wait_ge(s_pg, b * NG + i + 1)
                        dve.scalar_tensor_tensor(x_sb[:, b * QT + at, :], bank, 1.0 / L.so,
                                                 x_sb[:, b * QT + at, :], ALU.mult, ALU.add).then_inc(s_gd, 1)
                        return
                    dve.wait_ge(s_ga, b * NA + sum(by_act[:i + 1]))
                    if kind == "T":
                        src, scale = bank.rearrange("p (c n) -> p c n", c=DC), 1.0
                        hi, lo = (hT[:, s, :, at * P:(at + 1) * P] for s in range(2))
                    elif kind == "K":
                        m, n = at
                        a, ln = KCH[n]
                        src, scale = bank[0:L.MQ, 0:ln], 1.0 / L.sk
                        if L.stacked:
                            hi, lo = (k_flat[:, s, a:a + ln] for s in range(2))
                        else:
                            hi, lo = (k_tile[0:HD, s, m, a:a + ln] for s in range(2))
                    elif kind == "Q":
                        src, scale = bank[0:L.MQ, :].rearrange("p (h q) -> p h q", q=QL), 1.0 / L.sq
                        hi, lo = q_dst(0, at), q_dst(1, at)
                    elif kind == "V":
                        n = L.rows(at)
                        src, scale = bank[0:n, 0:L.KV].rearrange("p (g d) -> p g d", g=G), 1.0 / L.sv
                        hi, lo = (v_all[0:n, s, at, :, 0:HD] for s in range(2))
                    else:
                        j, n = at
                        src, scale = bank.rearrange("p (c n) -> p c n", c=4), 1.0
                        hi, lo = (aT[:, s, 4 * n:4 * n + 4, j * P:(j + 1) * P] for s in range(2))
                    dve.scalar_tensor_tensor(lo, src, scale, hi, ALU.mult, ALU.subtract).then_inc(s_gd, 1)

                def maximum(g, k):
                    m, n = divmod(k, NC)
                    dve.wait_ge(s_mx, b * (G * JOBS) + g * JOBS + k + 1)
                    dve.tensor_reduce(mpart[:, m, n:n + 1], mx[:, k % NMX, 0:KCH[n][1]], AX,
                                      ALU.max).then_inc(s_red, 1)

                def shift(g, base, k):
                    dve.wait_ge(s_red, b * (G * JOBS) + g * JOBS + JOBS)
                    dve.tensor_reduce(negm[:, :], mpart[:, :, :], AX, ALU.max, negate=True).then_inc(s_step, 1)
                    dve.wait_ge(s_step, base + k + 1)
                    dve.tensor_scalar(mm[:, :, 0], negm[:, :], lift, None, ALU.add).then_inc(s_step, 1)
                    dve.wait_ge(s_step, base + k + 2)
                    dve.scalar_tensor_tensor(mm[:, :, 1], negm[:, :], lift, mm[:, :, 0], ALU.add,
                                             ALU.subtract).then_inc(s_m, 1)

                def norm(g, base, k):
                    dve.wait_ge(s_tr, b * G + g + 1)
                    if L.stacked:
                        o = mx[:, 0, 0:QT * P].rearrange("p (j r n) -> p j r n", j=QT, r=R)
                        r4 = rec[:, :].rearrange("p (j r o) -> p j r o", j=QT, o=1)
                        dve.reciprocal(r4, o[:, :, :, HD:HD + 1]).then_inc(s_step, 1)
                        dve.wait_ge(s_step, base + k + 1)
                        dst = attn[:, :, bass.ds(g * (R * HD), R * HD)].rearrange("p j (r d) -> p j r d", r=R)
                        dve.tensor_tensor(dst, o[:, :, :, 0:HD], r4.to_broadcast([P, QT, R, HD]),
                                          ALU.mult).then_inc(s_norm, 1)
                    else:
                        o = mx[:, 0:2, 0:4 * VW].rearrange("p a (m n) -> p a m n", m=4)
                        r4 = rec[:, :].rearrange("p (a m o) -> p a m o", a=2, o=1)
                        dve.reciprocal(r4, o[:, :, :, HD:HD + 1]).then_inc(s_step, 1)
                        dve.wait_ge(s_step, base + k + 1)
                        for a in range(2):
                            dst = attn_g[:, g, :, 2 * a * HD:(2 * a + 2) * HD].rearrange(
                                "p j (r d) -> p r j d", r=2)
                            src = o[:, a, :, 0:HD].rearrange("p (r j) d -> p r j d", r=2)
                            rb = rec[:, 4 * a:4 * a + 4].rearrange("p (r j o) -> p r j o", r=2, o=1)
                            dve.tensor_tensor(dst, src, rb.to_broadcast([P, 2, QT, HD]),
                                              ALU.mult).then_inc(s_norm, 1)

                def take_oT(g):
                    dve.wait_ge(s_pv, b * (G * T) + g * T + T)
                    if L.stacked:
                        dst, src = scratch[:, 0:QL], oT[:, 0, 0:QL]
                    else:
                        dst, src = scratch[0:VW, :], oT[0:VW, :, :].rearrange("p a n -> p (a n)")
                    dve.tensor_copy(dst, src).then_inc(s_otc, 1)

                for what, i in opening:
                    if what == "M":
                        maximum(0, i)
                    elif by_dve[i]:
                        take(i)
                before = b * STEPS + step[0]
                shift(0, before, 0)

                def phase(g, par, more, start):
                    here = before + 2 + g * 3 - (0 if start else 1)
                    k = 0
                    for t in range(T):
                        if not L.stacked:
                            n, buf = L.rows(t), (par + t) % 2
                            for h in range(2):
                                dve.wait_ge(s_exp, 2 * (b * (G * T) + g * T + t) + h + 1)
                                cols = slice(h * BANK, (h + 1) * BANK)
                                dve.tensor_tensor(p_buf[0:n, buf, 1, cols], p32[0:n, h, :],
                                                  p_buf[0:n, buf, 0, cols], ALU.subtract).then_inc(s_plo, 1)
                        if t == 0 and not start:
                            norm(g - 1, here, 0)
                            k = 1
                        if more:
                            for job in jobs_beside(t):
                                maximum(g + 1, job)
                            if t == SLOTS - 1:
                                shift(g + 1, here, k)
                    take_oT(g)

                run_phases(dve, phase)
                norm(G - 1, before + 2 + (G - 1) * 3, 0)
                for i in range(len(first), NG):
                    if by_dve[i]:
                        take(i)

        NORMS = 1 if L.stacked else 2

        @block.tensor
        def _(pe):
            PASSES = ((0, 0), (0, 1), (1, 0))
            pe.wait_ge(s_const, NCONST)
            with pe.Fori(0, B) as b:
                def product(i):
                    kind, at = groups[i]
                    bank = psum[:, i % NP, :]
                    if i >= NP:
                        if by_dve[i - NP]:
                            pe.wait_ge(s_gd, b * ND + sum(by_dve[:i - NP + 1]))
                        else:
                            pe.wait_ge(s_ga, b * NA + sum(by_act[:i - NP + 1]))
                    if i == 0:
                        pe.wait_ge(s_ctx, b * DC + DC)
                    if kind == "T":
                        pe.wait_ge(s_xn, b * QT + at + 1)
                        for c in range(DC):
                            ins = pe.transpose(bank[:, c * P:(c + 1) * P], xn[:, at, c * P:(c + 1) * P], id32[:, :])
                    elif kind in "KQV":
                        if groups[i - 1][0] == "T":
                            pe.wait_ge(s_lo, NW)
                            pe.wait_ge(s_gd, b * ND + sum(by_dve[:i]))
                        ops = [(c, wp, xp) for c in range(DC) for wp, xp in PASSES]
                        if kind == "K":
                            m, n = at
                            a, ln = KCH[n]
                            for o, (c, wp, xp) in enumerate(ops):
                                ins = pe.matmul(bank[0:L.MQ, 0:ln], wkT[:, wp, c, m * L.MQ:(m + 1) * L.MQ],
                                                hT[:, xp, c, L.K0 + a:L.K0 + a + ln],
                                                start=o == 0, stop=o == len(ops) - 1)
                        elif kind == "Q":
                            for u in range(qper):
                                m = at * qper + u
                                for o, (c, wp, xp) in enumerate(ops):
                                    ins = pe.matmul(bank[0:L.MQ, u * QL:(u + 1) * QL],
                                                    wqT[:, wp, c, m * L.MQ:(m + 1) * L.MQ],
                                                    hT[:, xp, c, 0:QL], start=o == 0, stop=o == len(ops) - 1)
                        else:
                            n = L.rows(at)
                            for o, (c, wp, xp) in enumerate(ops):
                                ins = pe.matmul(bank[0:n, 0:L.KV], hT[:, xp, c, L.K0 + at * P:L.K0 + at * P + n],
                                                wvT[:, wp, c, :], start=o == 0, stop=o == len(ops) - 1)
                    elif kind == "A":
                        j, n = at
                        for c in range(4):
                            ins = pe.transpose(bank[:, c * P:(c + 1) * P], attn_block(j, 4 * n + c), id32[:, :])
                    else:
                        if at == 0:
                            pe.wait_ge(s_gd, b * ND + sum(by_dve[:NG - QT]))
                        o = 0
                        for c in range(CO):
                            for wp, xp in PASSES:
                                ins = pe.matmul(bank, aT[:, xp, c, at * P:(at + 1) * P], woT[:, wp, c, :],
                                                start=o == 0, stop=o == 3 * CO - 1)
                                o += 1
                    ins.then_inc(s_pg, 1)

                def max_job(g, k, head):
                    m, n = divmod(k, NC)
                    a, ln = KCH[n]
                    if k >= NMX:
                        pe.wait_ge(s_red, b * (G * JOBS) + g * JOBS + k - NMX + 1)
                    elif head == 1 and k < 2:
                        pe.wait_ge(s_shc, b * G + g)
                    elif head >= 2 and k < 2:
                        pe.wait_ge(s_norm, (b * G + g - 1) * NORMS)
                    pe.matmul(mx[:, k % NMX, 0:ln], q_tile[0:SHIFT, 0, g, m * P:(m + 1) * P],
                              k_tile[0:SHIFT, 0, g, a:a + ln], start=True, stop=True).then_inc(s_mx, 1)

                def turn_shift(g):
                    pe.wait_ge(s_m, b * G + g + 1)
                    for m in range(R * QT):
                        ins = pe.matmul(mx[SHIFT:KR, m // 4, (m % 4) * P:(m % 4 + 1) * P], mm[:, m, :], id16[:, :],
                                        start=True, stop=True, tile_position=(0, SHIFT))
                    ins.then_inc(s_sh, 1)

                def score_T(g, t, par, start):
                    e = b * (G * T) + g * T + t
                    n = L.rows(t)
                    if t == 0:
                        pe.wait_ge(s_shc, b * G + g + 1)
                    passes = ((0, 0),) if L.stacked else PASSES
                    for h in range(2):
                        if not (start and 2 * t + h < NST):
                            pe.wait_ge(s_exp, 2 * e + h + 1 - NST)
                        for o, (kp, qp) in enumerate(passes):
                            kr = KR if o == 0 else HD
                            ins = pe.matmul(psum[0:n, score_bank(par, t, h), :], k_tile[0:kr, kp, g, t * P:t * P + n],
                                            q_tile[0:kr, qp, g, h * BANK:(h + 1) * BANK],
                                            start=o == 0, stop=o == len(passes) - 1)
                        ins.then_inc(s_st, 1)

                def p_v(g, t, par):
                    e = b * (G * T) + g * T + t
                    n = L.rows(t)
                    buf = (par + t) % 2
                    if L.stacked:
                        pe.wait_ge(s_exp, 2 * e + 2)
                        if t == 0:
                            pe.wait_ge(s_vg, b * G + g + 1)
                        for r in range(R):
                            ins = pe.matmul(oT[32 * r:32 * r + VW, 0, 0:QL], v_g[0:n, par, t, :],
                                            p_buf[0:n, buf, r * QL:(r + 1) * QL], start=t == 0, stop=t == T - 1,
                                            tile_position=(0, 32 * r))
                    else:
                        pe.wait_ge(s_plo, 2 * e + 2)
                        for o, (vp, pp) in enumerate(((1, 0), (0, 0), (0, 1))):
                            for h in range(2):
                                ins = pe.matmul(oT[0:VW, h, :], v_all[0:n, vp, t, g, :],
                                                p_buf[0:n, buf, pp, h * BANK:(h + 1) * BANK],
                                                start=t == 0 and o == 0, stop=t == T - 1 and o == 2)
                    ins.then_inc(s_pv, 1)

                def turn_o(g):
                    pe.wait_ge(s_otc, b * G + g + 1)
                    if L.stacked:
                        for j in range(QT):
                            ins = pe.transpose(mx[:, 0, j * P:(j + 1) * P], scratch[:, j * P:(j + 1) * P],
                                               id32[:, :])
                    else:
                        for m in range(R * QT):
                            ins = pe.transpose(mx[:, m // 4, (m % 4) * VW:(m % 4 + 1) * VW],
                                               scratch[0:VW, m * P:(m + 1) * P], id32[0:VW, 0:VW])
                    ins.then_inc(s_tr, 1)

                for what, i in opening:
                    if what == "P":
                        product(i)
                        continue
                    if i == 0:
                        pe.wait_ge(s_gd, b * ND + sum(by_dve[:NKQP]))
                        if L.stacked:
                            pe.wait_ge(s_kq, (b + 1) * NKQ)
                    max_job(0, i, 0)
                turn_shift(0)
                pe.wait_ge(s_ga, b * NA + sum(by_act[:len(first)]))
                pe.wait_ge(s_gd, b * ND + sum(by_dve[:len(first)]))
                score_T(0, 0, 0, True)

                def phase(g, par, more, start):
                    for t in range(T):
                        if t + 1 < T:
                            score_T(g, t + 1, par, start)
                        elif more:
                            score_T(g + 1, 0, 1 - par, False)
                        if t == 0 and not start:
                            turn_o(g - 1)
                        if more:
                            for k in jobs_beside(t):
                                max_job(g + 1, k, 1 if start else 2)
                            if t == SLOTS:
                                turn_shift(g + 1)
                        p_v(g, t, par)

                run_phases(pe, phase)
                turn_o(G - 1)
                pe.wait_ge(s_norm, (b + 1) * G * NORMS)
                for i in range(len(first), NG):
                    product(i)
                pe.wait_ge(s_gd, (b + 1) * ND)


def routed_ffn(nc, x_sb, ident32, wA, wB, wR, keysT, tag):
    E, RANK, RD, SCALING = 64, 8, 16, 2.0
    NB = E * RANK
    SW = 64.0
    NEG = -3.0e38
    ctx = ExitStack()
    sb = lambda name, shape, dt: ctx.enter_context(nc.sbuf_tensor(f"{tag}_{name}", shape, dt))
    sem = lambda name: ctx.enter_context(nc.semaphore(f"{tag}_{name}"))
    with ctx:
        wa32 = sb("wa32", [P, DC, NB], F32)
        wb32 = sb("wb32", [P, NB // P, D], F32)
        wr32 = sb("wr32", [P, DC, RD], F32)
        keys = sb("keys", [RD, E], F32)
        wa = sb("wa", [P, 2, DC, NB], F16)
        wb = sb("wb", [P, 2, NB // P, D], F16)
        wr = sb("wr", [P, 2, DC, RD], F16)
        xn = sb("xn", [P, D], F32)
        xT = sb("xT", [P, 2, DC, P], F16)
        zT = sb("zT", [P, 2, NB // P, P], F16)
        zg = sb("zg", [P, E, RANK], F32)
        qT = sb("qT", [RD, P], F32)
        sc = sb("sc", [P, E], F32)
        w1 = sb("w1", [P, E], F32)
        w2 = sb("w2", [P, E], F32)
        mask = sb("mask", [P, E], F32)
        ex = sb("ex", [P, E], F32)
        gm = sb("gm", [P, E], F32)
        gate = sb("gate", [P, E], F32)
        top = sb("top", [P, 2, 8], F32)
        stats = sb("stats", [P, 6], F32)
        mv = sb("mv", [P, 2], F32)
        small = sb("small", [P, 8], F32)
        psum = ctx.enter_context(nc.psum_tensor(f"{tag}_ps", [P, 6, BANK], F32))
        p_xT, p_q, p_s, p_z, p_zT, p_y = (psum[:, i, :] for i in range(6))

        s_in, s_hi, s_lo = sem("in"), sem("hi"), sem("lo")
        s_var, s_std, s_xn = sem("var"), sem("std"), sem("xn")
        s_xT, s_xhi, s_xlo = sem("xT"), sem("xhi"), sem("xlo")
        s_q, s_qc, s_s, s_z = sem("q"), sem("qc"), sem("s"), sem("z")
        s_nmax, s_ex, s_zg = sem("nmax"), sem("ex"), sem("zg")
        s_zT, s_zhi, s_zlo, s_y, s_x = sem("zT"), sem("zhi"), sem("zlo"), sem("y"), sem("x")
        s_step = sem("dve_step")
        block = ctx.enter_context(nc.Block())
        pairs = ((wa32, wa), (wb32, wb), (wr32, wr))

        @block.sync
        def _(sp):
            for dst, src in ((wa32, wA), (wb32, wB), (wr32, wR)):
                sp.dma_start(dst[:, :, :], src.rearrange("(c p) n -> p c n", p=P)).then_inc(s_in, 16)
            sp.dma_start(keys[:, :], keysT).then_inc(s_in, 16)

        @block.scalar
        def _(act):
            act.wait_ge(s_in, 64)
            for src, dst in pairs:
                act.activation(dst[:, 0, :, :], src[:, :, :], ACT.Copy, scale=SW).then_inc(s_hi, 1)
            with act.Fori(0, TT) as i:
                act.wait_ge(s_var, i + 1)
                act.activation(small[:, 1:2], small[:, 0:1], ACT.Sqrt).then_inc(s_std, 1)
                act.wait_ge(s_xT, i + 1)
                act.activation(xT[:, 0, :, :], p_xT.rearrange("p (c n) -> p c n", c=DC), ACT.Copy).then_inc(s_xhi, 1)
                act.wait_ge(s_q, i + 1)
                act.activation(qT[:, :], p_q[0:RD, 0:P], ACT.Copy, scale=1.0 / SW).then_inc(s_qc, 1)
                act.wait_ge(s_nmax, i + 1)
                act.activation(ex[:, :], sc[:, :], ACT.Exp, bias=small[:, 3:4]).then_inc(s_ex, 1)
                act.wait_ge(s_zT, i + 1)
                act.activation(zT[:, 0, :, :], p_zT.rearrange("p (c n) -> p c n", c=NB // P),
                               ACT.Copy).then_inc(s_zhi, 1)

        STEPS = 7

        @block.vector
        def _(dve):
            for n, (src, dst) in enumerate(pairs):
                dve.wait_ge(s_hi, n + 1)
                dve.scalar_tensor_tensor(dst[:, 1, :, :], src[:, :, :], SW, dst[:, 0, :, :], ALU.mult,
                                         ALU.subtract).then_inc(s_lo, 1)
            with dve.Fori(0, TT) as i:
                count = [0]

                def step(ins):
                    count[0] += 1
                    ins.then_inc(s_step, 1)
                    dve.wait_ge(s_step, i * STEPS + count[0])

                dve.bn_stats(stats[:, :], x_sb[:, i, :])
                dve.drain()
                step(dve.bn_aggr(mv[:, :], stats[:, :]))
                dve.tensor_scalar(small[:, 0:1], mv[:, 1:2], LN_EPS, None, ALU.add).then_inc(s_var, 1)
                dve.wait_ge(s_std, i + 1)
                step(dve.reciprocal(small[:, 2:3], small[:, 1:2]))
                dve.tensor_scalar(xn[:, :], x_sb[:, i, :], mv[:, 0:1], small[:, 2:3], ALU.subtract,
                                  ALU.mult).then_inc(s_xn, 1)
                dve.wait_ge(s_xhi, i + 1)
                dve.tensor_tensor(xT[:, 1, :, :], p_xT.rearrange("p (c n) -> p c n", c=DC), xT[:, 0, :, :],
                                  ALU.subtract).then_inc(s_xlo, 1)
                dve.wait_ge(s_s, i + 1)
                dve.tensor_copy(sc[:, :], p_s[:, 0:E])
                dve.drain()
                step(dve.max(top[:, 0, :], sc[:, :]))
                dve.tensor_scalar(small[:, 3:4], top[:, 0, 0:1], -1.0, None, ALU.mult).then_inc(s_nmax, 1)
                dve.match_replace(w1[:, :], top[:, 0, :], sc[:, :], NEG)
                dve.drain()
                dve.max(top[:, 1, :], w1[:, :])
                dve.drain()
                step(dve.match_replace(w2[:, :], top[:, 1, :], w1[:, :], NEG))
                step(dve.tensor_scalar(mask[:, :], w2[:, :], NEG, None, ALU.is_equal))
                dve.wait_ge(s_ex, i + 1)
                step(dve.tensor_tensor_reduce(gm[:, :], ex[:, :], mask[:, :], 1.0, 0.0, ALU.mult, ALU.add,
                                              small[:, 4:5]))
                step(dve.reciprocal(small[:, 5:6], small[:, 4:5]))
                dve.tensor_scalar(gate[:, :], gm[:, :], small[:, 5:6], SCALING / SW, ALU.mult,
                                  ALU.mult).then_inc(s_zg, 1)
                dve.wait_ge(s_zg, 2 * i + 1)
                dve.wait_ge(s_z, i + 1)
                dve.tensor_tensor(zg[:, :, :], p_z.rearrange("p (e r) -> p e r", r=RANK),
                                  gate[:, :].rearrange("p (e o) -> p e o", o=1).to_broadcast([P, E, RANK]),
                                  ALU.mult).then_inc(s_zg, 1)
                dve.wait_ge(s_zhi, i + 1)
                dve.tensor_tensor(zT[:, 1, :, :], p_zT.rearrange("p (c n) -> p c n", c=NB // P), zT[:, 0, :, :],
                                  ALU.subtract).then_inc(s_zlo, 1)
                dve.wait_ge(s_y, i + 1)
                dve.scalar_tensor_tensor(x_sb[:, i, :], p_y, 1.0 / SW, x_sb[:, i, :], ALU.mult,
                                         ALU.add).then_inc(s_x, 1)
                assert count[0] == STEPS

        @block.tensor
        def _(pe):
            pe.wait_ge(s_lo, len(pairs))
            with pe.Fori(0, TT) as i:
                ops = [(c, wp, xp) for c in range(DC) for wp, xp in ((0, 0), (0, 1), (1, 0))]
                pe.wait_ge(s_xn, i + 1)
                for c in range(DC):
                    ins = pe.transpose(p_xT[:, c * P:(c + 1) * P], xn[:, c * P:(c + 1) * P], ident32)
                ins.then_inc(s_xT, 1)
                pe.wait_ge(s_xlo, i + 1)
                for o, (c, wp, xp) in enumerate(ops):
                    ins = pe.matmul(p_q[0:RD, 0:P], wr[:, wp, c, :], xT[:, xp, c, :], start=o == 0,
                                    stop=o == len(ops) - 1)
                ins.then_inc(s_q, 1)
                for o, (c, wp, xp) in enumerate(ops):
                    ins = pe.matmul(p_z, xT[:, xp, c, :], wa[:, wp, c, :], start=o == 0, stop=o == len(ops) - 1)
                ins.then_inc(s_z, 1)
                pe.wait_ge(s_qc, i + 1)
                pe.matmul(p_s[:, 0:E], qT[:, :], keys[:, :], start=True, stop=True).then_inc(s_s, 1)
                pe.wait_ge(s_zg, 2 * i + 2)
                zf = zg[:, :, :].rearrange("p e r -> p (e r)")
                for c in range(NB // P):
                    ins = pe.transpose(p_zT[:, c * P:(c + 1) * P], zf[:, c * P:(c + 1) * P], ident32)
                ins.then_inc(s_zT, 1)
                pe.wait_ge(s_zlo, i + 1)
                for o, (c, wp, xp) in enumerate(ops):
                    ins = pe.matmul(p_y, zT[:, xp, c, :], wb[:, wp, c, :], start=o == 0, stop=o == len(ops) - 1)
                ins.then_inc(s_y, 1)


def int8_ffn(nc, x_sb, ident32, ident16, norm_w, Wg, Wu, Wd, out, tag):
    I = Wg.shape[0]
    IT = cdiv(I, P)
    ICH = chunks(I, BANK)
    QMAX, FLOOR, EPS = 127.0, 1e-8, 1e-6
    ROUND = 1.5 * 2.0 ** 23
    ctx = ExitStack()
    sb = lambda name, shape, dt: ctx.enter_context(nc.sbuf_tensor(f"{tag}_{name}", shape, dt))
    sem = lambda name: ctx.enter_context(nc.semaphore(f"{tag}_{name}"))
    with ctx:
        wgT = sb("wgT", [P, DC, I], F16)
        wuT = sb("wuT", [P, DC, I], F16)
        wdT = sb("wdT", [P, IT, D], F16)
        wsg = sb("wsg", [P, I], F32)
        wsu = sb("wsu", [P, I], F32)
        wsd = sb("wsd", [P, D], F32)
        items = []
        for W, dst, row, width in ((Wg, wgT, wsg, D), (Wu, wuT, wsu, D), (Wd, wdT, wsd, I)):
            for a, n in chunks(W.shape[0], P):
                items.append((W[a:a + n, :], dst, row, a, n, width))
        NI = len(items)
        raw = sb("raw", [P, 2, I], F32)
        work = sb("work", [P, I], F32)
        quant = sb("quant", [P, 2, I], F16)
        wsc = sb("wsc", [P, 4], F32)
        wcol = sb("wcol", [P, P], F32)
        ones = sb("ones", [P, P], F32)
        nw = sb("nw", [P, D], F32)
        xn = sb("xn", [P, D], F32)
        xr = sb("xr", [P, D], F32)
        xq = sb("xq", [P, D], F16)
        xqT = sb("xqT", [P, DC, P], F16)
        gl = sb("gl", [P, I], F32)
        ul = sb("ul", [P, I], F32)
        hq = sb("hq", [P, I], F16)
        hqT = sb("hqT", [P, IT, P], F16)
        res = sb("res", [P, D], F32)
        stats = sb("stats", [P, 6], F32)
        mv = sb("mv", [P, 2], F32)
        sm = sb("sm", [P, 12], F32)
        pbig = ctx.enter_context(nc.psum_tensor(f"{tag}_pb", [P, 6, BANK], F32))
        ptr = ctx.enter_context(nc.psum_tensor(f"{tag}_pt", [P, 1024], F16))
        py = ctx.enter_context(nc.psum_tensor(f"{tag}_py", [P, BANK], F32))

        s_raw = [sem("raw0"), sem("raw1")]
        s_nw, s_out = sem("nw"), sem("out")
        s_wq, s_wt, s_wc, s_wr, s_wb, s_step = sem("wq"), sem("wt"), sem("wc"), sem("wr"), sem("wb"), sem("step")
        s_ones = sem("ones")
        s_var, s_std, s_xq, s_xT, s_xTc = sem("var"), sem("std"), sem("xq"), sem("xT"), sem("xTc")
        s_gu, s_gl, s_sl, s_hq, s_hT, s_hTc, s_y, s_x = (sem(n) for n in ("gu", "gl", "sl", "hq", "hT", "hTc", "y", "x"))
        batches = []
        for n, it in enumerate(items):
            for a, m in chunks(cdiv(it[5], P), 8):
                batches.append((n, a, m))
        block = ctx.enter_context(nc.Block())

        @block.sync
        def _(sp):
            sp.dma_start(nw[:, :], norm_w.partition_broadcast(P)).then_inc(s_nw, 16)
            for n, (src, _, _, a, m, width) in enumerate(items):
                wait(sp, s_wq, n - 1)
                sp.dma_start(raw[0:m, n % 2, 0:width], src).then_inc(s_raw[n % 2], 16)
            with sp.Fori(0, TT) as i:
                sp.wait_ge(s_x, i + 1)
                sp.dma_start(out[bass.ds(i * P, P), :], x_sb[:, i, :]).then_inc(s_out, 16)
            sp.wait_ge(s_out, 16 * TT)

        @block.gpsimd
        def _(pool):
            pool.memset(ones[:, :], 1.0).then_inc(s_ones, 1)

        @block.scalar
        def _(act):
            for k, (n, a, m) in enumerate(batches):
                _, dst, _, col, rows, width = items[n]
                act.wait_ge(s_wt, k + 1)
                full = m if (a + m) * P <= width else m - 1
                src = ptr[:, 0:m * P].rearrange("p (c n) -> p c n", c=m)
                last = None
                if full:
                    last = act.activation(dst[:, a:a + full, col:col + rows], src[:, 0:full, 0:rows], ACT.Copy)
                if full < m:
                    if last is not None:
                        last.then_inc(s_wc, 1)
                    part = width - (a + full) * P
                    last = act.activation(dst[0:part, a + full, col:col + rows], src[0:part, full, 0:rows], ACT.Copy)
                last.then_inc(s_wc, 1)
            with act.Fori(0, TT) as i:
                for k in range(2):
                    act.wait_ge(s_var, 2 * i + k + 1)
                    act.activation(sm[:, 1:2], sm[:, 0:1], ACT.Sqrt).then_inc(s_std, 1)
                act.wait_ge(s_xT, i + 1)
                act.activation(xqT[:, :, :], ptr[:, 0:DC * P].rearrange("p (c n) -> p c n", c=DC),
                               ACT.Copy).then_inc(s_xTc, 1)
                act.wait_ge(s_gl, i + 1)
                act.activation(gl[:, :], gl[:, :], ACT.Silu, scale=sm[:, 4:5]).then_inc(s_sl, 1)
                for k, (a, m) in enumerate(chunks(IT, 8)):
                    act.wait_ge(s_hT, 2 * i + k + 1)
                    src = ptr[:, 0:m * P].rearrange("p (c n) -> p c n", c=m)
                    full = m if (a + m) * P <= I else m - 1
                    act.activation(hqT[:, a:a + full, :], src[:, 0:full, :], ACT.Copy).then_inc(s_hTc, 1)
                    if full < m:
                        part = I - (a + full) * P
                        act.activation(hqT[0:part, a + full, :], src[0:part, full, :], ACT.Copy).then_inc(s_hTc, 1)

        WSTEPS = 5
        XSTEPS = 19

        @block.vector
        def _(dve):
            def quantise(step, rows, width, src, scale, inverse, tmp, dst):
                step(dve.tensor_reduce(scale, src, AX, ALU.max, apply_absolute_value=True))
                step(dve.tensor_scalar(scale, scale, 1.0 / QMAX, FLOOR, ALU.mult, ALU.max))
                step(dve.reciprocal(inverse, scale))
                step(dve.tensor_scalar(tmp, src, inverse, QMAX, ALU.mult, ALU.min))
                step(dve.tensor_scalar(tmp, tmp, -QMAX, ROUND, ALU.max, ALU.add))
                return dve.tensor_scalar(dst, tmp, ROUND, None, ALU.subtract)

            dve.wait_ge(s_ones, 1)
            for n, (_, _, row, a, m, width) in enumerate(items):
                count = [0]

                def wstep(ins):
                    count[0] += 1
                    ins.then_inc(s_step, 1)
                    dve.wait_ge(s_step, n * WSTEPS + count[0])

                dve.wait_ge(s_raw[n % 2], 16 * (n // 2 + 1))
                if n >= 2:
                    dve.wait_ge(s_wt, sum(1 for t in batches if t[0] <= n - 2))
                quantise(wstep, m, width, raw[0:m, n % 2, 0:width], wsc[0:m, 0:1], wsc[0:m, 1:2],
                         work[0:m, 0:width], quant[0:m, n % 2, 0:width]).then_inc(s_wq, 1)
                wait(dve, s_wr, n)
                dve.tensor_scalar(wcol[0:m, :], ones[0:m, :], wsc[0:m, 0:1], None, ALU.mult).then_inc(s_wb, 1)
                dve.wait_ge(s_wr, n + 1)
                dve.tensor_copy(row[:, a:a + m], py[:, 0:m]).then_inc(s_wb, 1)
                assert count[0] == WSTEPS
            dve.wait_ge(s_wq, NI)
            dve.wait_ge(s_wb, 2 * NI)
            dve.wait_ge(s_nw, 16)
            with dve.Fori(0, TT) as i:
                count = [0]

                def step(ins):
                    count[0] += 1
                    ins.then_inc(s_step, 1)
                    dve.wait_ge(s_step, NI * WSTEPS + i * XSTEPS + count[0])

                dve.bn_stats(stats[:, :], x_sb[:, i, :])
                dve.drain()
                step(dve.bn_aggr(mv[:, :], stats[:, :]))
                dve.tensor_scalar(sm[:, 0:1], mv[:, 1:2], LN_EPS, None, ALU.add).then_inc(s_var, 1)
                dve.wait_ge(s_std, 2 * i + 1)
                step(dve.reciprocal(sm[:, 2:3], sm[:, 1:2]))
                step(dve.tensor_scalar(xn[:, :], x_sb[:, i, :], mv[:, 0:1], sm[:, 2:3], ALU.subtract, ALU.mult))
                step(dve.tensor_tensor_reduce(xr[:, :], xn[:, :], xn[:, :], 1.0, 0.0, ALU.mult, ALU.add, sm[:, 3:4]))
                dve.tensor_scalar(sm[:, 0:1], sm[:, 3:4], 1.0 / D, EPS, ALU.mult, ALU.add).then_inc(s_var, 1)
                dve.wait_ge(s_std, 2 * i + 2)
                step(dve.reciprocal(sm[:, 2:3], sm[:, 1:2]))
                step(dve.scalar_tensor_tensor(xr[:, :], xn[:, :], sm[:, 2:3], nw[:, :], ALU.mult, ALU.mult))
                quantise(step, P, D, xr[:, :], sm[:, 4:5], sm[:, 5:6], xn[:, :], xq[:, :]).then_inc(s_xq, 1)
                dve.wait_ge(s_gu, 2 * i + 1)
                dve.tensor_tensor(gl[:, :], pbig[:, 0:3, :].rearrange("p a n -> p (a n)")[:, 0:I], wsg[:, :],
                                  ALU.mult).then_inc(s_gl, 1)
                dve.wait_ge(s_gu, 2 * i + 2)
                step(dve.tensor_tensor(ul[:, :], pbig[:, 3:6, :].rearrange("p a n -> p (a n)")[:, 0:I], wsu[:, :],
                                       ALU.mult))
                dve.wait_ge(s_sl, i + 1)
                step(dve.scalar_tensor_tensor(ul[:, :], ul[:, :], sm[:, 4:5], gl[:, :], ALU.mult, ALU.mult))
                quantise(step, P, I, ul[:, :], sm[:, 6:7], sm[:, 7:8], work[:, :], hq[:, :]).then_inc(s_hq, 1)
                dve.wait_ge(s_y, i + 1)
                step(dve.scalar_tensor_tensor(res[:, :], py[:, :], sm[:, 6:7], wsd[:, :], ALU.mult, ALU.mult))
                dve.tensor_tensor(x_sb[:, i, :], res[:, :], x_sb[:, i, :], ALU.add).then_inc(s_x, 1)
                assert count[0] == XSTEPS, count[0]

        @block.tensor
        def _(pe):
            taken = 0
            k = 0
            for n, (_, dst, row, col, rows, width) in enumerate(items):
                pe.wait_ge(s_wq, n + 1)
                for a, m in chunks(cdiv(width, P), 8):
                    wait(pe, s_wc, taken)
                    for c in range(m):
                        w = min(P, width - (a + c) * P)
                        ins = pe.transpose(ptr[0:w, c * P:c * P + rows],
                                           quant[0:rows, n % 2, (a + c) * P:(a + c) * P + w], ident16[0:rows, 0:rows])
                    ins.then_inc(s_wt, 1)
                    full = m if (a + m) * P <= width else m - 1
                    taken += (1 if full else 0) + (1 if full < m else 0)
                    k += 1
                pe.wait_ge(s_wb, 2 * n + 1)
                pe.matmul(py[:, 0:rows], wcol[0:rows, :], ident32[0:rows, 0:rows], start=True,
                          stop=True).then_inc(s_wr, 1)
            pe.wait_ge(s_wc, taken)
            pe.wait_ge(s_wb, 2 * NI)
            with pe.Fori(0, TT) as i:
                pe.wait_ge(s_xq, i + 1)
                for c in range(DC):
                    ins = pe.transpose(ptr[:, c * P:(c + 1) * P], xq[:, c * P:(c + 1) * P], ident16)
                ins.then_inc(s_xT, 1)
                pe.wait_ge(s_xTc, i + 1)
                for half, w in enumerate((wgT, wuT)):
                    for n, (a, m) in enumerate(ICH):
                        for c in range(DC):
                            ins = pe.matmul(pbig[:, 3 * half + n, 0:m], xqT[:, c, :], w[:, c, a:a + m],
                                            start=c == 0, stop=c == DC - 1)
                    ins.then_inc(s_gu, 1)
                pe.wait_ge(s_hq, i + 1)
                for k, (a, m) in enumerate(chunks(IT, 8)):
                    if k == 1:
                        pe.wait_ge(s_hTc, 3 * i + 1)
                    for c in range(m):
                        w = min(P, I - (a + c) * P)
                        ins = pe.transpose(ptr[0:w, c * P:(c + 1) * P], hq[:, (a + c) * P:(a + c) * P + w], ident16)
                    ins.then_inc(s_hT, 1)
                pe.wait_ge(s_hTc, 3 * i + 3)
                for c in range(IT):
                    w = min(P, I - c * P)
                    ins = pe.matmul(py[:, :], hqT[0:w, c, :], wdT[0:w, c, :], start=c == 0, stop=c == IT - 1)
                ins.then_inc(s_y, 1)


def build(nc, a, out, upto=4, start=0):
    with ExitStack() as ctx:
        sb = lambda name, shape, dt: ctx.enter_context(nc.sbuf_tensor(name, shape, dt))
        x_sb = sb("x_sb", [P, TT, D], F32)
        id32 = sb("id32", [P, P], F32)
        id16 = sb("id16", [P, P], F16)
        L0 = Layer(32, 8, 16, False, 1, (16.0, 16.0, 64.0, 64.0))
        L1 = Layer(16, 4, 96, True, 3, (16.0, 16.0, 64.0, 64.0))
        def projections(L, tag, names, stack):
            tiles = [stack.enter_context(nc.sbuf_tensor(f"{tag}_{n}T", [P, 2, DC, w], F16))
                     for n, w in (("wq", L.DO), ("wk", L.KV), ("wv", L.KV))]
            loads = [split_items(a[n], t, s) for n, t, s in zip(names, tiles, (L.sq, L.sk, L.sv))]
            return tiles, loads
        with ExitStack() as inner:
            w1, loads1 = projections(L1, "a1", ("wq1", "wk1", "wv1"), inner)
            with ExitStack() as own:
                w0, loads0 = projections(L0, "a0", ("wq0", "wk0", "wv0"), own)
                if upto >= 1 > start:
                    attention(nc, L0, x_sb, id32, id16, a["ctxT"], w0, a["wo0"], a["ln_w"], "a0", x_in=a["x"],
                              own=loads0, later=[it for w in loads1 for it in w])
            ident32, ident16 = id32[:, :], id16[:, :]
            if upto >= 2 > start:
                routed_ffn(nc, x_sb, ident32, a["wA"], a["wB"], a["wR"], a["keysT"], "f0")
            if upto >= 3 > start:
                attention(nc, L1, x_sb, id32, id16, a["ctxT"], w1, a["wo1"], None, "a1",
                          x_in=a["x"] if start else None, own=loads1 if start else ())
        if upto >= 4 > start:
            int8_ffn(nc, x_sb, ident32, ident16, a["norm_w"], a["Wg"], a["Wu"], a["Wd"], out, "f1")
        else:
            s_dbg = ctx.enter_context(nc.semaphore("dbg"))
            with nc.Block() as block:
                @block.sync
                def _(sp):
                    sp.dma_start(out.rearrange("(t p) n -> p t n", p=P), x_sb[:, :, :]).then_inc(s_dbg, 16)
                    sp.wait_ge(s_dbg, 16)


def lay_out(x, ctx_4096, L0_xattn_wq, L0_xattn_wk, L0_xattn_wv, L0_xattn_wo, L0_xattn_ln_w, L0_ffn_A_w, L0_ffn_B_w,
            L0_ffn_Wq_w, L0_ffn_keys, L1_xattn_Wq, L1_xattn_Wk, L1_xattn_Wv, L1_xattn_Wo, L1_ffn_rmsnorm_weight,
            L1_ffn_Wg, L1_ffn_Wu, L1_ffn_Wd):
    n = np.asarray
    t = lambda w: np.ascontiguousarray(n(w).T)
    return {
        "x": n(x).reshape(TOK, D), "ctxT": np.ascontiguousarray(n(ctx_4096).transpose(0, 2, 1)),
        "wq0": t(L0_xattn_wq), "wk0": t(L0_xattn_wk), "wv0": t(L0_xattn_wv), "wo0": t(L0_xattn_wo),
        "ln_w": n(L0_xattn_ln_w), "wA": t(L0_ffn_A_w), "wB": t(L0_ffn_B_w), "wR": t(L0_ffn_Wq_w),
        "keysT": t(L0_ffn_keys), "wq1": t(L1_xattn_Wq), "wk1": t(L1_xattn_Wk), "wv1": t(L1_xattn_Wv),
        "wo1": t(L1_xattn_Wo), "norm_w": n(L1_ffn_rmsnorm_weight), "Wg": n(L1_ffn_Wg), "Wu": n(L1_ffn_Wu),
        "Wd": n(L1_ffn_Wd),
    }


def kernel(**inputs):
    import concourse.bacc as bacc
    from concourse.bass_utils import run_bass_kernel_spmd

    nc = bacc.Bacc("TRN2", target_bir_lowering=False, num_devices=1)
    arrays = lay_out(**inputs)
    aps = {k: nc.dram_tensor(f"in_{k}", v.shape, mybir.dt.from_np(v.dtype), kind="ExternalInput").ap()
           for k, v in arrays.items()}
    out = nc.dram_tensor("out", (TOK, D), F32, kind="ExternalOutput").ap()
    build(nc, aps, out)
    r = run_bass_kernel_spmd(nc, [{f"in_{k}": v for k, v in arrays.items()}], core_ids=[0])
    return r.results[0]["out"].reshape(B, QL, D)
```

```python
from contextlib import ExitStack

import numpy as np

import concourse.bass as bass
from concourse import mybir

F32 = mybir.dt.float32
F16 = mybir.dt.float16
ACT = mybir.ActivationFunctionType
ALU = mybir.AluOpType
AX = mybir.AxisListType.X

P = 128
B, QL, D = 4, 256, 512
CTX = 1601
DC = D // P
TOK = B * QL
TT = TOK // P
QT = QL // P
BANK = 512
S_KEY = QL + CTX
LN_EPS = 1e-5
RMS_EPS = 1e-5


def cdiv(a, b):
    return -(-a // b)


class Layer:

    def __init__(self, heads, kv, hd, latents_are_keys, parts, scales):
        self.H, self.G, self.HD = heads, kv, hd
        self.R = heads // kv
        self.K0 = 0 if latents_are_keys else QL
        self.NK = S_KEY - self.K0
        self.T = cdiv(self.NK, P)
        self.DO = heads * hd
        self.CO = self.DO // P
        self.KV = kv * hd
        self.parts = parts
        self.sq, self.sk, self.sv, self.so = scales
        self.stacked = parts == 1
        self.VW = 32 if self.stacked else hd + 1
        self.NQ = self.DO // P
        self.NKT = self.KV // P

    def rows(self, t):
        return min(P, self.NK - t * P)


def wait(eng, sem, value):
    if not (isinstance(value, int) and value <= 0):
        eng.wait_ge(sem, value)


def chunks(n, step):
    return [(a, min(step, n - a)) for a in range(0, n, step)]


def split_items(src, dst, scale):
    _, _, nchunk, width = dst.shape
    per = max(m for m in range(1, nchunk + 1) if nchunk % m == 0 and m * width <= CTX)
    return [(src.rearrange("(c p) n -> p c n", p=P)[:, c:c + per, :], dst[:, 0, c:c + per, :],
             dst[:, 1, c:c + per, :], scale, per, width) for c in range(0, nchunk, per)]


def attention(nc, L, x_sb, id32, id16, ctxT, wqkv, wo, ln_w, tag, x_in=None, own=(), later=(), hT=None):
    G, R, T, CO, VW, HD = L.G, L.R, L.T, L.CO, L.VW, L.HD
    KCH = chunks(L.NK, 4 * cdiv(L.NK, 4 * cdiv(L.NK, BANK)) if L.stacked else BANK)
    NC = len(KCH)
    JOBS = R * QT * NC
    SHIFT = 96
    KR = SHIFT + 2
    RQ = R * QL
    NP, NMX = 5, 3
    NST = 4 if L.stacked else 3
    BOOST = 0.0 if L.stacked else 1024.0
    lift = float(np.log(BOOST) * HD ** 0.5) if BOOST else 0.0

    qper = BANK // QL
    keys = [[("K", (m, n)) for m in range(L.NKT)] for n in range(NC)]
    tokens = [("T", j) for j in range(QT)]
    queries = [("Q", n) for n in range(L.NQ // qper)]
    if L.stacked:
        first = tokens + keys[0] + queries + sum(keys[1:], [])
    else:
        first = sum(keys[1:-1], []) + tokens + keys[-1] + keys[0] + queries
    NKQP = len(first)
    first += [("V", t) for t in range(T)]
    second = [("A", (j, n)) for n in range(CO // 4) for j in range(QT)] + [("O", j) for j in range(QT)]
    groups = first + second
    EARLY = 0 if L.stacked else 3
    by_act = [k in "TKQVA" for k, _ in groups]
    by_dve = [k in "TKQAO" or (k == "V" and not L.stacked) for k, _ in groups]
    NA, ND, NG = sum(by_act), sum(by_dve), len(groups)
    early = NKQP - 2 if L.stacked else NKQP + 2
    opening, done = [("P", i) for i in range(early)], 0
    for i in range(early, len(first)):
        opening.append(("P", i))
        upto = cdiv(JOBS * (i - early + 1), len(first) - early)
        opening += [("M", k) for k in range(done, upto)]
        done = upto

    def chunk_of(head, k):
        if L.stacked and head is None:
            return k % (R * QT), k // (R * QT)
        return divmod(k, NC)

    TS = 9 if L.stacked else 11
    AHEAD = JOBS * (T - TS) // T
    turns_taken = []

    def turn_of(kind, head, k, g):
        at = len(turns_taken)
        turns_taken.append((kind, head, k))
        last = None
        if at >= NMX:
            last = turns_taken[at - NMX]
            last = (last[0], last[1] - g, last[2])
        return kind, head - g, k, at % NMX, last

    FIRST = NMX
    opening_turns = [turn_of("M", 0, k, 0) for k in range(JOBS)]
    opening_turns += [turn_of("M", 1, k, 0) for k in range(FIRST)] + [turn_of("S", 0, k, 0) for k in range(2)]
    plan = []
    for g in range(G):
        tiles = []
        begun = AHEAD if g else FIRST
        for t in range(T):
            here = []
            if t < TS and g + 1 < G:
                part = JOBS - begun
                here += [turn_of("M", g + 1, begun + k, g) for k in range(part * t // TS, part * (t + 1) // TS)]
            if t == 1 and g:
                here += [turn_of("O", g - 1, k, g) for k in range(2)]
            if t == TS + 1 and g + 1 < G:
                here += [turn_of("S", g + 1, k, g) for k in range(2)]
            if t >= TS and g + 2 < G:
                here += [turn_of("M", g + 2, k, g) for k in range(AHEAD * (t - TS) // (T - TS),
                                                                  AHEAD * (t - TS + 1) // (T - TS))]
            tiles.append(here)
        plan.append(tiles)
    closing_turns = [turn_of("O", G - 1, k, G - 1) for k in range(2)]
    LOOP = (G - 4) // 2 if L.stacked else 0
    assert all(plan[1 + n] == plan[1 + n % 2] for n in range(2 * LOOP))

    def score_bank(par, t, h):
        return (2 * ((par + t) % 2) + h) if L.stacked else (2 * t + h) % 3

    ctx = ExitStack()
    sb = lambda name, shape, dt: ctx.enter_context(nc.sbuf_tensor(f"{tag}_{name}", shape, dt))
    sem = lambda name: ctx.enter_context(nc.semaphore(f"{tag}_{name}"))
    with ctx:
        wqT, wkT, wvT = wqkv
        woT = sb("woT", [P, 2, CO, D], F16)
        stage = sb("stage", [P, 2, CTX], F32)
        given = hT is not None
        if not given:
            hT = sb("hT", [P, 2, DC, S_KEY], F16)
        q_raw = sb("q", [P, G, (1 if L.stacked else 2) * RQ], F16)
        q_tile = q_raw[:, :, :].rearrange("p g (s n) -> p s g n", n=RQ)
        if L.stacked:
            k_tile = sb("k", [P, 1, G, L.NK], F16)
            k_flat = sb("k_flat", [P, 2, L.NK], F16)
            q_flat = sb("q_flat", [P, 2, L.NQ, QL], F16)
            v_all = sb("v", [P, T, G, VW], F32)
            v_g = sb("v_g", [P, 2, T, VW], F32)
            p_buf = sb("p", [P, 2, RQ], F32)
            attn = sb("attn", [P, QT, L.DO], F32)
            aT_raw = sb("aT", [P, 2 * CO * QL], F16)[:, :]
            attn_block = lambda j, c: attn[:, j, c * P:(c + 1) * P]
        else:
            k_raw = sb("k", [P, 2, G * L.NK], F16)
            k_tile = k_raw[:, :, :].rearrange("p s (g n) -> p s g n", g=G)
            v_all = sb("v", [P, 2, T, G, VW], F16)
            p32 = sb("p32", [P, 2, BANK], F32)
            p_buf = sb("p", [P, 2, 2, RQ], F16)
            attn_g = q_raw[:, :, :].bitcast(F32)[:, :, 0:QT * R * HD].rearrange("p g (j n) -> p g j n", j=QT)
            aT_raw = k_raw[:, 1, 0:2 * CO * QL]
            per_g = R * HD // P
            attn_block = lambda j, c: attn_g[:, c // per_g, j, (c % per_g) * P:(c % per_g + 1) * P]
        aT = aT_raw.rearrange("p (s c n) -> p s c n", s=2, c=CO)
        scratch = sb("scratch", [P, RQ], F32)
        xn = scratch[:, :].rearrange("p (j n) -> p j n", j=QT)
        lnw = sb("lnw", [P, D], F32) if ln_w is not None else None
        one = sb("one", [P, 1], F32)
        stats = sb("stats", [P, QT, 6], F32)
        mv = sb("mv", [P, QT, 2], F32)
        var = sb("var", [P, QT], F32)
        std = sb("std", [P, QT], F32)
        rstd = sb("rstd", [P, QT], F32)
        mpart = sb("mpart", [P, R * QT, NC], F32)
        negm = sb("negm", [P, R * QT], F32)
        mm = sb("mm", [P, R * QT, 2], F16)
        rec = sb("rec", [P, R * QT], F32)

        psum = ctx.enter_context(nc.psum_tensor(f"{tag}_ps", [P, 8, BANK], F32))
        oT = psum[:, 4:5, :] if L.stacked else psum[:, 3:5, :]
        mx = psum[:, NP:8, :]

        s_w = [sem(f"loaded{i}") for i in range(2)]
        s_x = [sem("x_first"), sem("x_rest")]
        s_lnw = sem("lnw_in")
        s_const = sem("const")
        s_hi = sem("hi")
        s_lo = sem("lo")
        s_wo = sem("wo_split")
        s_ctx = sem("context")
        s_pool = sem("pool_step")
        s_var = sem("var_ready")
        s_std = sem("std_ready")
        s_xn = sem("xn_ready")
        s_pg = sem("product")
        s_ga = sem("act_took")
        s_gd = sem("dve_took")
        s_kq = sem("kq_placed")
        s_kd, s_qd = sem("k_in_dram"), sem("q_in_dram")
        s_vg = sem("v_placed")
        s_mx = sem("mx")
        s_red = sem("red")
        s_m = sem("m_ready")
        s_sh = sem("shift_turned")
        s_shc = sem("shift_placed")
        s_st = sem("st")
        s_exp = sem("exp")
        s_plo = sem("p_lo")
        s_pv = sem("pv")
        s_half = sem("oT_half")
        s_otc = [sem(f"oT_taken{k}") for k in range(2)]
        s_tr = sem("o_turned")
        s_norm = sem("o_normed")
        s_step = sem("dve_step")

        items = [it for w in own for it in w]
        NW = len(items)
        ND0 = 0 if given else DC
        items += [(ctxT[0, c * P:(c + 1) * P, :], hT[:, 0, c, QL:S_KEY], hT[:, 1, c, QL:S_KEY], 1.0, 1, CTX)
                  for c in range(ND0)]
        wo_items = split_items(wo, woT, L.so)
        NWO = len(wo_items)
        NI = NW + ND0 + NWO
        assert NI % 2 == 0 and len(later) % 2 == 0

        def stage_of(i, m, width):
            return stage[:, i % 2, 0:m * width].rearrange("p (c n) -> p c n", c=m)

        def shaped(ap, m):
            return ap.rearrange("p (c n) -> p c n", c=1) if len(ap.shape) == 2 else ap

        NKQ = 16 * 3 * (1 + L.NQ) if L.stacked else 0
        last_of = {k: max(i for i, g in enumerate(groups) if g[0] == k) + 1 for k in "KQ"}
        if L.stacked:
            k_dram = nc.dram_tensor(f"{tag}_k_parts", (2, P, L.NK), F16, kind="Internal").ap()
            q_dram = nc.dram_tensor(f"{tag}_q_parts", (2, P, L.NQ * QL), F16, kind="Internal").ap()

        def pieces(kind, at, bank):
            if kind == "K":
                m, n = at
                cols = slice(KCH[n][0], KCH[n][0] + KCH[n][1])
                if L.stacked:
                    return [(bank[:, 0:KCH[n][1]], [k_flat[:, s, cols] for s in range(2)])]
                part = 32 * m
                return [(bank[0:HD, 0:KCH[n][1]], [k_tile[0:HD, s, m, cols] for s in range(2)]),
                        (bank[HD:P, 0:KCH[n][1]], [k_tile[part:part + P - HD, s, 3, cols] for s in range(2)])]
            if L.stacked:
                return [(bank.rearrange("p (h q) -> p h q", q=QL),
                         [q_flat[:, s, qper * at:qper * at + qper, :] for s in range(2)])]
            out = []
            for u in range(qper):
                g, m = divmod(qper * at + u, 3)
                part = 32 * m
                src = bank[:, u * QL:(u + 1) * QL]
                out += [(src[0:HD, :], [q_tile[0:HD, s, g, m * QL:(m + 1) * QL] for s in range(2)]),
                        (src[HD:P, :], [q_tile[part:part + P - HD, s, g, 3 * QL:4 * QL] for s in range(2)])]
            return out

        def run_phases(eng, phase):
            phase(0, 0, plan[0], True, True)
            if LOOP:
                with eng.Fori(0, LOOP) as i:
                    phase(2 * i + 1, 1, plan[1], True, False)
                    phase(2 * i + 2, 0, plan[2], True, False)
            for g in range(1 + 2 * LOOP, G):
                phase(g, g % 2, plan[g], g < G - 1, False)

        NID = 5 if x_in is not None else 0
        NVC = max(NID, 1) + 2
        NCONST = NVC + (3 if L.stacked else 1)
        block = ctx.enter_context(nc.Block())

        @block.sync
        def _(sp):
            def load_x(n):
                if x_in is not None:
                    t0, t1 = (QT, TT) if n else (0, QT)
                    sp.dma_start(x_sb[:, t0:t1, :],
                                 x_in[t0 * P:t1 * P, :].rearrange("(t p) n -> p t n", p=P)).then_inc(s_x[n], 16)

            load_x(0)
            for i, (src, _, _, _, m, width) in enumerate(items + wo_items):
                if i >= NW + ND0 + 2:
                    sp.wait_ge(s_wo, i - 1 - NW - ND0)
                elif i >= NW + 2:
                    sp.wait_ge(s_ctx, i - 1 - NW)
                elif i >= 2:
                    sp.wait_ge(s_lo, i - 1)
                sp.dma_start(stage_of(i, m, width), shaped(src, m)).then_inc(s_w[i % 2], 16)
                if i == 1 and lnw is not None:
                    sp.dma_start(lnw[:, :], ln_w.partition_broadcast(P)).then_inc(s_lnw, 16)
                if i == NW + ND0 - 1:
                    load_x(1)
            sp.wait_ge(s_wo, NWO)

            def place_kq(b, again):
                if again:
                    sp.wait_ge(s_kq, b * NKQ)
                sp.wait_ge(s_gd, b * ND + sum(by_dve[:last_of["Q"]]))
                for part in range(2):
                    sp.dma_start(q_dram[part], q_flat[:, part, :, :].rearrange("p m q -> p (m q)")).then_inc(s_qd, 16)
                if not again:
                    sp.wait_ge(s_const, NCONST)
                sp.wait_ge(s_qd, (b + 1) * 32)
                for s, part in enumerate((0, 1, 0)):
                    for m in range(L.NQ):
                        sp.dma_start(q_tile[s * HD:(s + 1) * HD, 0, :, m * QL:(m + 1) * QL],
                                     q_dram[part][:, m * QL:(m + 1) * QL].rearrange("(g d) q -> d g q", d=HD)
                                     ).then_inc(s_kq, 16)
                sp.wait_ge(s_gd, b * ND + sum(by_dve[:last_of["K"]]))
                for part in range(2):
                    sp.dma_start(k_dram[part], k_flat[:, part, :]).then_inc(s_kd, 16)
                sp.wait_ge(s_kd, (b + 1) * 32)
                for s, part in enumerate((0, 0, 1)):
                    sp.dma_start(k_tile[s * HD:(s + 1) * HD, 0, :, :],
                                 k_dram[part].rearrange("(g d) n -> d g n", d=HD)).then_inc(s_kq, 16)

            if L.stacked:
                place_kq(0, False)
            with sp.Fori(1, B) as b:
                for c in range(DC):
                    sp.wait_ge(s_ctx, b * DC + c - 1)
                    sp.dma_start(stage[:, c % 2, :], ctxT[b, c * P:(c + 1) * P, :]).then_inc(s_w[c % 2], 16)
                if L.stacked:
                    place_kq(b, True)
            for i, (src, _, _, _, m, width) in enumerate(later):
                sp.wait_ge(s_ctx, B * DC + i - 1)
                sp.dma_start(stage_of(i, m, width), src).then_inc(s_w[i % 2], 16)


        @block.gpsimd
        def _(pool):
            if given:
                pool.memset(rec[:, 0:1], 0.0).then_inc(s_ctx, DC)
            sets = [(one[:, :], 1.0)]
            if x_in is not None:
                sets += [(id32[:, :], 0.0), (id16[:, :], 0.0), (id32, None), (id16, None)]
            if L.stacked:
                sets += [(v_all[:, :, :, :], 0.0), (v_all[:, :, :, HD:HD + 1], 1.0), (k_tile[:, 0, :, :], 0.0),
                         (q_tile[:, 0, :, :], 0.0)]
            else:
                sets += [(v_all[:, 0, :, :, HD:HD + 1], 1.0), (v_all[:, 1, :, :, HD:HD + 1], 0.0)]
            sets.append((k_tile[SHIFT:KR, 0, :, :], 1.0))
            for n, (ap, value) in enumerate(sets):
                wait(pool, s_const, n)
                if value is None:
                    pool.affine_select(out=ap[:, :], in_=ap[:, :], compare_op=ALU.not_equal, fill=1.0, base=0,
                                       pattern=[[-1, P]], channel_multiplier=1).then_inc(s_const, 1)
                else:
                    pool.memset(ap, value).then_inc(s_const, 1)
            assert len(sets) == NCONST
            pool.wait_ge(s_const, NCONST)
            def split(i, item, before, done):
                _, hi, lo, scale, m, width = item
                pool.wait_ge(s_w[i % 2], 16 * (i // 2 + 1))
                pool.tensor_scalar(hi, stage_of(i, m, width), scale, 0.0, ALU.mult, ALU.add).then_inc(s_pool, 1)
                pool.wait_ge(s_pool, before + 1)
                pool.tensor_scalar(stage_of(i, m, width), stage_of(i, m, width), scale, 0.0, ALU.mult,
                                   ALU.add).then_inc(s_pool, 1)
                pool.wait_ge(s_pool, before + 2)
                pool.tensor_tensor(lo, stage_of(i, m, width), hi, ALU.subtract).then_inc(done, 1)

            for n, item in enumerate(wo_items):
                split(NW + ND0 + n, item, 2 * n, s_wo)
            with pool.Fori(1, B) as b:
                for c in range(DC):
                    pool.wait_ge(s_w[c % 2], 16 * (NI // 2 + c // 2 + 1) + (b - 1) * (16 * (DC // 2)))
                    pool.wait_ge(s_pg, (b - 1) * NG + len(first))
                    pool.tensor_tensor(hT[:, 0, c, QL:S_KEY], stage[:, c % 2, :],
                                       one[:, :].to_broadcast([P, CTX]), ALU.mult).then_inc(s_pool, 1)
                    pool.wait_ge(s_pool, 2 * NWO + (b - 1) * DC + c + 1)
                    pool.tensor_tensor(hT[:, 1, c, QL:S_KEY], stage[:, c % 2, :], hT[:, 0, c, QL:S_KEY],
                                       ALU.subtract).then_inc(s_ctx, 1)
            for n, item in enumerate(later):
                split(NI + (B - 1) * DC + n, item, 2 * NWO + (B - 1) * DC + 2 * n, s_ctx)

        @block.scalar
        def _(act):
            def root(count):
                act.wait_ge(s_var, count)
                act.activation(std[:, :], var[:, :], ACT.Sqrt).then_inc(s_std, 1)

            root(1)
            for i, (_, hi, _, scale, m, width) in enumerate(items):
                act.wait_ge(s_w[i % 2], 16 * (i // 2 + 1))
                act.activation(shaped(hi, m), stage_of(i, m, width), ACT.Copy, scale=scale).then_inc(s_hi, 1)
            with act.Fori(0, B) as b:
                def take(i):
                    kind, at = groups[i]
                    bank = psum[:, i % NP, :]
                    act.wait_ge(s_pg, b * NG + i + 1)
                    if kind == "T":
                        act.activation(hT[:, 0, :, at * P:(at + 1) * P],
                                       bank.rearrange("p (c n) -> p c n", c=DC), ACT.Copy).then_inc(s_ga, 1)
                    elif kind in "KQ":
                        for src, dst in pieces(kind, at, bank):
                            ins = act.activation(dst[0], src, ACT.Copy, scale=1.0 / (L.sk if kind == "K" else L.sq))
                        ins.then_inc(s_ga, 1)
                    elif kind == "V":
                        if at == 0:
                            act.wait_ge(s_const, NVC)
                        n = L.rows(at)
                        dst = v_all[0:n, at, :, 0:HD] if L.stacked else v_all[0:n, 0, at, :, 0:HD]
                        act.activation(dst, bank[0:n, 0:L.KV].rearrange("p (g d) -> p g d", g=G),
                                       ACT.Copy, scale=1.0 / L.sv).then_inc(s_ga, 1)
                    elif kind == "A":
                        j, n = at
                        act.activation(aT[:, 0, 4 * n:4 * n + 4, j * P:(j + 1) * P],
                                       bank.rearrange("p (c n) -> p c n", c=4), ACT.Copy).then_inc(s_ga, 1)

                for i in range(len(first)):
                    if by_act[i]:
                        take(i)

                def place_shift(turns, g):
                    for kind, dh, k, bank, _ in turns:
                        if kind == "S":
                            act.wait_ge(s_sh, 2 * (b * G + g + dh) + k + 1)
                            act.activation(q_tile[SHIFT:KR, 0, g + dh, k * BANK:(k + 1) * BANK],
                                           mx[SHIFT:KR, bank, :], ACT.Copy).then_inc(s_shc, 1)

                def place_v(g, par):
                    act.activation(v_g[:, par, :, :], v_all[:, :, g, :], ACT.Copy).then_inc(s_vg, 1)

                def phase(g, par, turns, more, start):
                    for t in range(T):
                        e = b * (G * T) + g * T + t
                        n = L.rows(t)
                        buf = (par + t) % 2
                        if not (start and t < 2):
                            act.wait_ge(s_pv, e - 1)
                        for h in range(2):
                            act.wait_ge(s_st, 2 * e + h + 1)
                            src = psum[0:n, score_bank(par, t, h), :]
                            cols = slice(h * BANK, (h + 1) * BANK)
                            if L.stacked:
                                act.activation(p_buf[0:n, buf, cols], src, ACT.Exp,
                                               scale=float(HD) ** -0.5).then_inc(s_exp, 1)
                            else:
                                if not (start and t == 0):
                                    act.wait_ge(s_plo, 2 * e + h - 1)
                                act.activation(p32[0:n, h, :], src, ACT.Exp, scale=float(HD) ** -0.5)
                                act.activation(p_buf[0:n, buf, 0, cols], src, ACT.Exp,
                                               scale=float(HD) ** -0.5).then_inc(s_exp, 1)
                        if more and t == 4 and L.stacked:
                            place_v(g + 1, 1 - par)
                        place_shift(turns[t], g)
                    if L.stacked:
                        act.wait_ge(s_pv, b * (G * T) + g * T + T)
                        dst, src = scratch[:, 0:QL], oT[:, 0, 0:QL]
                    else:
                        act.wait_ge(s_half, b * G + g + 1)
                        dst, src = scratch[0:VW, 0:BANK], oT[0:VW, 0, :]
                    act.activation(dst, src, ACT.Copy).then_inc(s_otc[0], 1)

                act.wait_ge(s_const, NCONST)
                place_shift(opening_turns, 0)
                if L.stacked:
                    act.wait_ge(s_ga, b * NA + sum(by_act[:len(first)]))
                    place_v(0, 0)
                run_phases(act, phase)
                for i in range(len(first), NG):
                    if by_act[i]:
                        take(i)
                root(b + 2)

        NSTEPS = QT + 1 + (QT if lnw is not None else 0)
        STEPS = NSTEPS + G * 4

        @block.vector
        def _(dve):
            step = [0]

            def after(ins):
                step[0] += 1
                ins.then_inc(s_step, 1)

            def settle(b):
                dve.wait_ge(s_step, b * STEPS + step[0])

            def variances(batch, b):
                for j in range(QT):
                    dve.bn_stats(stats[:, j, :], x_sb[:, batch * QT + j, :])
                dve.drain()
                for j in range(QT):
                    after(dve.bn_aggr(mv[:, j, :], stats[:, j, :]))
                settle(b)
                if lnw is None:
                    dve.tensor_scalar(var[:, :], mv[:, :, 1], LN_EPS, None, ALU.add).then_inc(s_var, 1)
                else:
                    dve.tensor_scalar(var[:, :], mv[:, :, 1], 1.0 + RMS_EPS, RMS_EPS * LN_EPS, ALU.mult,
                                      ALU.add).then_inc(s_var, 1)

            def normalise(batch, b, count):
                dve.wait_ge(s_std, count)
                after(dve.reciprocal(rstd[:, :], std[:, :]))
                settle(b)
                for j in range(QT):
                    ins = dve.tensor_scalar(xn[:, j, :], x_sb[:, batch * QT + j, :], mv[:, j, 0:1], rstd[:, j:j + 1],
                                            ALU.subtract, ALU.mult)
                    if lnw is None:
                        ins.then_inc(s_xn, 1)
                    else:
                        after(ins)
                if lnw is not None:
                    settle(b)
                    for j in range(QT):
                        dve.tensor_tensor(xn[:, j, :], xn[:, j, :], lnw[:, :], ALU.mult).then_inc(s_xn, 1)

            if x_in is not None:
                dve.wait_ge(s_x[0], 16)
            variances(0, 0)
            if lnw is not None:
                dve.wait_ge(s_lnw, 16)
            normalise(0, 0, 1)
            for i, (_, hi, lo, scale, m, width) in enumerate(items):
                dve.wait_ge(s_hi, i + 1)
                dve.scalar_tensor_tensor(shaped(lo, m), stage_of(i, m, width), scale, shaped(hi, m), ALU.mult,
                                         ALU.subtract).then_inc(s_lo if i < NW else s_ctx, 1)
            with dve.Fori(0, B) as b:
                step[0] = NSTEPS
                def take(i):
                    kind, at = groups[i]
                    bank = psum[:, i % NP, :]
                    if kind == "O":
                        dve.wait_ge(s_pg, b * NG + i + 1)
                        dve.scalar_tensor_tensor(x_sb[:, b * QT + at, :], bank, 1.0 / L.so,
                                                 x_sb[:, b * QT + at, :], ALU.mult, ALU.add).then_inc(s_gd, 1)
                        return
                    dve.wait_ge(s_ga, b * NA + sum(by_act[:i + 1]))
                    if kind == "T":
                        src, scale = bank.rearrange("p (c n) -> p c n", c=DC), 1.0
                        hi, lo = (hT[:, s, :, at * P:(at + 1) * P] for s in range(2))
                    elif kind in "KQ":
                        for src, (hi, lo) in pieces(kind, at, bank):
                            ins = dve.scalar_tensor_tensor(lo, src, 1.0 / (L.sk if kind == "K" else L.sq), hi,
                                                           ALU.mult, ALU.subtract)
                        ins.then_inc(s_gd, 1)
                        return
                    elif kind == "V":
                        n = L.rows(at)
                        src, scale = bank[0:n, 0:L.KV].rearrange("p (g d) -> p g d", g=G), 1.0 / L.sv
                        hi, lo = (v_all[0:n, s, at, :, 0:HD] for s in range(2))
                    else:
                        j, n = at
                        src, scale = bank.rearrange("p (c n) -> p c n", c=4), 1.0
                        hi, lo = (aT[:, s, 4 * n:4 * n + 4, j * P:(j + 1) * P] for s in range(2))
                    dve.scalar_tensor_tensor(lo, src, scale, hi, ALU.mult, ALU.subtract).then_inc(s_gd, 1)

                def maximum(g, k, bank, begun=True):
                    m, n = chunk_of(g if begun else None, k)
                    dve.wait_ge(s_mx, b * (G * JOBS) + g * JOBS + k + 1)
                    dve.tensor_reduce(mpart[:, m, n:n + 1], mx[:, bank, 0:KCH[n][1]], AX,
                                      ALU.max).then_inc(s_red, 1)

                def shift(g, base, k):
                    dve.wait_ge(s_red, b * (G * JOBS) + g * JOBS + JOBS)
                    dve.tensor_reduce(negm[:, :], mpart[:, :, :], AX, ALU.max, negate=True).then_inc(s_step, 1)
                    dve.wait_ge(s_step, base + k + 1)
                    dve.tensor_scalar(mm[:, :, 0], negm[:, :], lift, None, ALU.add).then_inc(s_step, 1)
                    dve.wait_ge(s_step, base + k + 2)
                    dve.scalar_tensor_tensor(mm[:, :, 1], negm[:, :], lift, mm[:, :, 0], ALU.add,
                                             ALU.subtract).then_inc(s_m, 1)

                def norm(turns, g, base):
                    o = []
                    if turns is closing_turns:
                        dve.wait_ge(s_norm, 2 * (b * G + g))
                    for kind, dh, k, bank, _ in turns:
                        if kind != "O":
                            continue
                        dve.wait_ge(s_tr, 2 * (b * G + g + dh) + k + 1)
                        width = P // R if L.stacked else VW
                        o.append(mx[:, bank, 0:4 * width].rearrange("p (m n) -> p m n", m=4))
                        dve.reciprocal(rec[:, 4 * k:4 * k + 4].rearrange("p (m o) -> p m o", o=1),
                                       o[k][:, :, HD:HD + 1]).then_inc(s_step, 1)
                        head = g + dh
                    dve.wait_ge(s_step, base + 2)
                    for k in range(2):
                        rk = rec[:, 4 * k:4 * k + 4]
                        if L.stacked:
                            dst = attn[:, k, bass.ds(head * (R * HD), R * HD)].rearrange("p (r d) -> p r d", r=R)
                            src = o[k][:, :, 0:HD]
                            by = rk.rearrange("p (m o) -> p m o", o=1).to_broadcast([P, R, HD])
                        else:
                            dst = attn_g[:, head, :, 2 * k * HD:(2 * k + 2) * HD].rearrange("p j (r d) -> p r j d", r=2)
                            src = o[k][:, :, 0:HD].rearrange("p (r j) d -> p r j d", r=2)
                            by = rk.rearrange("p (r j o) -> p r j o", r=2, o=1).to_broadcast([P, 2, QT, HD])
                        dve.tensor_tensor(dst, src, by, ALU.mult).then_inc(s_norm, 1)

                follows = (b + 1) & (B - 1)
                for what, i in opening:
                    if what == "P" and i == early:
                        if x_in is not None:
                            dve.wait_ge(s_x[1], 16)
                        variances(follows, b)
                    if what == "M":
                        maximum(0, i, opening_turns[i][3], False)
                    elif by_dve[i]:
                        take(i)
                before = b * STEPS + step[0]
                shift(0, before, 0)
                step[0] += 4 * G
                for kind, dh, k, bank, _ in opening_turns[JOBS:]:
                    if kind == "M":
                        maximum(dh, k, bank)

                def phase(g, par, turns, more, start):
                    here = before + 2 + g * 4 - (0 if start else 2)
                    for t in range(T):
                        if not L.stacked:
                            n, buf = L.rows(t), (par + t) % 2
                            for h in range(2):
                                dve.wait_ge(s_exp, 2 * (b * (G * T) + g * T + t) + h + 1)
                                cols = slice(h * BANK, (h + 1) * BANK)
                                dve.tensor_tensor(p_buf[0:n, buf, 1, cols], p32[0:n, h, :],
                                                  p_buf[0:n, buf, 0, cols], ALU.subtract).then_inc(s_plo, 1)
                        if more and t == TS:
                            shift(g + 1, here, 0 if start else 2)
                        for kind, dh, k, bank, _ in turns[t]:
                            if kind == "M":
                                maximum(g + dh, k, bank)
                            elif kind == "O" and k == 0:
                                norm(turns[t], g, here)
                    if not L.stacked:
                        dve.wait_ge(s_pv, b * (G * T) + g * T + T)
                        dve.tensor_copy(scratch[0:VW, BANK:], oT[0:VW, 1, :]).then_inc(s_otc[1], 1)

                run_phases(dve, phase)
                for i in range(len(first), len(first) + EARLY):
                    take(i)
                norm(closing_turns, G - 1, before + 2 + (G - 1) * 4)
                for i in range(len(first) + EARLY, NG - QT):
                    take(i)
                normalise(follows, b, b + 2)
                for i in range(NG - QT, NG):
                    take(i)
                assert step[0] == NSTEPS + STEPS

        @block.tensor
        def _(pe):
            PASSES = ((0, 0), (0, 1), (1, 0))
            wait(pe, s_const, NID)
            with pe.Fori(0, B) as b:
                def product(i):
                    kind, at = groups[i]
                    bank = psum[:, i % NP, :]
                    if i >= NP:
                        if by_dve[i - NP]:
                            pe.wait_ge(s_gd, b * ND + sum(by_dve[:i - NP + 1]))
                        else:
                            pe.wait_ge(s_ga, b * NA + sum(by_act[:i - NP + 1]))
                    if kind == "K" and (i == 0 or groups[i - 1][0] != "K"):
                        pe.wait_ge(s_ctx, b * DC + DC)
                    if kind == "T":
                        pe.wait_ge(s_xn, b * QT + at + 1)
                        for c in range(DC):
                            ins = pe.transpose(bank[:, c * P:(c + 1) * P], xn[:, at, c * P:(c + 1) * P], id32[:, :])
                    elif kind in "KQV":
                        if (kind, at) == (("Q", 0) if L.stacked else ("K", (0, 0))):
                            wait(pe, s_lo, len(own[0]) if L.stacked else NW)
                            pe.wait_ge(s_gd, b * ND + sum(by_dve[:groups.index(("T", QT - 1)) + 1]))
                        ops = [(c, wp, xp) for c in range(DC) for wp, xp in PASSES]
                        if kind == "K":
                            m, n = at
                            a, ln = KCH[n]
                            for o, (c, wp, xp) in enumerate(ops):
                                ins = pe.matmul(bank[:, 0:ln], wkT[:, wp, c, m * P:(m + 1) * P],
                                                hT[:, xp, c, L.K0 + a:L.K0 + a + ln],
                                                start=o == 0, stop=o == len(ops) - 1)
                        elif kind == "Q":
                            for u in range(qper):
                                m = at * qper + u
                                for o, (c, wp, xp) in enumerate(ops):
                                    ins = pe.matmul(bank[:, u * QL:(u + 1) * QL],
                                                    wqT[:, wp, c, m * P:(m + 1) * P],
                                                    hT[:, xp, c, 0:QL], start=o == 0, stop=o == len(ops) - 1)
                        else:
                            n = L.rows(at)
                            for o, (c, wp, xp) in enumerate(ops):
                                ins = pe.matmul(bank[0:n, 0:L.KV], hT[:, xp, c, L.K0 + at * P:L.K0 + at * P + n],
                                                wvT[:, wp, c, :], start=o == 0, stop=o == len(ops) - 1)
                    elif kind == "A":
                        j, n = at
                        for c in range(4):
                            ins = pe.transpose(bank[:, c * P:(c + 1) * P], attn_block(j, 4 * n + c), id32[:, :])
                    else:
                        if at == 0:
                            pe.wait_ge(s_wo, NWO)
                            pe.wait_ge(s_gd, b * ND + sum(by_dve[:NG - QT]))
                        o = 0
                        for c in range(CO):
                            for wp, xp in PASSES:
                                ins = pe.matmul(bank, aT[:, xp, c, at * P:(at + 1) * P], woT[:, wp, c, :],
                                                start=o == 0, stop=o == 3 * CO - 1)
                                o += 1
                    ins.then_inc(s_pg, 1)

                def take_turn(turn, g, begun=True):
                    kind, dh, k, bank, last = turn
                    h = g + dh
                    if last is not None:
                        kind0, h0, k0 = last[0], g + last[1], last[2]
                        if kind0 == "M":
                            pe.wait_ge(s_red, b * (G * JOBS) + h0 * JOBS + k0 + 1)
                        elif kind0 == "S":
                            pe.wait_ge(s_shc, 2 * (b * G + h0) + k0 + 1)
                        else:
                            pe.wait_ge(s_norm, 2 * (b * G + h0) + k0 + 1)
                    if kind == "M":
                        m, n = chunk_of(h if begun else None, k)
                        a, ln = KCH[n]
                        if L.stacked and not begun:
                            qm, km = q_flat[0:HD, 0, m // QT, m % QT * P:(m % QT + 1) * P], k_flat[0:HD, 0, a:a + ln]
                        else:
                            qm, km = q_tile[0:SHIFT, 0, h, m * P:(m + 1) * P], k_tile[0:SHIFT, 0, h, a:a + ln]
                        pe.matmul(mx[:, bank, 0:ln], qm, km, start=True, stop=True).then_inc(s_mx, 1)
                    elif kind == "S":
                        if k == 0:
                            pe.wait_ge(s_m, b * G + h + 1)
                        for m in range(4):
                            ins = pe.matmul(mx[SHIFT:KR, bank, m * P:(m + 1) * P], mm[:, 4 * k + m, :], id16[:, :],
                                            start=True, stop=True, tile_position=(0, SHIFT))
                        ins.then_inc(s_sh, 1)
                    else:
                        if k == 0 or not L.stacked:
                            pe.wait_ge(s_otc[k], b * G + h + 1)
                        if L.stacked:
                            ins = pe.transpose(mx[:, bank, 0:P], scratch[:, k * P:(k + 1) * P], id32[:, :])
                        else:
                            for m in range(4):
                                ins = pe.transpose(mx[:, bank, m * VW:(m + 1) * VW],
                                                   scratch[0:VW, (4 * k + m) * P:(4 * k + m + 1) * P], id32[0:VW, 0:VW])
                        ins.then_inc(s_tr, 1)

                def score_T(g, t, par, start, between=(), head=0):
                    e = b * (G * T) + g * T + t
                    n = L.rows(t)
                    if t == 0:
                        pe.wait_ge(s_shc, 2 * (b * G + g + 1))
                    passes = ((0, 0),) if L.stacked else PASSES
                    for h in range(2):
                        for turn in between[h:h + 1]:
                            take_turn(turn, head)
                        if not (start and 2 * t + h < NST):
                            pe.wait_ge(s_exp, 2 * e + h + 1 - NST)
                        for o, (kp, qp) in enumerate(passes):
                            kr = KR if o == 0 else HD
                            ins = pe.matmul(psum[0:n, score_bank(par, t, h), :], k_tile[0:kr, kp, g, t * P:t * P + n],
                                            q_tile[0:kr, qp, g, h * BANK:(h + 1) * BANK],
                                            start=o == 0, stop=o == len(passes) - 1)
                        ins.then_inc(s_st, 1)

                def p_v(g, t, par, start):
                    e = b * (G * T) + g * T + t
                    n = L.rows(t)
                    buf = (par + t) % 2
                    if L.stacked:
                        if t == 0 and not start:
                            pe.wait_ge(s_otc[0], b * G + g)
                        pe.wait_ge(s_exp, 2 * e + 2)
                        if t == 0:
                            pe.wait_ge(s_vg, b * G + g + 1)
                        for r in range(R):
                            ins = pe.matmul(oT[32 * r:32 * r + VW, 0, 0:QL], v_g[0:n, par, t, :],
                                            p_buf[0:n, buf, r * QL:(r + 1) * QL], start=t == 0, stop=t == T - 1,
                                            tile_position=(0, 32 * r))
                    else:
                        pe.wait_ge(s_plo, 2 * e + 2)
                        for h in range(2):
                            if t == 0 and not start:
                                pe.wait_ge(s_otc[h], b * G + g)
                            if h == 1 and t == T - 1:
                                ins.then_inc(s_half, 1)
                            for o, (vp, pp) in enumerate(((1, 0), (0, 0), (0, 1))):
                                ins = pe.matmul(oT[0:VW, h, :], v_all[0:n, vp, t, g, :],
                                                p_buf[0:n, buf, pp, h * BANK:(h + 1) * BANK],
                                                start=t == 0 and o == 0, stop=t == T - 1 and o == 2)
                    ins.then_inc(s_pv, 1)

                for what, i in opening:
                    if what == "P":
                        product(i)
                        continue
                    if L.stacked:
                        if i % (R * QT) == 0:
                            n = max(groups.index(("K", (0, i // (R * QT)))) + 1, last_of["Q"])
                            pe.wait_ge(s_ga, b * NA + sum(by_act[:n]))
                    elif i == 0:
                        pe.wait_ge(s_const, NCONST)
                        pe.wait_ge(s_gd, b * ND + sum(by_dve[:NKQP]))
                    take_turn(opening_turns[i], 0, False)
                pe.wait_ge(s_const, NCONST)
                if L.stacked:
                    pe.wait_ge(s_kq, (b + 1) * NKQ)
                for turn in opening_turns[JOBS:]:
                    take_turn(turn, 0)
                pe.wait_ge(s_ga, b * NA + sum(by_act[:len(first)]))
                pe.wait_ge(s_gd, b * ND + sum(by_dve[:len(first)]))
                score_T(0, 0, 0, True)

                def phase(g, par, turns, more, start):
                    for t in range(T):
                        between = turns[t][:2] if all(turn[0] == "M" for turn in turns[t][:2]) else []
                        if t + 1 < T:
                            score_T(g, t + 1, par, start, between, g)
                        elif more:
                            score_T(g + 1, 0, 1 - par, False, between, g)
                        else:
                            between = []
                        for turn in turns[t][len(between):]:
                            take_turn(turn, g)
                        p_v(g, t, par, start)

                run_phases(pe, phase)
                if EARLY:
                    pe.wait_ge(s_norm, 2 * (b * G + G - 1))
                    assert all((len(first) + n) % NP < 3 for n in range(EARLY))
                for i in range(len(first), len(first) + EARLY):
                    product(i)
                for turn in closing_turns:
                    take_turn(turn, G - 1)
                pe.wait_ge(s_norm, 2 * (b + 1) * G)
                for i in range(len(first) + EARLY, NG):
                    product(i)
                pe.wait_ge(s_gd, (b + 1) * ND)


def routed_ffn(nc, x_sb, ident32, wA, wB, wR, keysT, context, hT, tag):
    E, RANK, RD, SCALING = 64, 8, 16, 2.0
    NB = E * RANK
    NBC = NB // P
    SW = 64.0
    NEG = -3.0e38
    ctx = ExitStack()
    sb = lambda name, shape, dt: ctx.enter_context(nc.sbuf_tensor(f"{tag}_{name}", shape, dt))
    sem = lambda name: ctx.enter_context(nc.semaphore(f"{tag}_{name}"))
    with ctx:
        wr32 = sb("wr32", [P, DC, RD], F32)
        wa32 = sb("wa32", [P, DC, NB], F32)
        wb32 = sb("wb32", [P, NBC, D], F32)
        keys = sb("keys", [RD, E], F32)
        wr = sb("wr", [P, 2, DC, RD], F16)
        wa = sb("wa", [P, 2, DC, NB], F16)
        wb = sb("wb", [P, 2, NBC, D], F16)
        xn = sb("xn", [P, TT, D], F32)
        xT = sb("xT", [P, 2, DC, TOK], F16)
        qT = sb("qT", [RD, TOK], F32)
        sc, w1, w2, diff, ex, mask, gm, gate = (sb(n, [P, TT, E], F32)
                                                for n in ("sc", "w1", "w2", "diff", "ex", "mask", "gm", "gate"))
        top = sb("top", [P, TT, 2, 8], F32)
        total, inv = sb("total", [P, TT], F32), sb("inv", [P, TT], F32)
        stats = sb("stats", [P, TT, 6], F32)
        mv = sb("mv", [P, TT, 2], F32)
        var, std, rstd = (sb(n, [P, TT], F32) for n in ("var", "std", "rstd"))
        zg = sb("zg", [P, E, RANK], F32)
        zT = sb("zT", [P, 2, NBC, P], F16)
        stage = sb("stage", [P, 2, CTX], F32)
        psum = ctx.enter_context(nc.psum_tensor(f"{tag}_ps", [P, 8, BANK], F32))
        NXB = 4
        QB, SB, ZB, ZTB, YB = 4, 6, 7, 0, 1
        blocks = lambda bank: psum[:, bank, :].rearrange("p (c n) -> p c n", n=P)

        s_in = [sem(f"in{n}") for n in range(4)]
        s_ctx = [sem(f"context_in{n}") for n in range(2)]
        s_chi, s_clo = sem("context_hi"), sem("context_lo")
        s_hi, s_lo = sem("hi"), sem("lo")
        s_var, s_std, s_xn, s_xT, s_xhi, s_xlo = (sem(n) for n in ("var", "std", "xn", "xT", "xhi", "xlo"))
        s_q, s_qc, s_s, s_diff, s_ex = (sem(n) for n in ("q", "qc", "s", "diff", "ex"))
        s_z, s_zg, s_zT, s_zhi, s_zlo, s_y, s_x = (sem(n) for n in ("z", "zg", "zT", "zhi", "zlo", "y", "x"))
        block = ctx.enter_context(nc.Block())
        pairs = ((wr32, wr), (wa32, wa), (wb32, wb))

        def over_tiles(eng, first, middle, last):
            first()
            with eng.Fori(1, TT - 1) as i:
                middle(i)
            last()

        @block.sync
        def _(sp):
            for n, (dst, src) in enumerate(((wr32, wR), (wa32, wA), (wb32, wB))):
                sp.dma_start(dst[:, :, :], src.rearrange("(c p) n -> p c n", p=P)).then_inc(s_in[n], 16)
            sp.dma_start(keys[:, :], keysT).then_inc(s_in[3], 16)
            for c in range(DC):
                wait(sp, s_clo, c - 1)
                sp.dma_start(stage[:, c % 2, :], context[c * P:(c + 1) * P, :]).then_inc(s_ctx[c % 2], 16)

        @block.gpsimd
        def _(pool):
            for c in range(DC):
                pool.wait_ge(s_ctx[c % 2], 16 * (c // 2 + 1))
                pool.tensor_scalar(hT[:, 0, c, QL:S_KEY], stage[:, c % 2, :], 1.0, 0.0, ALU.mult,
                                   ALU.add).then_inc(s_chi, 1)
                pool.wait_ge(s_chi, c + 1)
                pool.tensor_tensor(hT[:, 1, c, QL:S_KEY], stage[:, c % 2, :], hT[:, 0, c, QL:S_KEY],
                                   ALU.subtract).then_inc(s_clo, 1)

        @block.scalar
        def _(act):
            def high(n):
                act.wait_ge(s_in[n], 16)
                act.activation(pairs[n][1][:, 0, :, :], pairs[n][0][:, :, :], ACT.Copy, scale=SW).then_inc(s_hi, 1)

            act.wait_ge(s_var, 1)
            act.activation(std[:, :], var[:, :], ACT.Sqrt).then_inc(s_std, 1)
            high(0)
            for i in range(TT):
                act.wait_ge(s_xT, i + 1)
                act.activation(xT[:, 0, :, i * P:(i + 1) * P], blocks(i % NXB), ACT.Copy).then_inc(s_xhi, 1)
                if i == 3:
                    high(1)
            high(2)
            for n in range(TOK // BANK):
                act.wait_ge(s_q, n + 1)
                act.activation(qT[:, n * BANK:(n + 1) * BANK], psum[0:RD, QB + n, :], ACT.Copy,
                               scale=1.0 / SW).then_inc(s_qc, 1)
            act.wait_ge(s_diff, 1)
            act.activation(ex[:, :, :], diff[:, :, :], ACT.Exp).then_inc(s_ex, 1)

            def z_high(i):
                act.wait_ge(s_zT, i + 1)
                act.activation(zT[:, 0, :, :], blocks(ZTB), ACT.Copy).then_inc(s_zhi, 1)

            over_tiles(act, lambda: z_high(0), z_high, lambda: z_high(TT - 1))

        @block.vector
        def _(dve):
            def low(n):
                dve.wait_ge(s_hi, n + 1)
                dve.scalar_tensor_tensor(pairs[n][1][:, 1, :, :], pairs[n][0][:, :, :], SW, pairs[n][1][:, 0, :, :],
                                         ALU.mult, ALU.subtract).then_inc(s_lo, 1)

            for i in range(TT):
                dve.bn_stats(stats[:, i, :], x_sb[:, i, :])
            dve.drain()
            for i in range(TT):
                dve.bn_aggr(mv[:, i, :], stats[:, i, :])
            dve.drain()
            dve.tensor_scalar(var[:, :], mv[:, :, 1], LN_EPS, None, ALU.add).then_inc(s_var, 1)
            dve.wait_ge(s_std, 1)
            dve.reciprocal(rstd[:, :], std[:, :])
            dve.drain()
            for i in range(TT):
                dve.tensor_scalar(xn[:, i, :], x_sb[:, i, :], mv[:, i, 0:1], rstd[:, i:i + 1], ALU.subtract,
                                  ALU.mult).then_inc(s_xn, 1)
            low(0)
            for i in range(TT):
                dve.wait_ge(s_xhi, i + 1)
                dve.tensor_tensor(xT[:, 1, :, i * P:(i + 1) * P], blocks(i % NXB), xT[:, 0, :, i * P:(i + 1) * P],
                                  ALU.subtract).then_inc(s_xlo, 1)
            low(1)
            low(2)
            dve.wait_ge(s_s, 1)
            dve.tensor_copy(sc[:, :, :], psum[:, SB, :].rearrange("p (t e) -> p t e", t=TT))
            dve.drain()
            for i in range(TT):
                dve.max(top[:, i, 0, :], sc[:, i, :])
            dve.drain()
            dve.tensor_tensor(diff[:, :, :], sc[:, :, :], top[:, :, 0, 0:1].to_broadcast([P, TT, E]),
                              ALU.subtract).then_inc(s_diff, 1)
            for i in range(TT):
                dve.match_replace(w1[:, i, :], top[:, i, 0, :], sc[:, i, :], NEG)
            dve.drain()
            for i in range(TT):
                dve.max(top[:, i, 1, :], w1[:, i, :])
            dve.drain()
            for i in range(TT):
                dve.match_replace(w2[:, i, :], top[:, i, 1, :], w1[:, i, :], NEG)
            dve.drain()
            dve.tensor_scalar(mask[:, :, :], w2[:, :, :], NEG, None, ALU.is_equal)
            dve.wait_ge(s_ex, 1)
            dve.drain()
            dve.tensor_tensor(gm[:, :, :], ex[:, :, :], mask[:, :, :], ALU.mult)
            dve.drain()
            dve.tensor_reduce(total[:, :], gm[:, :, :], AX, ALU.add)
            dve.drain()
            dve.reciprocal(inv[:, :], total[:, :])
            dve.drain()
            dve.scalar_tensor_tensor(gate[:, :, :], gm[:, :, :], SCALING / SW,
                                     inv[:, :].rearrange("p (t o) -> p t o", o=1).to_broadcast([P, TT, E]), ALU.mult,
                                     ALU.mult)
            dve.drain()

            def gated(i):
                dve.wait_ge(s_z, i + 1)
                gi = gate[:, bass.ds(i, 1), :].rearrange("p t e -> p (t e)").rearrange("p (e o) -> p e o", o=1)
                dve.tensor_tensor(zg[:, :, :], psum[:, ZB, :].rearrange("p (e r) -> p e r", r=RANK),
                                  gi.to_broadcast([P, E, RANK]), ALU.mult).then_inc(s_zg, 1)

            def z_low(i):
                dve.wait_ge(s_zhi, i + 1)
                dve.tensor_tensor(zT[:, 1, :, :], blocks(ZTB), zT[:, 0, :, :], ALU.subtract).then_inc(s_zlo, 1)

            def result(i):
                dve.wait_ge(s_y, i + 1)
                dve.scalar_tensor_tensor(x_sb[:, i, :], psum[:, YB, :], 1.0 / SW, x_sb[:, i, :], ALU.mult,
                                         ALU.add).then_inc(s_x, 1)

            def first():
                gated(0)
                z_low(0)
                gated(1)

            def middle(i):
                result(i - 1)
                z_low(i)
                gated(i + 1)

            def last():
                result(TT - 2)
                z_low(TT - 1)
                result(TT - 1)

            over_tiles(dve, first, middle, last)

        @block.tensor
        def _(pe):
            ops = [(c, wp, xp) for c in range(DC) for wp, xp in ((0, 0), (0, 1), (1, 0))]
            for i in range(TT):
                pe.wait_ge(s_xn, i + 1)
                wait(pe, s_xlo, i - NXB + 1)
                for c in range(DC):
                    ins = pe.transpose(psum[:, i % NXB, c * P:(c + 1) * P], xn[:, i, c * P:(c + 1) * P], ident32)
                ins.then_inc(s_xT, 1)
            pe.wait_ge(s_lo, 1)
            for n in range(TOK // BANK):
                pe.wait_ge(s_xlo, (n + 1) * BANK // P)
                for o, (c, wp, xp) in enumerate(ops):
                    ins = pe.matmul(psum[0:RD, QB + n, :], wr[:, wp, c, :], xT[:, xp, c, n * BANK:(n + 1) * BANK],
                                    start=o == 0, stop=o == len(ops) - 1)
                ins.then_inc(s_q, 1)

            def z_of(i):
                for o, (c, wp, xp) in enumerate(ops):
                    ins = pe.matmul(psum[:, ZB, :], xT[:, xp, c, bass.ds(i * P, P)], wa[:, wp, c, :], start=o == 0,
                                    stop=o == len(ops) - 1)
                ins.then_inc(s_z, 1)

            pe.wait_ge(s_in[3], 16)
            for i in range(TT):
                if i * P % BANK == 0:
                    pe.wait_ge(s_qc, i * P // BANK + 1)
                ins = pe.matmul(psum[:, SB, i * E:(i + 1) * E], qT[:, i * P:(i + 1) * P], keys[:, :], start=True,
                                stop=True)
            ins.then_inc(s_s, 1)
            pe.wait_ge(s_lo, 2)
            z_of(0)
            pe.wait_ge(s_lo, 3)
            zf = zg[:, :, :].rearrange("p e r -> p (e r)")

            def turn(i):
                pe.wait_ge(s_zg, i + 1)
                for c in range(NBC):
                    ins = pe.transpose(psum[:, ZTB, c * P:(c + 1) * P], zf[:, c * P:(c + 1) * P], ident32)
                ins.then_inc(s_zT, 1)

            def result(i):
                pe.wait_ge(s_zlo, i + 1)
                for o, (c, wp, xp) in enumerate(ops):
                    ins = pe.matmul(psum[:, YB, :], zT[:, xp, c, :], wb[:, wp, c, :], start=o == 0,
                                    stop=o == len(ops) - 1)
                ins.then_inc(s_y, 1)

            def middle(i):
                turn(i)
                z_of(i + 1)
                result(i)

            def last():
                turn(TT - 1)
                result(TT - 1)

            over_tiles(pe, lambda: middle(0), middle, last)


def int8_ffn(nc, x_sb, ident32, ident16, norm_w, Wg, Wu, Wd, out, tag):
    I = Wg.shape[0]
    IT = cdiv(I, P)
    IP = IT * P
    ICH = chunks(I, BANK)
    HB = 8
    QMAX, FLOOR, EPS = 127.0, 1e-8, 1e-6
    ROUND = 1.5 * 2.0 ** 23
    ctx = ExitStack()
    sb = lambda name, shape, dt: ctx.enter_context(nc.sbuf_tensor(f"{tag}_{name}", shape, dt))
    sem = lambda name: ctx.enter_context(nc.semaphore(f"{tag}_{name}"))
    with ctx:
        wgT = sb("wgT", [P, DC, I], F16)
        wuT = sb("wuT", [P, DC, I], F16)
        wdT = sb("wdT", [P, IT, D], F16)
        wsg = sb("wsg", [P, I], F32)
        wsu = sb("wsu", [P, I], F32)
        wsd = sb("wsd", [P, D], F32)
        groups, items, at = [], [], 0
        for W, dst, row in ((Wg, wgT, wsg), (Wu, wuT, wsu), (Wd, wdT, wsd)):
            width = W.shape[1]
            per = HB // cdiv(width, P) or 1
            for a, n in chunks(W.shape[0] // P, per) + [(W.shape[0] // P, 0)]:
                rows, n = (P, n) if n else (W.shape[0] - a * P, 1)
                if rows:
                    groups.append(dict(src=W[a * P:a * P + n * rows, :], dst=dst, col=a * P, rows=rows, n=n,
                                       width=width, at=at, first=len(items)))
                    items += [(row, a * P + k * P, rows) for k in range(n)]
                    at += n * width
        NG, NI, RAW = len(groups), len(items), at
        turns = [(g, a, m) for g, G in enumerate(groups) for a, m in chunks(cdiv(G["width"], P), HB // G["n"])]
        last_turn = [max(k for k, t in enumerate(turns) if t[0] == g) for g in range(NG)]
        spans = []
        for n, (row, col, rows) in enumerate(items):
            if col % BANK == 0:
                spans.append([row, col, 0, []])
            spans[-1][2] += rows
            spans[-1][3].append(n)
        NS = len(spans)
        raw = sb("raw", [P, RAW], F32)
        quant = sb("quant", [P, 3, IP], F16)
        wmax = sb("wmax", [P, NI], F32)
        wscale = sb("wscale", [P, NI], F32)
        winv = sb("winv", [P, NI], F32)
        diag = sb("diag", [P, 4, P], F32)
        ones = sb("ones", [P, P], F32)
        nw = sb("nw", [P, D], F32)
        work = sb("work", [P, 6, I], F32)
        y = work[:, :, :].rearrange("p a n -> p (a n)")[:, 0:TT * D].rearrange("p (t n) -> p t n", t=TT)
        gate, up, hid = (work[:, 2 * n:2 * n + 2, :] for n in range(3))
        xq = sb("xq", [P, TT, D], F16)
        xqT = sb("xqT", [P, TT, DC, P], F16)
        hq = sb("hq", [P, 2, IP], F16)
        hqT = sb("hqT", [P, IT, P], F16)
        res = sb("res", [P, 2, D], F32)
        stats = sb("stats", [P, TT, 6], F32)
        mv = sb("mv", [P, TT, 2], F32)
        names = ("var", "std", "norm", "ymax", "yn", "xs", "xinv", "xratio", "xs127")
        var, std, norm, ymax, yn, xs, xinv, xratio, xs127 = (sb(n, [P, TT], F32) for n in names)
        hmax, hs, hinv, hratio = (sb(n, [P, TT], F32) for n in ("hmax", "hs", "hinv", "hratio"))
        psum = ctx.enter_context(nc.psum_tensor(f"{tag}_ps", [P, 8, BANK], F32))
        half = lambda bank: psum[:, bank, :].bitcast(F16)
        TURN, SCALE, XT, UP, HT, Y = 0, 4, 6, 3, 6, 7
        NTURN, NSCALE = 4, 2

        s_raw = [sem(f"raw{g}") for g in range(NG)]
        s_nw, s_out, s_ones = sem("nw"), sem("out"), sem("ones")
        s_step = sem("step")
        s_winv, s_wround, s_wq = sem("winv"), sem("wround"), sem("wq")
        s_turned, s_placed = sem("turned"), sem("placed")
        s_diag, s_scaled, s_placed_row = sem("diag"), sem("scaled"), sem("placed_row")
        s_var, s_std, s_xratio, s_xround, s_xq = (sem(n) for n in ("var", "std", "xratio", "xround", "xq"))
        s_xT, s_xTc = sem("xT"), sem("xTc")
        s_g, s_u, s_gate, s_up, s_silu, s_hid = (sem(n) for n in ("g", "u", "gate", "up", "silu", "hid"))
        s_hratio, s_hround, s_hq, s_hT, s_hTc = (sem(n) for n in ("hratio", "hround", "hq", "hT", "hTc"))
        s_y, s_res, s_x = sem("y"), sem("res"), sem("x")
        block = ctx.enter_context(nc.Block())
        XTN = HB // DC
        NXT = TT // XTN
        NMS = 6
        XROUND, XCLIP = 5, 7

        def raw_group(g):
            G = groups[g]
            return raw[0:G["rows"], G["at"]:G["at"] + G["n"] * G["width"]]

        def quant_group(g):
            G = groups[g]
            return quant[0:G["rows"], g % 3, 0:G["n"] * G["width"]]

        def column(t, k):
            return t[:, bass.ds(k, 1)]

        def in_pairs(eng, head, tile, tail):
            head()
            with eng.Fori(1, TT // 2) as j:
                for par in range(2):
                    tile(2 * j + par, par)
            tail()

        @block.sync
        def _(sp):
            sp.dma_start(nw[:, :], norm_w.partition_broadcast(P)).then_inc(s_nw, 16)
            for g, G in enumerate(groups):
                sp.dma_start(raw_group(g).rearrange("p (t n) -> p t n", t=G["n"]),
                             G["src"].rearrange("(t p) n -> p t n", t=G["n"])).then_inc(s_raw[g], 16)
            with sp.Fori(0, TT) as i:
                sp.wait_ge(s_x, i + 1)
                sp.dma_start(out[bass.ds(i * P, P), :], x_sb[:, i, :]).then_inc(s_out, 16)
            sp.wait_ge(s_out, 16 * TT)

        @block.gpsimd
        def _(pool):
            pool.memset(ones[:, :], 1.0).then_inc(s_ones, 1)
            for n in range(3):
                pool.memset(quant[:, n, I:IP], 0.0).then_inc(s_ones, 1)
            for n in range(2):
                pool.memset(hq[:, n, I:IP], 0.0).then_inc(s_ones, 1)
            pool.wait_ge(s_ones, NMS)
            for g, G in enumerate(groups):
                rows = G["rows"]
                pool.wait_ge(s_winv, g + 1)
                for n in range(G["first"], G["first"] + G["n"]):
                    wait(pool, s_scaled, n - 3)
                    pool.tensor_scalar(diag[0:rows, n % 4, 0:rows], ident32[0:rows, 0:rows],
                                       wscale[0:rows, n:n + 1], None, ALU.mult).then_inc(s_diag, 1)

            def multiply(i, par):
                pool.wait_ge(s_silu, i + 1)
                pool.wait_ge(s_up, i + 1)
                pool.tensor_tensor(hid[:, par, :], gate[:, par, :], up[:, par, :], ALU.mult).then_inc(s_hid, 1)

            def add(k, par):
                pool.wait_ge(s_res, k + 1)
                pool.tensor_tensor(x_sb[:, k, :], res[:, par, :], x_sb[:, k, :], ALU.add).then_inc(s_x, 1)

            def tile(i, par):
                pool.wait_ge(s_hq, i - 1)
                multiply(i, par)
                add(i - 2, par)

            in_pairs(pool, lambda: (multiply(0, 0), multiply(1, 1)), tile, lambda: (add(TT - 2, 0), add(TT - 1, 1)))

        @block.scalar
        def _(act):
            act.wait_ge(s_var, 1)
            act.activation(std[:, :], var[:, :], ACT.Sqrt).then_inc(s_std, 1)

            def place(k):
                g, a, m = turns[k]
                G = groups[g]
                cols = (G["n"] - 1) * P + G["rows"]
                act.wait_ge(s_turned, k + 1)
                act.activation(G["dst"][:, a:a + m, G["col"]:G["col"] + cols],
                               half(TURN + k % NTURN)[:, 0:m * G["n"] * P].rearrange("p (c n) -> p c n", c=m)[:, :, 0:cols],
                               ACT.Copy).then_inc(s_placed, 1)

            def place_row(s):
                row, col, n, _ = spans[s]
                act.wait_ge(s_scaled, spans[s][3][-1] + 1)
                act.activation(row[:, col:col + n], psum[:, SCALE + s % NSCALE, 0:n], ACT.Copy).then_inc(s_placed_row, 1)

            k = s = 0
            for g, G in enumerate(groups):
                act.wait_ge(s_winv, g + 1)
                for n in range(G["n"]):
                    part = raw[0:G["rows"], G["at"] + n * G["width"]:G["at"] + (n + 1) * G["width"]]
                    ins = act.activation(part, part, ACT.Copy, bias=ROUND,
                                         scale=winv[0:G["rows"], G["first"] + n:G["first"] + n + 1])
                ins.then_inc(s_wround, 1)
                while turns[k][0] < g-1:
                    place(k)
                    k += 1
                while spans[s][3][-1] < groups[g]["first"]:
                    place_row(s)
                    s += 1
                if g == XROUND:
                    act.wait_ge(s_xratio, 1)
                    for i in range(TT):
                        ins = act.activation(y[:, i, :], y[:, i, :], ACT.Copy, bias=ROUND, scale=xratio[:, i:i + 1])
                    ins.then_inc(s_xround, 1)
                if XCLIP + 1 < g <= XCLIP + 1 + NXT:
                    n = g - XCLIP - 2
                    act.wait_ge(s_xT, n + 1)
                    act.activation(xqT[:, n * XTN:(n + 1) * XTN, :, :],
                                   half(XT + n % 2)[:, :].rearrange("p (t c n) -> p t c n", t=XTN, c=DC),
                                   ACT.Copy).then_inc(s_xTc, 1)
            for k in range(k, len(turns)):
                place(k)
            for s in range(s, NS):
                place_row(s)

            def silu(i, par):
                act.wait_ge(s_gate, i + 1)
                act.activation(gate[:, par, :], gate[:, par, :], ACT.Silu, scale=column(xs, i)).then_inc(s_silu, 1)

            def rounding(k, par):
                act.wait_ge(s_hratio, k + 1)
                act.activation(hid[:, par, :], hid[:, par, :], ACT.Copy, bias=ROUND,
                               scale=column(hratio, k)).then_inc(s_hround, 1)

            def turned(k, n):
                a, m = chunks(IT, HB)[n]
                act.wait_ge(s_hT, 2 * k + n + 1)
                act.activation(hqT[:, a:a + m, :], half(HT)[:, 0:m * P].rearrange("p (c n) -> p c n", c=m),
                               ACT.Copy).then_inc(s_hTc, 1)

            def tile(i, par):
                turned(i - 2, 0)
                silu(i, par)
                turned(i - 2, 1)
                rounding(i - 1, 1 - par)

            def head():
                silu(0, 0)
                silu(1, 1)
                rounding(0, 0)

            def tail():
                turned(TT - 2, 0)
                turned(TT - 2, 1)
                rounding(TT - 1, 1)
                turned(TT - 1, 0)
                turned(TT - 1, 1)

            in_pairs(act, head, tile, tail)

        @block.vector
        def _(dve):
            steps = [0]

            def step(ins, base=0):
                steps[0] += 1
                ins.then_inc(s_step, 1)
                dve.wait_ge(s_step, base + steps[0])

            def weight_scale(g):
                G = groups[g]
                at = slice(G["first"], G["first"] + G["n"])
                dve.wait_ge(s_raw[g], 16)
                step(dve.tensor_reduce(wmax[0:G["rows"], at], raw_group(g).rearrange("p (t n) -> p t n", t=G["n"]),
                                       AX, ALU.max, apply_absolute_value=True))
                step(dve.tensor_scalar(wscale[0:G["rows"], at], wmax[0:G["rows"], at], 1.0 / QMAX, FLOOR, ALU.mult,
                                       ALU.max))
                dve.reciprocal(winv[0:G["rows"], at], wscale[0:G["rows"], at]).then_inc(s_winv, 1)

            def weight_clip(g):
                dve.wait_ge(s_wround, g + 1)
                if g >= 3:
                    dve.wait_ge(s_turned, last_turn[g - 3] + 1)
                step(dve.tensor_scalar(quant_group(g), raw_group(g), ROUND, QMAX, ALU.subtract, ALU.min))
                dve.tensor_scalar(quant_group(g), quant_group(g), -QMAX, None, ALU.max).then_inc(s_wq, 1)

            for i in range(TT):
                dve.bn_stats(stats[:, i, :], x_sb[:, i, :])
            dve.drain()
            for i in range(TT):
                dve.bn_aggr(mv[:, i, :], stats[:, i, :])
            dve.drain()
            dve.tensor_scalar(var[:, :], mv[:, :, 1], 1.0 + EPS, EPS * LN_EPS, ALU.mult, ALU.add).then_inc(s_var, 1)
            dve.wait_ge(s_std, 1)
            step(dve.reciprocal(norm[:, :], std[:, :]))
            dve.wait_ge(s_nw, 16)
            for g in range(NG):
                weight_scale(g)
                if g < TT // 2:
                    for i in (2 * g, 2 * g + 1):
                        step(dve.scalar_tensor_tensor(y[:, i, :], x_sb[:, i, :], mv[:, i, 0:1], nw[:, :],
                                                      ALU.subtract, ALU.mult))
                        step(dve.tensor_reduce(ymax[:, i:i + 1], y[:, i, :], AX, ALU.max,
                                               apply_absolute_value=True))
                if g == TT // 2:
                    step(dve.tensor_tensor(yn[:, :], ymax[:, :], norm[:, :], ALU.mult))
                    step(dve.tensor_scalar(xs[:, :], yn[:, :], 1.0 / QMAX, FLOOR, ALU.mult, ALU.max))
                    step(dve.reciprocal(xinv[:, :], xs[:, :]))
                    dve.tensor_tensor(xratio[:, :], xinv[:, :], norm[:, :], ALU.mult).then_inc(s_xratio, 1)
                    step(dve.tensor_scalar(xs127[:, :], xs[:, :], 1.0 / QMAX, None, ALU.mult))
                if g == XCLIP:
                    dve.wait_ge(s_xround, 1)
                    step(dve.tensor_scalar(xq[:, :, :], y, ROUND, QMAX, ALU.subtract, ALU.min))
                    dve.tensor_scalar(xq[:, :, :], xq[:, :, :], -QMAX, None, ALU.max).then_inc(s_xq, 1)
                if g > 0:
                    weight_clip(g - 1)
            weight_clip(NG - 1)
            dve.wait_ge(s_placed_row, NS)
            dve.wait_ge(s_placed, len(turns))
            DSTEPS = 4

            def gate_of(i, par):
                dve.wait_ge(s_g, i + 1)
                dve.tensor_tensor(gate[:, par, :], psum[:, 0:UP, :].rearrange("p a n -> p (a n)")[:, 0:I], wsg[:, :],
                                  ALU.mult).then_inc(s_gate, 1)

            def up_of(i, par):
                dve.wait_ge(s_u, i + 1)
                dve.tensor_tensor(up[:, par, :], psum[:, UP:UP + 3, :].rearrange("p a n -> p (a n)")[:, 0:I],
                                  wsu[:, :], ALU.mult).then_inc(s_up, 1)

            def scale_of(k, par, base=0):
                at = lambda t: column(t, k)
                dve.wait_ge(s_hid, k + 1)
                step(dve.tensor_reduce(at(hmax), hid[:, par, :], AX, ALU.max, apply_absolute_value=True), base)
                step(dve.tensor_scalar(at(hs), at(hmax), at(xs127), FLOOR, ALU.mult, ALU.max), base)
                step(dve.reciprocal(at(hinv), at(hs)), base)
                dve.tensor_scalar(at(hratio), at(hinv), at(xs), None, ALU.mult).then_inc(s_hratio, 1)

            def clip_of(k, par, base=0):
                dve.wait_ge(s_hround, k + 1)
                step(dve.tensor_scalar(hq[:, par, 0:I], hid[:, par, :], ROUND, QMAX, ALU.subtract, ALU.min), base)
                dve.tensor_scalar(hq[:, par, 0:I], hq[:, par, 0:I], -QMAX, None, ALU.max).then_inc(s_hq, 1)

            def result_of(k, par):
                dve.wait_ge(s_y, k + 1)
                dve.scalar_tensor_tensor(res[:, par, :], psum[:, Y, :], column(hs, k), wsd[:, :], ALU.mult,
                                         ALU.mult).then_inc(s_res, 1)

            def tile(i, par):
                before, steps[0] = steps[0], before_loop
                base = (i - 2) * DSTEPS
                dve.wait_ge(s_hid, i - 1)
                gate_of(i, par)
                scale_of(i - 1, 1 - par, base)
                up_of(i, par)
                clip_of(i - 1, 1 - par, base)
                result_of(i - 2, par)
                assert steps[0] == before_loop + DSTEPS
                steps[0] = before + DSTEPS * (TT - 2) // 2

            gate_of(0, 0)
            up_of(0, 0)
            gate_of(1, 1)
            scale_of(0, 0)
            up_of(1, 1)
            clip_of(0, 0)
            before_loop = steps[0]
            in_pairs(dve, lambda: None, tile, lambda: None)
            scale_of(TT - 1, 1)
            clip_of(TT - 1, 1)
            result_of(TT - 2, 0)
            dve.wait_ge(s_x, TT - 2)
            result_of(TT - 1, 1)

        @block.tensor
        def _(pe):
            pe.wait_ge(s_ones, NMS)
            k = 0
            for g, G in enumerate(groups):
                if XCLIP < g <= XCLIP + NXT:
                    n = g - XCLIP - 1
                    pe.wait_ge(s_xq, 1)
                    wait(pe, s_xTc, n - 1)
                    for t in range(XTN):
                        for c in range(DC):
                            at = (t * DC + c) * P
                            ins = pe.transpose(half(XT + n % 2)[:, at:at + P], xq[:, n * XTN + t, c * P:(c + 1) * P],
                                               ident16)
                    ins.then_inc(s_xT, 1)
                rows, wide = G["rows"], G["width"]
                pe.wait_ge(s_wq, g + 1)
                while k < len(turns) and turns[k][0] == g:
                    a, m = turns[k][1:]
                    wait(pe, s_placed, k - NTURN + 1)
                    for c in range(m):
                        for n in range(G["n"]):
                            at, src = (c * G["n"] + n) * P, n * wide + (a + c) * P
                            ins = pe.transpose(half(TURN + k % NTURN)[:, at:at + rows],
                                               quant[0:rows, g % 3, src:src + P], ident16[0:rows, 0:rows])
                    ins.then_inc(s_turned, 1)
                    k += 1
                for n in range(G["first"], G["first"] + G["n"]):
                    s = next(s for s in range(NS) if n in spans[s][3])
                    if n == spans[s][3][0]:
                        wait(pe, s_placed_row, s - NSCALE + 1)
                    at = items[n][1] - spans[s][1]
                    pe.wait_ge(s_diag, n + 1)
                    pe.matmul(psum[:, SCALE + s % NSCALE, at:at + rows], ones[0:rows, :], diag[0:rows, n % 4, 0:rows],
                              start=True, stop=True).then_inc(s_scaled, 1)
            pe.wait_ge(s_placed_row, NS)
            pe.wait_ge(s_placed, len(turns))
            pe.wait_ge(s_xTc, NXT)

            def product(i, weights, bank, done):
                for n, (a, m) in enumerate(ICH):
                    for c in range(DC):
                        ins = pe.matmul(psum[:, bank + n, 0:m], xqT[:, i, c, :], weights[:, c, a:a + m],
                                        start=c == 0, stop=c == DC - 1)
                ins.then_inc(done, 1)

            def turn(k, par, n):
                a, m = chunks(IT, HB)[n]
                if n == 0:
                    pe.wait_ge(s_hq, k + 1)
                else:
                    pe.wait_ge(s_hTc, 2 * k + 1)
                for c in range(m):
                    ins = pe.transpose(half(HT)[:, c * P:(c + 1) * P], hq[:, par, (a + c) * P:(a + c + 1) * P], ident16)
                ins.then_inc(s_hT, 1)

            def down(k):
                for c in range(IT):
                    if c % HB == 0:
                        pe.wait_ge(s_hTc, 2 * k + c // HB + 1)
                    ins = pe.matmul(psum[:, Y, :], hqT[:, c, :], wdT[:, c, :], start=c == 0, stop=c == IT - 1)
                ins.then_inc(s_y, 1)

            def tile(i, par):
                pe.wait_ge(s_gate, i)
                product(i, wgT, 0, s_g)
                turn(i - 2, par, 0)
                pe.wait_ge(s_up, i)
                product(i, wuT, UP, s_u)
                turn(i - 2, par, 1)
                pe.wait_ge(s_gate, i + 1)
                down(i - 2)

            def head():
                for i in range(2):
                    wait(pe, s_gate, i)
                    product(i, wgT, 0, s_g)
                    wait(pe, s_up, i)
                    product(i, wuT, UP, s_u)

            def tail():
                for k in (TT - 2, TT - 1):
                    turn(k, k % 2, 0)
                    turn(k, k % 2, 1)
                    pe.wait_ge(s_x, k)
                    down(k)

            in_pairs(pe, head, tile, tail)


def build(nc, a, out):
    with ExitStack() as ctx:
        sb = lambda name, shape, dt: ctx.enter_context(nc.sbuf_tensor(name, shape, dt))
        x_sb = sb("x_sb", [P, TT, D], F32)
        id32 = sb("id32", [P, P], F32)
        id16 = sb("id16", [P, P], F16)
        L0 = Layer(32, 8, 16, False, 1, (16.0, 16.0, 64.0, 64.0))
        L1 = Layer(16, 4, 96, True, 3, (16.0, 16.0, 64.0, 64.0))
        def projections(L, tag, names, stack):
            tiles = [stack.enter_context(nc.sbuf_tensor(f"{tag}_{n}T", [P, 2, DC, w], F16))
                     for n, w in (("wq", L.DO), ("wk", L.KV), ("wv", L.KV))]
            loads = [split_items(a[n], t, s) for n, t, s in zip(names, tiles, (L.sq, L.sk, L.sv))]
            return tiles, loads
        with ExitStack() as inner:
            w1, loads1 = projections(L1, "a1", ("wq1", "wk1", "wv1"), inner)
            with ExitStack() as own:
                w0, loads0 = projections(L0, "a0", ("wq0", "wk0", "wv0"), own)
                attention(nc, L0, x_sb, id32, id16, a["ctxT"], w0, a["wo0"], a["ln_w"], "a0", x_in=a["x"],
                          own=loads0, later=[it for w in loads1 for it in w])
            ident32, ident16 = id32[:, :], id16[:, :]
            hT = inner.enter_context(nc.sbuf_tensor("a1_hT", [P, 2, DC, S_KEY], F16))
            routed_ffn(nc, x_sb, ident32, a["wA"], a["wB"], a["wR"], a["keysT"], a["ctxT"][0], hT, "f0")
            attention(nc, L1, x_sb, id32, id16, a["ctxT"], w1, a["wo1"], None, "a1", hT=hT)
        int8_ffn(nc, x_sb, ident32, ident16, a["norm_w"], a["Wg"], a["Wu"], a["Wd"], out, "f1")


def lay_out(x, ctx_4096, L0_xattn_wq, L0_xattn_wk, L0_xattn_wv, L0_xattn_wo, L0_xattn_ln_w, L0_ffn_A_w, L0_ffn_B_w,
            L0_ffn_Wq_w, L0_ffn_keys, L1_xattn_Wq, L1_xattn_Wk, L1_xattn_Wv, L1_xattn_Wo, L1_ffn_rmsnorm_weight,
            L1_ffn_Wg, L1_ffn_Wu, L1_ffn_Wd):
    n = np.asarray
    t = lambda w: np.ascontiguousarray(n(w).T)

    def packed(w):
        w = n(w).reshape(-1, 4, 96, D)
        return np.concatenate([w[:, :3], w[:, 3].reshape(-1, 3, 32, D)], axis=2).reshape(-1, D)

    return {
        "x": n(x).reshape(TOK, D), "ctxT": np.ascontiguousarray(n(ctx_4096).transpose(0, 2, 1)),
        "wq0": t(n(L0_xattn_wq).reshape(8, 4, 16, D).transpose(1, 0, 2, 3).reshape(512, D)), "wk0": t(L0_xattn_wk), "wv0": t(L0_xattn_wv), "wo0": t(L0_xattn_wo),
        "ln_w": n(L0_xattn_ln_w), "wA": t(L0_ffn_A_w), "wB": t(L0_ffn_B_w), "wR": t(L0_ffn_Wq_w),
        "keysT": t(L0_ffn_keys), "wq1": t(packed(L1_xattn_Wq)), "wk1": t(packed(L1_xattn_Wk)), "wv1": t(L1_xattn_Wv),
        "wo1": t(L1_xattn_Wo), "norm_w": n(L1_ffn_rmsnorm_weight), "Wg": n(L1_ffn_Wg), "Wu": n(L1_ffn_Wu),
        "Wd": n(L1_ffn_Wd),
    }


def kernel(**inputs):
    import concourse.bacc as bacc
    from concourse.bass_utils import run_bass_kernel_spmd

    nc = bacc.Bacc("TRN2", target_bir_lowering=False, num_devices=1)
    arrays = lay_out(**inputs)
    aps = {k: nc.dram_tensor(f"in_{k}", v.shape, mybir.dt.from_np(v.dtype), kind="ExternalInput").ap()
           for k, v in arrays.items()}
    out = nc.dram_tensor("out", (TOK, D), F32, kind="ExternalOutput").ap()
    build(nc, aps, out)
    r = run_bass_kernel_spmd(nc, [{f"in_{k}": v for k, v in arrays.items()}], core_ids=[0])
    return r.results[0]["out"].reshape(B, QL, D)
```
